# Optimizing a Trainium2 kernel written in Bass

```python
import numpy as np
import jax
import jax.numpy as jnp

def _softmax(x, axis=-1):
    return jax.nn.softmax(x, axis=axis)

def _gelu(x):
    return jax.nn.gelu(x, approximate=True)

def _silu(x):
    return jax.nn.silu(x)

def _sigmoid(x):
    return jax.nn.sigmoid(x)

def _layernorm(x, axis=-1, eps=1e-05):
    m = jnp.mean(x, axis=axis, keepdims=True)
    v = jnp.var(x, axis=axis, keepdims=True)
    return (x - m) / jnp.sqrt(v + eps)

def _scatter_add(tgt, idx, src, axis=0):
    return tgt.at[idx].add(src)

def _segment_sum(src, seg, n):
    return jax.ops.segment_sum(src, seg, n)
kernel_name = 'mk_vit_tower_cls_d1_tok_img256_r4_590122'

def setup_inputs(seed: int=0):
    np.random.seed(seed)
    _w = jnp.asarray

    def _rec_inputs():
        import jax
        import jax.numpy as jnp
        _rk = jax.random.key(seed)
        x = -0.000202321 + 1.00025 * jax.random.normal(jax.random.fold_in(_rk, 1), (16, 64, 56, 56), jnp.float32)
        cls_tok = 0.02 * jax.random.normal(jax.random.fold_in(_rk, 5), (1, 1, 64), jnp.float32)
        return (x, cls_tok)
    x, cls_tok = _rec_inputs()

    def _L0_tok_setup():
        import jax, jax.numpy as jnp
        import numpy as np
        B, C, H, W = (8, 64, 56, 56)
        K = 3

        def _unfold3x3(x):
            b, c, h, w = x.shape
            xp = jnp.pad(x, ((0, 0), (0, 0), (1, 1), (1, 1)))
            patches = jnp.stack([xp[:, :, i:i + h, j:j + w] for i in range(K) for j in range(K)], axis=2)
            return patches.reshape(b, c * K * K, h * w).transpose(0, 2, 1)
        key = jax.random.key(seed)
        ks = jax.random.split(key, 8)
        d = C * K * K
        s1 = 1.0 / np.sqrt(d)
        s2 = 1.0 / np.sqrt(C)
        return {'x': jax.random.normal(ks[0], (B, C, H, W), jnp.float32), 'W1': jax.random.uniform(ks[1], (d, C), jnp.float32, -s1, s1), 'b1': jax.random.uniform(ks[2], (C,), jnp.float32, -s1, s1), 'W2': jax.random.uniform(ks[3], (C, d), jnp.float32, -s2, s2), 'b2': jax.random.uniform(ks[4], (d,), jnp.float32, -s2, s2), 'W3': jax.random.uniform(ks[5], (d, C), jnp.float32, -s1, s1), 'b3': jax.random.uniform(ks[6], (C,), jnp.float32, -s1, s1)}
    _L0_tok_all = _L0_tok_setup()
    _L0_tok_in = {k: v for k, v in _L0_tok_all.items() if k in ('W1', 'b1', 'W2', 'b2', 'W3', 'b3')}
    del _L0_tok_all

    def _L0_attn_setup():
        import jax, jax.numpy as jnp
        import numpy as np
        EPS_NORM = 1e-06
        EPS_ATTN = 1e-06
        HEADS = 8

        def rmsnorm(x, w):
            ms = jnp.mean(x * x, axis=-1, keepdims=True)
            return w * (x * jax.lax.rsqrt(ms + EPS_NORM))

        def linear_attention(x, w_qkv, w_out, b_out):
            B, N, D = x.shape
            hd = D // HEADS
            qkv = (x @ w_qkv).reshape(B, N, 3, HEADS, hd)
            q, k, v = (qkv[:, :, 0], qkv[:, :, 1], qkv[:, :, 2])
            q = jax.nn.elu(q) + 1.0
            k = jax.nn.elu(k) + 1.0
            kv = jnp.einsum('bnhd,bnhm->bhdm', k, v)
            z = 1.0 / (jnp.einsum('bnhd,bhd->bnh', q, k.sum(axis=1)) + EPS_ATTN)
            out = jnp.einsum('bnhd,bhdm,bnh->bnhm', q, kv, z)
            out = out.reshape(B, N, D)
            return out @ w_out + b_out
        key = jax.random.key(seed)
        ks = jax.random.split(key, 4)
        B, N, D = (16, 2048, 64)
        x = jax.random.normal(ks[0], (B, N, D), dtype=jnp.float32)
        w_norm1 = jnp.ones((D,), dtype=jnp.float32)
        w_qkv = jax.random.normal(ks[1], (D, 3 * D), dtype=jnp.float32) * 0.02
        w_out = jax.random.normal(ks[2], (D, D), dtype=jnp.float32) * 0.02
        b_out = jnp.zeros((D,), dtype=jnp.float32)
        w_norm2 = jnp.ones((D,), dtype=jnp.float32)
        return {'x': x, 'w_norm1': w_norm1, 'w_qkv': w_qkv, 'w_out': w_out, 'b_out': b_out, 'w_norm2': w_norm2}
    _L0_attn_all = _L0_attn_setup()
    _L0_attn_in = {k: v for k, v in _L0_attn_all.items() if k in ('w_norm1', 'w_qkv', 'w_out', 'b_out', 'w_norm2')}
    del _L0_attn_all

    def _L0_ffn_setup():
        import jax, jax.numpy as jnp
        import numpy as np
        E, D, H, TOP_K = (6, 64, 64, 2)
        ROUTER_H = D // 2
        key = jax.random.key(seed)
        ks = jax.random.split(key, 12)
        s = 1.0 / np.sqrt(D)
        sh = 1.0 / np.sqrt(H)
        sr = 1.0 / np.sqrt(ROUTER_H)
        return {'features': jax.random.normal(ks[0], (8, 1024, D), dtype=jnp.float32), 'router_w1': jax.random.uniform(ks[1], (D, ROUTER_H), jnp.float32, -s, s), 'router_b1': jnp.zeros((ROUTER_H,), jnp.float32), 'router_w2': jax.random.uniform(ks[2], (ROUTER_H, E), jnp.float32, -sr, sr), 'router_b2': jnp.zeros((E,), jnp.float32), 'expert_w1': jax.random.uniform(ks[3], (E, D, H), jnp.float32, -s, s), 'expert_b1': jnp.zeros((E, H), jnp.float32), 'expert_w2': jax.random.uniform(ks[4], (E, H, H), jnp.float32, -sh, sh), 'expert_b2': jnp.zeros((E, H), jnp.float32), 'expert_w3': jax.random.uniform(ks[5], (E, H, D), jnp.float32, -sh, sh), 'expert_b3': jnp.zeros((E, D), jnp.float32)}
    _L0_ffn_all = _L0_ffn_setup()
    _L0_ffn_in = {k: v for k, v in _L0_ffn_all.items() if k in ('router_w1', 'router_b1', 'router_w2', 'router_b2', 'expert_w1', 'expert_b1', 'expert_w2', 'expert_b2', 'expert_w3', 'expert_b3')}
    del _L0_ffn_all
    return {'x': x, 'cls_tok': cls_tok, 'L0_tok_W1': _L0_tok_in['W1'], 'L0_tok_b1': _L0_tok_in['b1'], 'L0_tok_W2': _L0_tok_in['W2'], 'L0_tok_b2': _L0_tok_in['b2'], 'L0_tok_W3': _L0_tok_in['W3'], 'L0_tok_b3': _L0_tok_in['b3'], 'L0_attn_w_norm1': _L0_attn_in['w_norm1'], 'L0_attn_w_qkv': _L0_attn_in['w_qkv'], 'L0_attn_w_out': _L0_attn_in['w_out'], 'L0_attn_b_out': _L0_attn_in['b_out'], 'L0_attn_w_norm2': _L0_attn_in['w_norm2'], 'L0_ffn_router_w1': _L0_ffn_in['router_w1'], 'L0_ffn_router_b1': _L0_ffn_in['router_b1'], 'L0_ffn_router_w2': _L0_ffn_in['router_w2'], 'L0_ffn_router_b2': _L0_ffn_in['router_b2'], 'L0_ffn_expert_w1': _L0_ffn_in['expert_w1'], 'L0_ffn_expert_b1': _L0_ffn_in['expert_b1'], 'L0_ffn_expert_w2': _L0_ffn_in['expert_w2'], 'L0_ffn_expert_b2': _L0_ffn_in['expert_b2'], 'L0_ffn_expert_w3': _L0_ffn_in['expert_w3'], 'L0_ffn_expert_b3': _L0_ffn_in['expert_b3']}

def reference(x, cls_tok, L0_tok_W1, L0_tok_b1, L0_tok_W2, L0_tok_b2, L0_tok_W3, L0_tok_b3, L0_attn_w_norm1, L0_attn_w_qkv, L0_attn_w_out, L0_attn_b_out, L0_attn_w_norm2, L0_ffn_router_w1, L0_ffn_router_b1, L0_ffn_router_w2, L0_ffn_router_b2, L0_ffn_expert_w1, L0_ffn_expert_b1, L0_ffn_expert_w2, L0_ffn_expert_b2, L0_ffn_expert_w3, L0_ffn_expert_b3):
    import jax
    import jax.numpy as jnp

    def _L0_tok_ref(x, W1, b1, W2, b2, W3, b3):
        import jax, jax.numpy as jnp
        import numpy as np
        B, C, H, W = (8, 64, 56, 56)
        K = 3

        def _unfold3x3(x):
            b, c, h, w = x.shape
            xp = jnp.pad(x, ((0, 0), (0, 0), (1, 1), (1, 1)))
            patches = jnp.stack([xp[:, :, i:i + h, j:j + w] for i in range(K) for j in range(K)], axis=2)
            return patches.reshape(b, c * K * K, h * w).transpose(0, 2, 1)
        t = _unfold3x3(x)
        h1 = jax.nn.relu(jnp.einsum('bld,dc->blc', t, W1) + b1)
        s = jax.nn.sigmoid(jnp.einsum('blc,cd->bld', h1, W2) + b2)
        out = jnp.einsum('bld,dc->blc', t * s, W3) + b3
        return out

    def _L0_attn_ref(x, w_norm1, w_qkv, w_out, b_out, w_norm2):
        import jax, jax.numpy as jnp
        import numpy as np
        EPS_NORM = 1e-06
        EPS_ATTN = 1e-06
        HEADS = 8

        def rmsnorm(x, w):
            ms = jnp.mean(x * x, axis=-1, keepdims=True)
            return w * (x * jax.lax.rsqrt(ms + EPS_NORM))

        def linear_attention(x, w_qkv, w_out, b_out):
            B, N, D = x.shape
            hd = D // HEADS
            qkv = (x @ w_qkv).reshape(B, N, 3, HEADS, hd)
            q, k, v = (qkv[:, :, 0], qkv[:, :, 1], qkv[:, :, 2])
            q = jax.nn.elu(q) + 1.0
            k = jax.nn.elu(k) + 1.0
            kv = jnp.einsum('bnhd,bnhm->bhdm', k, v)
            z = 1.0 / (jnp.einsum('bnhd,bhd->bnh', q, k.sum(axis=1)) + EPS_ATTN)
            out = jnp.einsum('bnhd,bhdm,bnh->bnhm', q, kv, z)
            out = out.reshape(B, N, D)
            return out @ w_out + b_out
        h = x + linear_attention(rmsnorm(x, w_norm1), w_qkv, w_out, b_out)
        return h + rmsnorm(h, w_norm2)

    def _L0_ffn_ref(features, router_w1, router_b1, router_w2, router_b2, expert_w1, expert_b1, expert_w2, expert_b2, expert_w3, expert_b3):
        import jax, jax.numpy as jnp
        import numpy as np
        E, D, H, TOP_K = (6, 64, 64, 2)
        ROUTER_H = D // 2
        rh = jax.nn.relu(features @ router_w1 + router_b1)
        expert_logits = jax.nn.softmax(rh @ router_w2 + router_b2, axis=-1)
        top_w, top_i = jax.lax.top_k(expert_logits, TOP_K)
        routing_weights = jax.nn.softmax(top_w, axis=-1)
        h1 = jax.nn.relu(jnp.einsum('bsd,edh->bseh', features, expert_w1) + expert_b1)
        h2 = jax.nn.relu(jnp.einsum('bseh,ehf->bsef', h1, expert_w2) + expert_b2)
        expert_out = jnp.einsum('bsef,efo->bseo', h2, expert_w3) + expert_b3
        sel = jnp.take_along_axis(expert_out, top_i[:, :, :, None], axis=2)
        combined = jnp.sum(sel * routing_weights[..., None], axis=2)
        return combined
    h = _L0_tok_ref(x, L0_tok_W1, L0_tok_b1, L0_tok_W2, L0_tok_b2, L0_tok_W3, L0_tok_b3)
    h = jnp.concatenate([jnp.broadcast_to(cls_tok, (h.shape[0], 1, h.shape[2])), h], axis=1)
    h = h + _L0_attn_ref(_layernorm(h, axis=-1), L0_attn_w_norm1, L0_attn_w_qkv, L0_attn_w_out, L0_attn_b_out, L0_attn_w_norm2)
    h = h + _L0_ffn_ref(_layernorm(h, axis=-1), L0_ffn_router_w1, L0_ffn_router_b1, L0_ffn_router_w2, L0_ffn_router_b2, L0_ffn_expert_w1, L0_ffn_expert_b1, L0_ffn_expert_w2, L0_ffn_expert_b2, L0_ffn_expert_w3, L0_ffn_expert_b3)
    return h

_drawn_inputs = setup_inputs


def setup_inputs(seed=0):
    import zlib

    import numpy as np

    out = dict(_drawn_inputs(seed))
    spreads = {'L0_attn_w_norm1': (1.0, 0.6),
     'L0_attn_b_out': (0.0, 0.1),
     'L0_attn_w_norm2': (1.0, 0.2),
     'L0_ffn_router_b1': (0.0, 0.451),
     'L0_ffn_router_b2': (0.0, 0.3),
     'L0_ffn_expert_b1': (0.0, 0.8),
     'L0_ffn_expert_b2': (0.0, 0.65),
     'L0_ffn_expert_b3': (0.0, 0.287)}
    factors = {'cls_tok': 38.438, 'L0_tok_b1': 8.0, 'L0_attn_w_qkv': 8.0, 'L0_attn_w_out': 8.0}
    for name, (base, spread) in spreads.items():
        noise = np.random.default_rng([zlib.crc32(name.encode()), seed]).standard_normal(out[name].shape)
        drawn = base * np.exp(spread * noise) if base else spread * noise
        out[name] = jnp.asarray(drawn.astype(out[name].dtype))
    for name, factor in factors.items():
        out[name] = (out[name] * factor).astype(out[name].dtype)
    return out
```

```python
from contextlib import ExitStack

import numpy as np

import concourse.bass as bass
from concourse import mybir

F32 = mybir.dt.float32
F32R = mybir.dt.float32r
I32 = mybir.dt.int32
ALU = mybir.AluOpType
ACT = mybir.ActivationFunctionType
AX_X = mybir.AxisListType.X

B, C, H, W = 16, 64, 56, 56
HEADS, HD = 8, 8
E, RH = 6, 32
TOKENS = H * W + 1
P = 128
PW = W + 2
ROWS = 8
CHUNKS = H // ROWS
N = ROWS * W
TILE, NT = 112, 4
PAIRS = B // 2
NCLS = PAIRS
UNITS = 9
XC_LEN = 9 * PW + W
XR_LEN = 7 * PW + W
EPS_LN, EPS_RMS, EPS_ATT = 1e-5, 1e-6, 1e-6

OFFSET_PAIRS = [((0, 0), (0, 1)), ((1, 0), (1, 1)), ((2, 0), (2, 1)), ((0, 2), (1, 2))]
LAST_OFFSET = (2, 2)


def columns():
    widths = [
        ("w2", 6 * P), ("ew1", 3 * P), ("rw1", 2 * P), ("gate_sel", 6 * P), ("eb3", P),
        ("w1", 4 * C + P), ("w3", 4 * C + P), ("wqkv", 3 * P), ("wo", P), ("ew2", 3 * P), ("ew3", 3 * C),
        ("rw2", 2 * E), ("ident", P), ("center", P), ("mean", 2), ("head_mask", P + 2 * HEADS),
        ("order", NT * 2 * E), ("rb2", NT * 2 * E), ("cls", NCLS),
        ("b1", 1), ("b2", 5), ("b3", 1), ("norm1", 1), ("bo", 1), ("norm2", 1), ("rb1", 1), ("eb1", 3), ("eb2", 3),
    ]
    out, at = {}, 0
    for name, width in widths:
        out[name] = (at, at + width)
        at += width
    return out, at


COLS, PACK_W = columns()
SPLIT_W = COLS["eb3"][1]


def build(nc, xpad, pack, out):
    ctx = ExitStack()
    with ctx:
        def sb(name, shape, dt=F32):
            return ctx.enter_context(nc.sbuf_tensor(name, shape, dt))

        def sem(name):
            return ctx.enter_context(nc.semaphore(name))

        packed = sb("packed", [P, PACK_W])
        split_hi = sb("split_hi", [P, SPLIT_W], F32R)
        split_lo = sb("split_lo", [P, SPLIT_W], F32R)
        w3_half = sb("w3_half", [P, 4 * C + P])
        wqkv_n = sb("wqkv_n", [P, 3 * P])
        b2_half = sb("b2_half", [P, 5])
        exponent = sb("exponent", [TILE, 4 * NT])

        def cst(name, a=0, b=None):
            lo, hi = COLS[name]
            return packed[:, lo + a:(hi if b is None else lo + b)]

        def hi_of(name, a=0, b=None):
            lo, hi = COLS[name]
            return split_hi[:, lo + a:(hi if b is None else lo + b)]

        def lo_of(name, a=0, b=None):
            lo, hi = COLS[name]
            return split_lo[:, lo + a:(hi if b is None else lo + b)]

        xc = [sb(f"xc{m}", [P, 10 * PW]) for m in range(2)]
        xr = [sb(f"xr{m}", [P, ROWS * PW]) for m in range(2)]
        xp = sb("xp", [P, ROWS * PW])
        h1 = sb("h1", [P, N])
        h1s = [sb(f"h1s{m}", [P, N], F32R) for m in range(2)]
        th = [sb(f"th{k}", [P, N]) for k in range(3)]
        gated = [sb(f"gated{k}", [P, N]) for k in range(3)]
        h_new = sb("h_new", [P, N])
        hn_new = sb("hn_new", [P, N])
        q_new = sb("q_new", [P, N])
        sq_a = sb("sq_a", [P, N])
        xc_a = sb("xc_a", [P, N])
        u_a = sb("u_a", [P, N])
        var_a = sb("var_a", [TILE, 4 * NT])
        rstd_a = sb("rstd_a", [TILE, 4 * NT])
        rx_a = sb("rx_a", [TILE, 2, NT * P])
        eq = sb("eq", [P, N])
        eq1 = sb("eq1", [P, N])
        ek = sb("ek", [TILE, NT, P])
        ek1 = sb("ek1", [TILE, NT, P])
        k_tok = sb("k_tok", [TILE, NT, P])
        v_tok = sb("v_tok", [TILE, NT, P + 2])
        kv_sum = sb("kv_sum", [P, P + 2])
        kv_cls = sb("kv_cls", [P, P + 2])
        ring = [sb(f"ring_{n}", [P, CHUNKS * N]) for n in ("h", "hn", "q")]
        cur = [sb(f"cur_{n}", [P, N]) for n in ("h", "hn", "q")]
        cls_h = cst("cls")
        cls_hn = sb("cls_hn", [P, NCLS])
        cls_q = sb("cls_q", [P, NCLS])
        kv_m = sb("kv_m", [P, P + 2 * HEADS])
        k_m = sb("k_m", [P, P])
        cls_den = sb("cls_den", [P, 2])
        cls_att = sb("cls_att", [P, NCLS])
        den = sb("den", [TILE, NT * 2 * HEADS])
        zed = sb("zed", [TILE, NT * 2 * HEADS])
        att = sb("att", [TILE, NT * P])
        att_c = sb("att_c", [P, N])
        h2 = sb("h2", [P, N])
        sq_b = sb("sq_b", [P, N])
        ms_b = sb("ms_b", [TILE, 2 * NT])
        rms_b = sb("rms_b", [TILE, 2 * NT])
        rx_b = sb("rx_b", [TILE, NT * P])
        sum_b = sb("sum_b", [P, N])
        nrm_b = sb("nrm_b", [P, N])
        h3 = sb("h3", [P, N])
        sq_c = sb("sq_c", [P, N])
        xc_b = sb("xc_b", [P, N])
        var_b = sb("var_b", [TILE, 2 * NT])
        rstd_b = sb("rstd_b", [TILE, 2 * NT])
        rx_c = sb("rx_c", [TILE, NT * P])
        y = sb("y", [P, N])
        ys = [sb(f"ys{m}", [P, N], F32R) for m in range(2)]
        rh = sb("rh", [2 * RH, N])
        G = NT * 2
        gates_shape = [TILE, G * E]
        g_logit, g_shift, g_exp, g_p, g_e1, g_o1, g_rest, g_e2, g_o2, g_a, g_b, g_sum = (
            sb(f"g_{n}", gates_shape)
            for n in ("logit", "shift", "exp", "p", "e1", "o1", "rest", "e2", "o2", "a", "b", "sum"))
        g_w1, g_w2 = sb("g_w1", gates_shape), sb("g_w2", gates_shape)
        g_max, g_tot, g_inv, g_top, g_i1, g_top2, g_i2, g_dif, g_ed, g_one, g_r1, g_r2 = (
            sb(f"gs_{n}", [TILE, G])
            for n in ("max", "tot", "inv", "top", "i1", "top2", "i2", "dif", "ed", "one", "r1", "r2"))
        g_parts = sb("g_parts", [TILE, NT, 2, 2 * E], F32R)
        gates_c = sb("gates_c", [4 * E, N], F32R)
        f1 = [sb(f"f1_{k}", [P, N]) for k in range(2)]
        f2 = [sb(f"f2_{k}", [P, N]) for k in range(2)]
        gh = [sb(f"gh_{k}", [P, N]) for k in range(2)]
        res = sb("res", [P, N])
        out_t = sb("out_t", [TILE, NT * P])

        ps = ctx.enter_context(nc.psum_tensor("ps", [P, 8, 512], F32))
        S0, S1, L0, L1, M0, F5, F6, F7 = range(8)

        pack_loaded, x_loaded, cur_loaded = sem("pack_loaded"), sem("x_loaded"), sem("cur_loaded")
        ring_stored, out_stored = sem("ring_stored"), sem("out_stored")
        setup_dve, setup_act = sem("setup_dve"), sem("setup_act")
        (w1_done, s_done, w3_done, ctr_done, vara_done, rxa_done, q_done, kv_done, kvp_done, clsatt_done) = (
            sem(n) for n in ("w1_done", "s_done", "w3_done", "ctr_done", "vara_done", "rxa_done", "q_done",
                             "kv_done", "kvp_done", "clsatt_done"))
        (attn_done, attc_done, wo_done, ms_done, rxb_done, ctrb_done, varb_done, rxc_done, router_done,
         logit_done, gt_done, fh1_done, fgb_done, fh2_done, fw3_done, outt_done) = (
            sem(n) for n in ("attn_done", "attc_done", "wo_done", "ms_done", "rxb_done", "ctrb_done",
                             "varb_done", "rxc_done", "router_done", "logit_done", "gt_done", "fh1_done",
                             "fgb_done", "fh2_done", "fw3_done", "outt_done"))
        (h1hi_set, th_set, h_set, sqa_set, eq_set, ek_set, v_set, attc_set, sqb_set, sqc_set, yhi_set, rh_set,
         gexp_set, ged_set, gatesc_set, f1_set, f2_set, outt_set) = (
            sem(n) for n in ("h1hi_set", "th_set", "h_set", "sqa_set", "eq_set", "ek_set", "v_set", "attc_set",
                             "sqb_set", "sqc_set", "yhi_set", "rh_set", "gexp_set", "ged_set", "gatesc_set",
                             "f1_set", "f2_set", "outt_set"))
        (h1_set, h1lo_set, gated_set, xca_set, var_set, rxa_set, hn_set, u_set, eq1_set, qf_set, ek1_set, kf_set,
         kvsum_set, kvm_set, clsden_set, clsatt_set) = (
            sem(n) for n in ("h1_set", "h1lo_set", "gated_set", "xca_set", "var_set", "rxa_set", "hn_set", "u_set",
                             "eq1_set", "qf_set", "ek1_set", "kf_set", "kvsum_set", "kvm_set", "clsden_set",
                             "clsatt_set"))
        (den_set, zed_set, att_set, h2_set, msb_set, rxb_set, nrm_set, h3_set, xcb_set, varb_set, rxc_set, y_set,
         ylo_set, gate_step, gh_set, res_set) = (
            sem(n) for n in ("den_set", "zed_set", "att_set", "h2_set", "msb_set", "rxb_set", "nrm_set", "h3_set",
                             "xcb_set", "varb_set", "rxc_set", "y_set", "ylo_set", "gate_step", "gh_set",
                             "res_set"))
        rstda_set, rmsb_set, rstdb_set, sumb_set = (
            sem(n) for n in ("rstda_set", "rmsb_set", "rstdb_set", "sumb_set"))
        GATE_STEPS = 24
        SETUP_DVE = 7

        def x_view(unit):
            if unit == 0:
                return xp[:, :].rearrange("p (r c) -> p r c", c=PW)[:, :, 0:W]
            m, img = (unit - 1) // 2, (unit - 1) % 2
            if m < 3:
                return xc[img][:, :].rearrange("p (r c) -> p r c", c=PW)[:, m:m + ROWS, 0:W]
            return xr[img][:, :].rearrange("p (r c) -> p r c", c=PW)[:, :, 0:W]

        def as_rows(ap):
            return ap.rearrange("p (r c) -> p r c", c=W)

        def bank(b, n=N, p0=0, p1=P):
            return ps[p0:p1, b, 0:n]

        def half(img):
            return slice(64 * img, 64 * img + 64)

        FULL, CLS = (NT, TILE), (1, NCLS)
        block = ctx.enter_context(nc.Block())

        @block.sync
        def _(sp):
            def prime(s, n):
                sp.sem_inc(s, n)

            prime(ring_stored, 48)
            prime(out_stored, 32)
            sp.dma_start(packed[:, :], pack).then_inc(pack_loaded, 16)

            def reg(v):
                return v if isinstance(v, int) else sp.snap(v)

            def settle():
                sp.wait_ge(pack_loaded, 16)

            def load_x(i, c, s):
                row, at, before = reg(i * P), reg(c * (ROWS * PW)), reg(UNITS * s)
                rows = [xpad[bass.ds(row + 64 * img, 64)] for img in range(2)]
                todo = []
                for img in range(2):
                    for part in range(2):
                        todo.append((xc[img][half(part), 0:XC_LEN], rows[img][:, bass.ds(at + part, XC_LEN)]))
                        todo.append((xr[img][half(part), 0:XR_LEN],
                                     rows[img][:, bass.ds(at + 2 + part * PW, XR_LEN)]))
                todo.append((xp[:, 0:XR_LEN], xpad[bass.ds(row, P)][:, bass.ds(at + 2 * PW + 2, XR_LEN)]))
                sp.wait_ge(gated_set, before)
                sp.wait_ge(w3_done, before)
                settle()
                for to, of in todo:
                    sp.dma_start(to, of).then_inc(x_loaded, 16)

            def load_cur(c, t):
                at, before, stored = reg(c * N), reg(t + 0), reg(48 * t + 48)
                sp.wait_ge(h3_set, before)
                sp.wait_ge(attn_done, before)
                sp.wait_ge(ring_stored, stored)
                settle()
                for to, of in zip(cur, ring):
                    sp.dma_start(to[:, :], of[:, bass.ds(at, N)]).then_inc(cur_loaded, 16)

            def store_ring(c, s, t):
                at, now = reg(c * N), reg(s + 1)
                loaded = None if t is None else reg(48 * t)
                if t is not None:
                    sp.wait_ge(cur_loaded, loaded)
                sp.wait_ge(h_set, now)
                sp.wait_ge(hn_set, now)
                sp.wait_ge(qf_set, now)
                settle()
                for to, of in zip(ring, (h_new, hn_new, q_new)):
                    sp.dma_start(to[:, bass.ds(at, N)], of[:, :]).then_inc(ring_stored, 16)

            def store_out(i, c, t):
                image, at, now = reg(i * 2), reg(c * N + 1), reg(t + 1)
                sp.wait_ge(outt_set, now)
                settle()
                for img in range(2):
                    dst = out[bass.ds(image + img, 1), bass.ds(at, N), :]
                    sp.dma_start(dst.rearrange("o (n p) c -> p (o n) c", p=TILE),
                                 out_t[:, :].rearrange("p (n m c) -> p n m c", m=2, c=C)[:, :, img, :]
                                 ).then_inc(out_stored, 16)

            load_x(0, 0, 1)
            with sp.Fori(1, CHUNKS) as c:
                load_x(0, c, c + 1)
                store_ring(c - 1, c, None)

            def pair(i, first):
                s = i * CHUNKS + 1
                load_x(i, 0, s)
                load_cur(0, s - CHUNKS)
                store_ring(CHUNKS - 1, s - 1, None if first else s - CHUNKS - 1)
                if not first:
                    store_out(i - 2, CHUNKS - 1, s - CHUNKS - 1)
                with sp.Fori(1, CHUNKS) as c:
                    s1 = s + c
                    load_x(i, c, s1)
                    load_cur(c, s1 - CHUNKS)
                    store_ring(c - 1, s1 - 1, s1 - CHUNKS - 1)
                    store_out(i - 1, c - 1, s1 - CHUNKS - 1)

            pair(1, True)
            with sp.Fori(2, PAIRS) as i:
                pair(i, False)
            t0 = (PAIRS - 1) * CHUNKS + 1
            load_cur(0, t0)
            store_ring(CHUNKS - 1, PAIRS * CHUNKS, t0 - 1)
            store_out(PAIRS - 2, CHUNKS - 1, t0 - 1)
            with sp.Fori(1, CHUNKS) as c:
                load_cur(c, c + t0)
                store_out(PAIRS - 1, c - 1, c + (t0 - 1))
            last = PAIRS * CHUNKS
            store_out(PAIRS - 1, CHUNKS - 1, last)
            sp.wait_ge(outt_set, last + 2)
            cls_rows = out.rearrange("(i m) t c -> i m t c", m=2)[:, :, 0, :]
            sp.dma_start(cls_rows, out_t[0:NCLS, 0:P].rearrange("p (m c) -> p m c", m=2)).then_inc(out_stored, 16)
            sp.wait_ge(out_stored, 32 + 32 * last + 16)

        @block.tensor
        def _(pe):
            ident = cst("ident")

            def w1(s):
                pe.wait_ge(x_loaded, 144 * s)
                pe.wait_ge(kvsum_set, s)
                pe.matmul(as_rows(bank(L0)), cst("w1", 4 * C), x_view(0), start=True, stop=False)
                for u in range(1, UNITS):
                    m, img = (u - 1) // 2, (u - 1) % 2
                    mm = pe.matmul(as_rows(bank(L0, p0=64 * img, p1=64 * img + 64)), cst("w1", m * C, (m + 1) * C),
                                   x_view(u), start=False, stop=(m == 3))
                mm.then_inc(w1_done, 1)

            def w2(s, u):
                if u == 0:
                    pe.wait_ge(h1hi_set, 2 * s + 2)
                    pe.wait_ge(h1lo_set, 2 * s + 2)
                    pe.wait_ge(kf_set, 2 * s)
                    pe.wait_ge(v_set, s)
                else:
                    if u >= 2:
                        pe.wait_ge(th_set, UNITS * s + u - 1)
                b = S0 + u % 2
                if u == 0:
                    todo = [(m, img, w) for m, img in ((4, 0), (5, 1)) for w in (hi_of, lo_of)]
                else:
                    todo = [((u - 1) // 2, (u - 1) % 2, w) for w in (hi_of, lo_of)]
                for n, (m, img, w) in enumerate(todo):
                    mm = pe.matmul(bank(b), w("w2", m * P, (m + 1) * P), h1s[img][:, :],
                                   start=(n == 0), stop=(n == len(todo) - 1))
                mm.then_inc(s_done, 1)

            def w3(s, u):
                pe.wait_ge(gated_set, UNITS * s + u + 1)
                if u == 0:
                    mm = pe.matmul(bank(L0), w3_half[:, 4 * C:], gated[0][:, :], start=True, stop=False)
                else:
                    m, img = (u - 1) // 2, (u - 1) % 2
                    mm = pe.matmul(bank(L0, p0=64 * img, p1=64 * img + 64), w3_half[:, m * C:(m + 1) * C],
                                   gated[u % 3][:, :], start=False, stop=(m == 3))
                mm.then_inc(w3_done, 1)

            def token_mean(b, src, geo, done):
                nt, tw = geo
                for k in range(nt):
                    mm = pe.matmul(ps[0:tw, b, 2 * k:2 * k + 2], src[:, k * tw:(k + 1) * tw], cst("mean"),
                                   start=True, stop=True)
                mm.then_inc(done, 1)

            def to_channels(b, src, geo):
                nt, tw = geo
                for k in range(nt):
                    mm = pe.transpose(bank(b)[:, k * tw:(k + 1) * tw], src[0:tw, k * P:(k + 1) * P],
                                      ident[0:tw, 0:tw])
                return mm

            def center_a(s, geo, h):
                n = geo[0] * geo[1]
                if s is not 0:
                    pe.wait_ge(h_set, s + 1)
                    pe.wait_ge(qf_set, s)
                pe.matmul(bank(L1, n), cst("center"), h[:, 0:n], start=True, stop=True).then_inc(ctr_done, 1)

            def var_mean_a(s, geo):
                pe.wait_ge(sqa_set, s + 1)
                token_mean(L0, sq_a, geo, vara_done)

            def spread_a(s, geo):
                pe.wait_ge(rxa_set, 2 * s + 2)
                pe.wait_ge(xca_set, s + 1)
                to_channels(L1, rx_a[:, 0, :], geo)
                to_channels(L0, rx_a[:, 1, :], geo).then_inc(rxa_done, 1)

            def q_prod(s, geo):
                n = geo[0] * geo[1]
                pe.wait_ge(u_set, s + 1)
                pe.wait_ge(hn_set, s + 1)
                pe.matmul(bank(L1, n), wqkv_n[:, 0:P], u_a[:, 0:n], start=True, stop=True).then_inc(q_done, 1)

            def kv_prod(s, geo):
                nt, tw = geo
                if s is not 0:
                    pe.wait_ge(th_set, UNITS * (s + 1))
                for k in range(nt):
                    at = 2 * P * (k % 2)
                    mm = pe.matmul(ps[0:tw, S0 + k // 2, at:at + 2 * P], u_a[:, k * tw:(k + 1) * tw],
                                   wqkv_n[:, P:3 * P], start=True, stop=True)
                mm.then_inc(kv_done, 1)

            def kv_outer(s, geo):
                nt, tw = geo if geo is FULL else (1, 1)
                pe.wait_ge(kf_set, 2 * s + 2)
                pe.wait_ge(v_set, s + 1)
                for k in range(nt):
                    mm = pe.matmul(bank(L0, P + 2), k_tok[0:tw, k, :], v_tok[0:tw, k, :],
                                   start=(k == 0), stop=(k == nt - 1))
                mm.then_inc(kvp_done, 1)

            def cls_attention(i):
                pe.wait_ge(kvm_set, i + 1)
                pe.matmul(ps[:, L1, 0:1], kv_m[:, 0:P], cls_q[:, 0:1], start=True, stop=True)
                pe.matmul(ps[:, L1, 1:2], k_m[:, :], cls_q[:, 0:1], start=True, stop=True).then_inc(clsatt_done, 1)
                pe.wait_ge(clsatt_set, i + 1)

            def attention(t):
                pe.wait_ge(cur_loaded, 48 * t)
                pe.wait_ge(res_set, t)
                pe.wait_ge(outt_set, t)
                for k in range(NT):
                    at = (P + 2 * HEADS) * (k % 2)
                    mm = pe.matmul(ps[0:TILE, M0 + k // 2, at:at + P + 2 * HEADS],
                                   cur[2][:, k * TILE:(k + 1) * TILE], kv_m[:, :], start=True, stop=True)
                mm.then_inc(attn_done, 1)

            def att_channels(t):
                pe.wait_ge(att_set, 2 * t + 2)
                pe.wait_ge(gh_set, E * t)
                to_channels(F6, att, FULL).then_inc(attc_done, 1)

            def out_proj(t, geo):
                n = geo[0] * geo[1]
                pe.wait_ge(attc_set, t + 1)
                if geo is CLS:
                    pe.wait_ge(res_set, t)
                    pe.wait_ge(outt_set, t)
                    pe.wait_ge(gh_set, E * t)
                pe.matmul(bank(M0, n), cst("wo"), att_c[:, 0:n], start=True, stop=True).then_inc(wo_done, 1)

            def mean_sq_b(t, geo):
                pe.wait_ge(sqb_set, t + 1)
                token_mean(F5, sq_b, geo, ms_done)

            def spread_b(t, geo):
                pe.wait_ge(rxb_set, t + 1)
                to_channels(F5, rx_b, geo).then_inc(rxb_done, 1)

            def center_b(t, geo):
                n = geo[0] * geo[1]
                pe.wait_ge(h3_set, t + 1)
                pe.matmul(bank(M0, n), cst("center"), h3[:, 0:n], start=True, stop=True).then_inc(ctrb_done, 1)

            def var_mean_b(t, geo):
                pe.wait_ge(sqc_set, t + 1)
                token_mean(F5, sq_c, geo, varb_done)

            def spread_c(t, geo):
                pe.wait_ge(rxc_set, t + 1)
                to_channels(F5, rx_c, geo).then_inc(rxc_done, 1)

            def router(t, geo):
                n = geo[0] * geo[1]
                pe.wait_ge(yhi_set, 2 * t + 2)
                pe.wait_ge(ylo_set, 2 * t + 2)
                k = 0
                for img in range(2):
                    for w in (hi_of, lo_of):
                        mm = pe.matmul(bank(F6, n), w("rw1", img * P, (img + 1) * P), ys[img][:, 0:n],
                                       start=(k == 0), stop=(k == 3))
                        k += 1
                mm.then_inc(router_done, 1)

            def logits(t, geo):
                nt, tw = geo
                pe.wait_ge(rh_set, t + 1)
                for k in range(nt):
                    mm = pe.matmul(ps[0:tw, F5, 2 * E * k:2 * E * (k + 1)], rh[:, k * tw:(k + 1) * tw],
                                   cst("rw2")[0:2 * RH, :], start=True, stop=True)
                mm.then_inc(logit_done, 1)

            def gates_channels(t, geo):
                nt, tw = geo
                pe.wait_ge(gate_step, GATE_STEPS * (t + 1))
                for k in range(nt):
                    mm = pe.transpose(ps[0:4 * E, F6, k * tw:(k + 1) * tw],
                                      g_parts[0:tw, k].rearrange("p a e -> p (a e)").bitcast(F32),
                                      ident[0:tw, 0:tw])
                mm.then_inc(gt_done, 1)

            def expert_h1(t, geo, j):
                n = geo[0] * geo[1]
                ep, img = j // 2, j % 2
                pe.wait_ge(f1_set, E * t + j)
                for w in (hi_of, lo_of):
                    mm = pe.matmul(bank(F7, n), w("ew1", ep * P, (ep + 1) * P), ys[img][:, 0:n],
                                   start=(w is hi_of), stop=(w is lo_of))
                mm.then_inc(fh1_done, 1)

            def expert_gate(t, geo, j):
                n = geo[0] * geo[1]
                if j == 0:
                    pe.wait_ge(gatesc_set, t + 1)
                else:
                    pe.wait_ge(gh_set, E * t + j)
                pe.matmul(bank(F6, n), hi_of("gate_sel", j * P, (j + 1) * P)[0:4 * E], gates_c[:, 0:n],
                          start=True, stop=True).then_inc(fgb_done, 1)

            def expert_h2(t, geo, j):
                n = geo[0] * geo[1]
                ep = j // 2
                pe.wait_ge(f1_set, E * t + j + 1)
                if j > 0:
                    pe.wait_ge(f2_set, E * t + j)
                pe.matmul(bank(F5, n), cst("ew2", ep * P, (ep + 1) * P), f1[j % 2][:, 0:n],
                          start=True, stop=True).then_inc(fh2_done, 1)

            def expert_bias(t, geo):
                n = geo[0] * geo[1]
                pe.wait_ge(xcb_set, t + 1)
                pe.wait_ge(sqc_set, t + 1)
                pe.matmul(bank(M0, n), hi_of("eb3")[0:4 * E], gates_c[:, 0:n], start=True, stop=False)
                pe.matmul(bank(M0, n), lo_of("eb3")[0:4 * E], gates_c[:, 0:n], start=False, stop=False)

            def expert_out(t, geo, j):
                n = geo[0] * geo[1]
                ep, img = j // 2, j % 2
                pe.wait_ge(gh_set, E * t + j + 1)
                pe.matmul(bank(M0, n, 64 * img, 64 * img + 64), cst("ew3", ep * C, (ep + 1) * C), gh[j % 2][:, 0:n],
                          start=False, stop=(j >= E - 2)).then_inc(fw3_done, 1)

            def out_tokens(t, geo):
                nt, tw = geo
                pe.wait_ge(res_set, t + 1)
                for k in range(nt):
                    mm = pe.transpose(ps[0:tw, F5, k * P:(k + 1) * P], res[:, k * tw:(k + 1) * tw], ident)
                mm.then_inc(outt_done, 1)

            def step(s, t, geo=FULL):
                A, Bs = s is not None, t is not None
                if Bs and geo is FULL: attention(t)
                if A: w1(s)
                if Bs and geo is FULL: att_channels(t)
                if A: w2(s, 0); w2(s, 1); w2(s, 2)
                if Bs: out_proj(t, geo)
                if A: w3(s, 0); w2(s, 3)
                if Bs: mean_sq_b(t, geo)
                if A: w3(s, 1); w3(s, 2); w2(s, 4)
                if Bs: spread_b(t, geo)
                if A: w2(s, 5); w3(s, 3); w3(s, 4)
                if Bs: center_b(t, geo)
                if A: w2(s, 6)
                if Bs: var_mean_b(t, geo)
                if A: w2(s, 7); w3(s, 5); w3(s, 6)
                if Bs: spread_c(t, geo)
                if A: w2(s, 8); w3(s, 7); w3(s, 8)
                if Bs: router(t, geo); expert_h1(t, geo, 0)
                if A: center_a(s, FULL, h_new)
                if Bs: logits(t, geo)
                if A: var_mean_a(s, FULL)
                if Bs: gates_channels(t, geo); expert_bias_first(t, geo)
                for j in range(E):
                    if Bs:
                        if j + 1 < E: expert_h1(t, geo, j + 1)
                        expert_gate(t, geo, j)
                        expert_h2(t, geo, j)
                        if j > 0: expert_out(t, geo, j - 1)
                    if A:
                        if j == 0: spread_a(s, FULL)
                        if j == 1: q_prod(s, FULL); kv_prod(s, FULL)
                        if j == 3: kv_outer(s, FULL)
                if Bs:
                    expert_out(t, geo, E - 1)
                    out_tokens(t, geo)

            def expert_bias_first(t, geo):
                pe.wait_ge(gatesc_set, t + 1)
                expert_bias(t, geo)

            pe.wait_ge(pack_loaded, 16)
            pe.wait_ge(setup_dve, SETUP_DVE)
            for s_, n_ in ((attn_done, 1), (w3_done, UNITS)):
                pe.sem_inc(s_, n_)
            prime_pe = [w1_done, wo_done, ms_done, rxb_done, ctrb_done, varb_done, rxc_done, router_done,
                        logit_done, gt_done, attc_done, outt_done]
            for s_ in prime_pe:
                pe.sem_inc(s_, 1)
            pe.sem_inc(s_done, UNITS)
            for s_ in (fh1_done, fgb_done, fh2_done, fw3_done):
                pe.sem_inc(s_, E)
            center_a(0, CLS, cls_h)
            var_mean_a(0, CLS)
            spread_a(0, CLS)
            q_prod(0, CLS)
            kv_prod(0, CLS)
            kv_outer(0, CLS)
            with pe.Fori(0, CHUNKS) as c:
                step(c + 1, None)
            cls_attention(0)
            with pe.Fori(1, PAIRS) as i:
                with pe.Fori(0, CHUNKS) as c:
                    s = i * CHUNKS + c + 1
                    step(s, s - CHUNKS)
                cls_attention(i)
            with pe.Fori(0, CHUNKS) as c:
                step(None, c + (PAIRS - 1) * CHUNKS + 1)
            step(None, PAIRS * CHUNKS + 1, CLS)

        @block.scalar
        def _(act):
            def unfold_hidden_hi(s):
                act.wait_ge(h1_set, s + 1)
                act.wait_ge(s_done, UNITS * s)
                for img in range(2):
                    act.activation(h1s[img][half(img), :], h1[half(img), :], ACT.Copy).then_inc(h1hi_set, 1)

            def gate_tanh(s, u):
                m = 4 if u == 0 else (u - 1) // 2
                act.wait_ge(s_done, UNITS * s + u + 1)
                act.wait_ge(gated_set, UNITS * s + u - 2)
                act.activation(th[u % 3][:, :], bank(S0 + u % 2), ACT.Tanh, bias=b2_half[:, m:m + 1],
                               scale=0.5).then_inc(th_set, 1)

            def unfold_out(s):
                act.wait_ge(w3_done, UNITS * (s + 1))
                act.wait_ge(ring_stored, 48 * s)
                act.activation(h_new[:, :], bank(L0), ACT.Identity, bias=cst("b3")).then_inc(h_set, 1)

            def square_a(s, geo):
                n = geo[0] * geo[1]
                act.wait_ge(xca_set, s + 1)
                act.activation(sq_a[:, 0:n], xc_a[:, 0:n], ACT.Square).then_inc(sqa_set, 1)

            def exp_q(s, geo):
                n = geo[0] * geo[1]
                act.wait_ge(q_done, s + 1)
                act.activation(eq[:, 0:n], bank(L1, n), ACT.Exp).then_inc(eq_set, 1)

            def exp_k(s, geo):
                nt, tw = geo
                act.wait_ge(kv_done, s + 1)
                for b in range((nt + 1) // 2):
                    k = min(2, nt - 2 * b)
                    src = ps[0:tw, S0 + b, 0:2 * P * k].rearrange("p (k c) -> p k c", k=k)
                    act.activation(ek[0:tw, 2 * b:2 * b + k, :], src[:, :, 0:P], ACT.Exp).then_inc(ek_set, 1)
                    op = act.activation(v_tok[0:tw, 2 * b:2 * b + k, 0:P], src[:, :, P:2 * P], ACT.Copy)
                    if b == (nt + 1) // 2 - 1:
                        op.then_inc(v_set, 1)
                if nt == 1:
                    act.sem_inc(ek_set, 1)

            def att_copy(t):
                act.wait_ge(attc_done, t + 1)
                act.activation(att_c[:, :], bank(F6), ACT.Copy).then_inc(attc_set, 1)

            def square_b(t, geo):
                n = geo[0] * geo[1]
                act.wait_ge(h2_set, t + 1)
                act.activation(sq_b[:, 0:n], h2[:, 0:n], ACT.Square).then_inc(sqb_set, 1)

            def square_c(t, geo):
                n = geo[0] * geo[1]
                act.wait_ge(xcb_set, t + 1)
                act.activation(sq_c[:, 0:n], xc_b[:, 0:n], ACT.Square).then_inc(sqc_set, 1)

            def y_hi(t, geo):
                n = geo[0] * geo[1]
                act.wait_ge(y_set, t + 1)
                for img in range(2):
                    act.activation(ys[img][half(img), 0:n], y[half(img), 0:n], ACT.Copy).then_inc(yhi_set, 1)

            def router_relu(t, geo):
                n = geo[0] * geo[1]
                act.wait_ge(router_done, t + 1)
                act.activation(rh[:, 0:n], ps[0:2 * RH, F6, 0:n], ACT.Relu,
                               bias=cst("rb1")[0:2 * RH]).then_inc(rh_set, 1)

            def gate_exp(t, geo):
                nt, tw = geo
                w = 2 * nt * E
                act.wait_ge(gate_step, GATE_STEPS * t + 3)
                act.activation(g_exp[0:tw, 0:w], g_shift[0:tw, 0:w], ACT.Exp).then_inc(gexp_set, 1)

            def gate_exp_top(t, geo):
                nt, tw = geo
                act.wait_ge(gate_step, GATE_STEPS * t + 15)
                act.activation(g_ed[0:tw, 0:2 * nt], g_dif[0:tw, 0:2 * nt], ACT.Exp).then_inc(ged_set, 1)

            def gates_copy(t, geo):
                n = geo[0] * geo[1]
                act.wait_ge(gt_done, t + 1)
                act.activation(gates_c[:, 0:n], ps[0:4 * E, F6, 0:n], ACT.Copy).then_inc(gatesc_set, 1)

            def relu1(t, geo, j):
                n = geo[0] * geo[1]
                act.wait_ge(fh1_done, E * t + j + 1)
                act.wait_ge(fh2_done, E * t + j - 1)
                act.activation(f1[j % 2][:, 0:n], bank(F7, n), ACT.Relu,
                               bias=cst("eb1")[:, j // 2:j // 2 + 1]).then_inc(f1_set, 1)

            def relu2(t, geo, j):
                n = geo[0] * geo[1]
                act.wait_ge(fh2_done, E * t + j + 1)
                act.wait_ge(gh_set, E * t + j - 1)
                act.activation(f2[j % 2][:, 0:n], bank(F5, n), ACT.Relu,
                               bias=cst("eb2")[:, j // 2:j // 2 + 1]).then_inc(f2_set, 1)

            def out_copy(t, geo):
                nt, tw = geo
                act.wait_ge(outt_done, t + 1)
                act.wait_ge(out_stored, 32 * t)
                act.activation(out_t[0:tw, 0:nt * P], ps[0:tw, F5, 0:nt * P], ACT.Copy).then_inc(outt_set, 1)

            def step(s, t, geo=FULL):
                A, Bs = s is not None, t is not None
                if A: unfold_hidden_hi(s)
                if Bs and geo is FULL: att_copy(t)
                if Bs and geo is CLS:
                    act.wait_ge(clsatt_set, PAIRS)
                    act.wait_ge(wo_done, t)
                    act.activation(att_c[:, 0:NCLS], cls_att[:, :], ACT.Copy).then_inc(attc_set, 1)
                if A: gate_tanh(s, 0); gate_tanh(s, 1); gate_tanh(s, 2)
                if Bs: square_b(t, geo)
                if A: gate_tanh(s, 3); gate_tanh(s, 4); gate_tanh(s, 5)
                if Bs: square_c(t, geo)
                if A: gate_tanh(s, 6); gate_tanh(s, 7)
                if A: gate_tanh(s, 8)
                if Bs: y_hi(t, geo); router_relu(t, geo)
                if A: unfold_out(s)
                if Bs: relu1(t, geo, 0)
                if A: square_a(s, FULL)
                if Bs: gate_exp(t, geo); gate_exp_top(t, geo); gates_copy(t, geo)
                for j in range(E):
                    if Bs:
                        if j + 1 < E: relu1(t, geo, j + 1)
                        relu2(t, geo, j)
                    if A and j == 1: exp_q(s, FULL); exp_k(s, FULL)
                if Bs: out_copy(t, geo)

            act.wait_ge(pack_loaded, 16)
            act.activation(b2_half[:, :], cst("b2"), ACT.Copy, scale=0.5).then_inc(setup_act, 1)
            act.activation(w3_half[:, :], cst("w3"), ACT.Copy, scale=0.5).then_inc(setup_act, 1)
            act.wait_ge(setup_act, 2)
            act.sem_inc(th_set, UNITS)
            act.sem_inc(h1hi_set, 2)
            act.sem_inc(h_set, 1)
            for s_ in (attc_set, sqb_set, sqc_set, rh_set, gexp_set, ged_set, gatesc_set, outt_set):
                act.sem_inc(s_, 1)
            act.sem_inc(yhi_set, 2)
            act.sem_inc(f1_set, E)
            act.sem_inc(f2_set, E)
            act.wait_ge(setup_dve, SETUP_DVE)
            square_a(0, CLS)
            exp_q(0, CLS)
            exp_k(0, CLS)
            with act.Fori(0, CHUNKS) as c:
                step(c + 1, None)
            with act.Fori(1, PAIRS) as i:
                with act.Fori(0, CHUNKS) as c:
                    s = i * CHUNKS + c + 1
                    step(s, s - CHUNKS)
            with act.Fori(0, CHUNKS) as c:
                step(None, c + (PAIRS - 1) * CHUNKS + 1)
            step(None, PAIRS * CHUNKS + 1, CLS)

        @block.gpsimd
        def _(pool):
            def power(dst, src, n, tw):
                return pool.tensor_tensor(dst[0:tw, 0:n], src[0:tw, 0:n], exponent[0:tw, 0:n], ALU.pow)

            def rstd_a_(s, geo):
                nt, tw = geo
                pool.wait_ge(var_set, 2 * s + 2)
                power(rstd_a, var_a, 4 * nt, tw).then_inc(rstda_set, 1)

            def sum_b_(t, geo, h):
                n = geo[0] * geo[1]
                pool.wait_ge(h2_set, t + 1)
                pool.wait_ge(h3_set, t)
                pool.tensor_tensor(sum_b[:, 0:n], h[:, 0:n], h2[:, 0:n], ALU.add).then_inc(sumb_set, 1)

            def rms_b_(t, geo):
                nt, tw = geo
                pool.wait_ge(msb_set, t + 1)
                power(rms_b, ms_b, 2 * nt, tw).then_inc(rmsb_set, 1)

            def rstd_b_(t, geo):
                nt, tw = geo
                pool.wait_ge(varb_set, t + 1)
                power(rstd_b, var_b, 2 * nt, tw).then_inc(rstdb_set, 1)

            def step(s, t, geo=FULL, h=cur[0]):
                if t is not None:
                    sum_b_(t, geo, h)
                    rms_b_(t, geo)
                    rstd_b_(t, geo)
                if s is not None:
                    rstd_a_(s, FULL)

            pool.wait_ge(setup_dve, SETUP_DVE)
            for s_ in (sumb_set, rmsb_set, rstdb_set):
                pool.sem_inc(s_, 1)
            rstd_a_(0, CLS)
            with pool.Fori(0, CHUNKS) as c:
                step(c + 1, None)
            with pool.Fori(1, PAIRS) as i:
                with pool.Fori(0, CHUNKS) as c:
                    s = i * CHUNKS + c + 1
                    step(s, s - CHUNKS)
            with pool.Fori(0, CHUNKS) as c:
                step(None, c + (PAIRS - 1) * CHUNKS + 1)
            step(None, PAIRS * CHUNKS + 1, CLS, cls_h)

        @block.vector
        def _(dve):
            def unfold_hidden(s):
                dve.wait_ge(w1_done, s + 1)
                dve.wait_ge(h1lo_set, 2 * s)
                dve.tensor_scalar(h1[:, :], bank(L0), cst("b1"), 0.0, ALU.add, ALU.max).then_inc(h1_set, 1)
                dve.wait_ge(h1_set, s + 1)
                for img in range(2):
                    dve.wait_ge(h1hi_set, 2 * s + 1 + img)
                    dve.tensor_tensor(h1s[img][half(1 - img), :], h1[half(img), :],
                                      h1s[img][half(img), :].bitcast(F32), ALU.subtract).then_inc(h1lo_set, 1)

            def gate_pixels(s, u):
                dve.wait_ge(th_set, UNITS * s + u + 1)
                dve.wait_ge(w3_done, UNITS * s + u - 2)
                dve.scalar_tensor_tensor(as_rows(gated[u % 3][:, :]), as_rows(th[u % 3][:, :]), 1.0, x_view(u),
                                         ALU.add, ALU.mult).then_inc(gated_set, 1)

            def centered_a(s, geo):
                n = geo[0] * geo[1]
                dve.wait_ge(ctr_done, s + 1)
                dve.tensor_copy(xc_a[:, 0:n], bank(L1, n)).then_inc(xca_set, 1)

            def deviations_a(s, geo):
                nt, tw = geo
                n = 2 * nt
                dve.wait_ge(vara_done, s + 1)
                dve.tensor_scalar(var_a[0:tw, 0:n], ps[0:tw, L0, 0:n], EPS_LN, None, ALU.add).then_inc(var_set, 1)
                dve.tensor_scalar(var_a[0:tw, n:2 * n], ps[0:tw, L0, 0:n], 1.0 + EPS_RMS, EPS_LN * EPS_RMS,
                                  ALU.mult, ALU.add).then_inc(var_set, 1)

            def spread_copy(dst, src, nt, tw, done):
                return dve.tensor_copy(dst.rearrange("p (g c) -> p g c", c=C),
                                       src.unsqueeze(2).to_broadcast([tw, 2 * nt, C])).then_inc(done, 1)

            def spread_a(s, geo):
                nt, tw = geo
                dve.wait_ge(rstda_set, s + 1)
                for k in range(2):
                    spread_copy(rx_a[0:tw, k, 0:nt * P], rstd_a[0:tw, 2 * nt * k:2 * nt * (k + 1)], nt, tw, rxa_set)

            def normed_a(s, geo, hn):
                n = geo[0] * geo[1]
                dve.wait_ge(rxa_done, s + 1)
                dve.wait_ge(xca_set, s + 1)
                if s is not 0:
                    dve.wait_ge(ring_stored, 48 * s)
                dve.tensor_tensor(hn[:, 0:n], xc_a[:, 0:n], bank(L1, n), ALU.mult).then_inc(hn_set, 1)
                dve.tensor_tensor(u_a[:, 0:n], xc_a[:, 0:n], bank(L0, n), ALU.mult).then_inc(u_set, 1)

            def elu_q(s, geo, q):
                n = geo[0] * geo[1]
                dve.wait_ge(eq_set, s + 1)
                dve.tensor_scalar(eq1[:, 0:n], eq[:, 0:n], 1.0, None, ALU.min).then_inc(eq1_set, 1)
                dve.wait_ge(eq1_set, s + 1)
                dve.scalar_tensor_tensor(q[:, 0:n], bank(L1, n), 1.0, eq1[:, 0:n], ALU.add, ALU.max).then_inc(qf_set, 1)

            def elu_k(s, geo):
                nt, tw = geo
                dve.wait_ge(ek_set, 2 * s + 2)
                dve.wait_ge(v_set, s + 1)
                dve.tensor_scalar(ek1[0:tw, 0:nt, :], ek[0:tw, 0:nt, :], 1.0, None, ALU.min).then_inc(ek1_set, 1)
                dve.wait_ge(ek1_set, s + 1)
                for b in range((nt + 1) // 2):
                    k = min(2, nt - 2 * b)
                    src = ps[0:tw, S0 + b, 0:2 * P * k].rearrange("p (k c) -> p k c", k=k)
                    dve.scalar_tensor_tensor(k_tok[0:tw, 2 * b:2 * b + k, :], src[:, :, 0:P], 1.0,
                                             ek1[0:tw, 2 * b:2 * b + k, :], ALU.add, ALU.max).then_inc(kf_set, 1)
                if nt == 1:
                    dve.sem_inc(kf_set, 1)

            def sum_kv(s):
                dve.wait_ge(kvp_done, s + 1)
                if s is 0:
                    dve.tensor_copy(kv_cls[:, :], bank(L0, P + 2)).then_inc(kvsum_set, 1)
                else:
                    dve.wait_ge(kvsum_set, s)
                    dve.tensor_tensor(kv_sum[:, :], kv_sum[:, :], bank(L0, P + 2), ALU.add).then_inc(kvsum_set, 1)

            def image_end(i, s, t):
                dve.wait_ge(kvsum_set, s)
                if t is not None:
                    dve.wait_ge(attn_done, t)
                    dve.wait_ge(clsatt_set, i)
                lo, _ = COLS["head_mask"]
                dve.tensor_tensor(kv_m[:, 0:P], kv_sum[:, 0:P], packed[:, lo:lo + P], ALU.mult)
                dve.tensor_scalar(kv_m[:, P:], packed[:, lo + P:lo + P + 2 * HEADS], kv_sum[:, P:P + 1], None,
                                  ALU.mult)
                dve.tensor_scalar(k_m[:, :], packed[:, lo:lo + P], kv_sum[:, P:P + 1], None,
                                  ALU.mult).then_inc(kvm_set, 1)
                dve.wait_ge(kvm_set, i + 1)
                dve.tensor_copy(kv_sum[:, :], kv_cls[:, :]).then_inc(clsden_set, 1)
                dve.wait_ge(clsatt_done, i + 1)
                dve.tensor_scalar(cls_den[:, 0:1], ps[:, L1, 1:2], EPS_ATT, None, ALU.add).then_inc(clsden_set, 1)
                dve.wait_ge(clsden_set, 3 * i + 2)
                dve.reciprocal(cls_den[:, 1:2], cls_den[:, 0:1]).then_inc(clsden_set, 1)
                dve.wait_ge(clsden_set, 3 * i + 3)
                dve.tensor_tensor(cls_att[:, bass.ds(i, 1)], cls_den[:, 1:2], ps[:, L1, 0:1],
                                  ALU.mult).then_inc(clsatt_set, 1)

            def attended(t):
                dve.wait_ge(attn_done, t + 1)
                wide = P + 2 * HEADS
                for b in range(2):
                    src = ps[0:TILE, M0 + b, 0:2 * wide].rearrange("p (k c) -> p k c", k=2)
                    dve.tensor_scalar(den[:, 32 * b:32 * b + 32].rearrange("p (k c) -> p k c", k=2),
                                      src[:, :, P:wide], EPS_ATT, None, ALU.add).then_inc(den_set, 1)
                dve.wait_ge(den_set, 2 * t + 2)
                dve.reciprocal(zed[:, :], den[:, :]).then_inc(zed_set, 1)
                dve.wait_ge(zed_set, t + 1)
                for k in range(NT):
                    src = ps[0:TILE, M0 + k // 2, wide * (k % 2):wide * (k % 2) + P]
                    op = dve.tensor_tensor(att[:, k * P:(k + 1) * P].rearrange("p (h c) -> p h c", c=HD),
                                           zed[:, 16 * k:16 * k + 16].unsqueeze(2).to_broadcast([TILE, 16, HD]),
                                           src.rearrange("p (h c) -> p h c", c=HD), ALU.mult)
                    if k % 2 == 1:
                        op.then_inc(att_set, 1)

            def residual(t, geo, hn):
                n = geo[0] * geo[1]
                dve.wait_ge(wo_done, t + 1)
                dve.wait_ge(sumb_set, t)
                dve.scalar_tensor_tensor(h2[:, 0:n], bank(M0, n), cst("bo"), hn[:, 0:n], ALU.add,
                                         ALU.add).then_inc(h2_set, 1)

            def mean_sq_b(t, geo):
                nt, tw = geo
                dve.wait_ge(ms_done, t + 1)
                dve.tensor_scalar(ms_b[0:tw, 0:2 * nt], ps[0:tw, F5, 0:2 * nt], EPS_RMS, None,
                                  ALU.add).then_inc(msb_set, 1)

            def spread_b(t, geo):
                nt, tw = geo
                dve.wait_ge(rmsb_set, t + 1)
                spread_copy(rx_b[0:tw, 0:nt * P], rms_b[0:tw, 0:2 * nt], nt, tw, rxb_set)

            def block_out(t, geo):
                n = geo[0] * geo[1]
                dve.wait_ge(rxb_done, t + 1)
                dve.scalar_tensor_tensor(nrm_b[:, 0:n], h2[:, 0:n], cst("norm2"), bank(F5, n), ALU.mult,
                                         ALU.mult).then_inc(nrm_set, 1)
                dve.wait_ge(nrm_set, t + 1)
                dve.wait_ge(sumb_set, t + 1)
                dve.tensor_tensor(h3[:, 0:n], nrm_b[:, 0:n], sum_b[:, 0:n], ALU.add).then_inc(h3_set, 1)

            def centered_b(t, geo):
                n = geo[0] * geo[1]
                dve.wait_ge(ctrb_done, t + 1)
                dve.tensor_copy(xc_b[:, 0:n], bank(M0, n)).then_inc(xcb_set, 1)

            def variance_b(t, geo):
                nt, tw = geo
                dve.wait_ge(varb_done, t + 1)
                dve.tensor_scalar(var_b[0:tw, 0:2 * nt], ps[0:tw, F5, 0:2 * nt], EPS_LN, None,
                                  ALU.add).then_inc(varb_set, 1)

            def spread_c(t, geo):
                nt, tw = geo
                dve.wait_ge(rstdb_set, t + 1)
                spread_copy(rx_c[0:tw, 0:nt * P], rstd_b[0:tw, 0:2 * nt], nt, tw, rxc_set)

            def normed_b(t, geo):
                n = geo[0] * geo[1]
                dve.wait_ge(rxc_done, t + 1)
                dve.wait_ge(xcb_set, t + 1)
                dve.tensor_tensor(y[:, 0:n], xc_b[:, 0:n], bank(F5, n), ALU.mult).then_inc(y_set, 1)

            def normed_b_lo(t, geo):
                n = geo[0] * geo[1]
                dve.wait_ge(y_set, t + 1)
                for img in range(2):
                    dve.wait_ge(yhi_set, 2 * t + 1 + img)
                    dve.tensor_tensor(ys[img][half(1 - img), 0:n], y[half(img), 0:n],
                                      ys[img][half(img), 0:n].bitcast(F32), ALU.subtract).then_inc(ylo_set, 1)

            def gates_part(t, geo, part):
                nt, tw = geo
                g, w = 2 * nt, 2 * nt * E

                def flat(x):
                    return x[0:tw, 0:w]

                def grp(x):
                    return x[0:tw, 0:w].rearrange("p (g e) -> p g e", e=E)

                def one(x):
                    return x[0:tw, 0:g]

                def wide(x):
                    return x[0:tw, 0:g].unsqueeze(2).to_broadcast([tw, g, E])

                def after(k):
                    dve.wait_ge(gate_step, GATE_STEPS * t + k)

                if part == 0:
                    dve.wait_ge(logit_done, t + 1)
                    dve.tensor_tensor(flat(g_logit), ps[0:tw, F5, 0:w], cst("rb2")[0:tw, 0:w],
                                      ALU.add).then_inc(gate_step, 1)
                    after(1)
                    dve.tensor_reduce(one(g_max), grp(g_logit), AX_X, ALU.max).then_inc(gate_step, 1)
                    after(2)
                    dve.tensor_tensor(grp(g_shift), grp(g_logit), wide(g_max), ALU.subtract).then_inc(gate_step, 1)
                    return
                if part == 1:
                    dve.wait_ge(gexp_set, t + 1)
                    dve.tensor_reduce(one(g_tot), grp(g_exp), AX_X, ALU.add).then_inc(gate_step, 1)
                    after(4)
                    dve.reciprocal(one(g_inv), one(g_tot)).then_inc(gate_step, 1)
                    after(5)
                    dve.tensor_tensor(grp(g_p), grp(g_exp), wide(g_inv), ALU.mult).then_inc(gate_step, 1)
                    after(6)
                    dve.tensor_reduce(one(g_top), grp(g_p), AX_X, ALU.max).then_inc(gate_step, 1)
                    after(7)
                    dve.tensor_tensor(grp(g_e1), grp(g_p), wide(g_top), ALU.is_equal).then_inc(gate_step, 1)
                    after(8)
                    dve.tensor_tensor(flat(g_w1), flat(g_e1), cst("order")[0:tw, 0:w], ALU.mult).then_inc(gate_step, 1)
                    after(9)
                    dve.tensor_reduce(one(g_i1), grp(g_w1), AX_X, ALU.max).then_inc(gate_step, 1)
                    after(10)
                    dve.tensor_tensor(grp(g_o1), grp(g_w1), wide(g_i1), ALU.is_equal).then_inc(gate_step, 1)
                    after(11)
                    dve.scalar_tensor_tensor(flat(g_rest), flat(g_o1), -4.0, flat(g_p), ALU.mult,
                                             ALU.add).then_inc(gate_step, 1)
                    after(12)
                    dve.tensor_reduce(one(g_top2), grp(g_rest), AX_X, ALU.max).then_inc(gate_step, 1)
                    after(13)
                    dve.tensor_tensor(grp(g_e2), grp(g_rest), wide(g_top2), ALU.is_equal).then_inc(gate_step, 1)
                    dve.tensor_tensor(one(g_dif), one(g_top2), one(g_top), ALU.subtract).then_inc(gate_step, 1)
                    after(14)
                    dve.tensor_tensor(flat(g_w2), flat(g_e2), cst("order")[0:tw, 0:w], ALU.mult).then_inc(gate_step, 1)
                    after(16)
                    dve.tensor_reduce(one(g_i2), grp(g_w2), AX_X, ALU.max).then_inc(gate_step, 1)
                    after(17)
                    dve.tensor_tensor(grp(g_o2), grp(g_w2), wide(g_i2), ALU.is_equal).then_inc(gate_step, 1)
                    return
                dve.wait_ge(ged_set, t + 1)
                dve.tensor_scalar(one(g_one), one(g_ed), 1.0, None, ALU.add).then_inc(gate_step, 1)
                after(19)
                dve.reciprocal(one(g_r1), one(g_one)).then_inc(gate_step, 1)
                after(20)
                dve.tensor_tensor(one(g_r2), one(g_r1), one(g_ed), ALU.mult)
                dve.tensor_tensor(grp(g_a), grp(g_o1), wide(g_r1), ALU.mult).then_inc(gate_step, 1)
                after(21)
                dve.tensor_tensor(grp(g_b), grp(g_o2), wide(g_r2), ALU.mult).then_inc(gate_step, 1)
                after(22)
                dve.tensor_tensor(flat(g_sum), flat(g_a), flat(g_b), ALU.add)
                by_tile = g_sum[0:tw, 0:w].rearrange("p (n e) -> p n e", n=nt)
                dve.tensor_tensor(g_parts[0:tw, 0:nt, 0, :], g_a[0:tw, 0:w].rearrange("p (n e) -> p n e", n=nt),
                                  g_b[0:tw, 0:w].rearrange("p (n e) -> p n e", n=nt), ALU.add).then_inc(gate_step, 1)
                after(23)
                dve.tensor_tensor(g_parts[0:tw, 0:nt, 1, :], by_tile, g_parts[0:tw, 0:nt, 0, :].bitcast(F32),
                                  ALU.subtract).then_inc(gate_step, 1)

            def gate_hidden(t, geo, j):
                n = geo[0] * geo[1]
                dve.wait_ge(f2_set, E * t + j + 1)
                dve.wait_ge(fgb_done, E * t + j + 1)
                dve.wait_ge(fw3_done, E * t + j - 1)
                dve.tensor_tensor(gh[j % 2][:, 0:n], f2[j % 2][:, 0:n], bank(F6, n), ALU.mult).then_inc(gh_set, 1)

            def result(t, geo):
                n = geo[0] * geo[1]
                dve.wait_ge(fw3_done, E * (t + 1))
                dve.wait_ge(outt_done, t)
                dve.tensor_tensor(res[:, 0:n], h3[:, 0:n], bank(M0, n), ALU.add).then_inc(res_set, 1)

            def step(s, t, geo=FULL, hn=cur[1]):
                A, Bs = s is not None, t is not None
                if Bs and geo is FULL: attended(t)
                if A: unfold_hidden(s)
                if A: gate_pixels(s, 0); gate_pixels(s, 1)
                if Bs: residual(t, geo, hn)
                if A: gate_pixels(s, 2)
                if Bs: mean_sq_b(t, geo)
                if A: gate_pixels(s, 3); gate_pixels(s, 4)
                if Bs: spread_b(t, geo); block_out(t, geo)
                if A: gate_pixels(s, 5)
                if Bs: centered_b(t, geo)
                if A: gate_pixels(s, 6)
                if Bs: variance_b(t, geo)
                if A: gate_pixels(s, 7)
                if Bs: spread_c(t, geo)
                if A: gate_pixels(s, 8)
                if Bs: normed_b(t, geo); normed_b_lo(t, geo)
                if A: centered_a(s, FULL)
                if Bs: gates_part(t, geo, 0)
                if A: deviations_a(s, FULL)
                if Bs: gates_part(t, geo, 1)
                if A: spread_a(s, FULL)
                if Bs: gates_part(t, geo, 2)
                if A and not Bs: normed_a(s, FULL, hn_new)
                for j in range(E):
                    if Bs: gate_hidden(t, geo, j)
                    if A and j == 0 and Bs: normed_a(s, FULL, hn_new)
                    if A and j == 2: elu_q(s, FULL, q_new); elu_k(s, FULL)
                    if A and j == 3: sum_kv(s)
                if Bs: result(t, geo)

            dve.wait_ge(pack_loaded, 16)
            dve.tensor_copy(split_hi[:, :], packed[:, 0:SPLIT_W]).then_inc(setup_dve, 1)
            dve.wait_ge(setup_dve, 1)
            dve.tensor_tensor(split_lo[:, :], packed[:, 0:SPLIT_W], split_hi[:, :].bitcast(F32),
                              ALU.subtract).then_inc(setup_dve, 1)
            dve.tensor_scalar(wqkv_n[:, :], cst("wqkv"), cst("norm1"), None, ALU.mult).then_inc(setup_dve, 1)
            dve.memset(exponent[:, :], -0.5).then_inc(setup_dve, 1)
            dve.memset(v_tok[:, :, :], 1.0).then_inc(setup_dve, 1)
            dve.wait_ge(setup_act, 2)
            dve.sem_inc(setup_dve, 2)
            dve.sem_inc(gated_set, UNITS)
            for s_ in (h1_set, den_set, den_set, zed_set, att_set, att_set, h2_set, msb_set, rxb_set, nrm_set, h3_set,
                       xcb_set, varb_set, rxc_set, y_set, res_set):
                dve.sem_inc(s_, 1)
            dve.sem_inc(h1lo_set, 2)
            dve.sem_inc(ylo_set, 2)
            dve.sem_inc(gate_step, GATE_STEPS)
            dve.sem_inc(gh_set, E)
            centered_a(0, CLS)
            deviations_a(0, CLS)
            spread_a(0, CLS)
            normed_a(0, CLS, cls_hn)
            elu_q(0, CLS, cls_q)
            elu_k(0, CLS)
            sum_kv(0)
            dve.wait_ge(kvsum_set, 1)
            dve.tensor_copy(kv_sum[:, :], kv_cls[:, :]).then_inc(setup_dve, 1)
            dve.wait_ge(setup_dve, SETUP_DVE + 1)
            with dve.Fori(0, CHUNKS) as c:
                step(c + 1, None)
            image_end(0, CHUNKS + 1, None)
            with dve.Fori(1, PAIRS) as i:
                with dve.Fori(0, CHUNKS) as c:
                    s = i * CHUNKS + c + 1
                    step(s, s - CHUNKS)
                image_end(i, i * CHUNKS + CHUNKS + 1, i * CHUNKS + 1)
            with dve.Fori(0, CHUNKS) as c:
                step(None, c + (PAIRS - 1) * CHUNKS + 1)
            step(None, PAIRS * CHUNKS + 1, CLS, cls_hn)


def kernel(**inputs):
    import concourse.bacc as bacc
    from concourse.bass_utils import run_bass_kernel_spmd

    a = {k: np.asarray(v) for k, v in inputs.items()}
    f32 = np.float32
    xpad = np.ascontiguousarray(np.pad(a["x"], ((0, 0), (0, 0), (1, 1), (1, 1))).reshape(B * C, PW * PW))

    def pair_diag(w):
        z = np.zeros((2 * w.shape[0], 2 * w.shape[1]), f32)
        z[:w.shape[0], :w.shape[1]] = w
        z[w.shape[0]:, w.shape[1]:] = w
        return z

    pack = np.zeros((P, PACK_W), f32)

    def put(name, v, at=0):
        lo, _ = COLS[name]
        pack[0:v.shape[0], lo + at:lo + at + v.shape[1]] = v

    w1, w2, w3 = a["L0_tok_W1"].reshape(C, 9, C), a["L0_tok_W2"].reshape(C, C, 9), a["L0_tok_W3"].reshape(C, 9, C)
    b2 = a["L0_tok_b2"].reshape(C, 9)

    def k_of(offset):
        return 3 * offset[0] + offset[1]

    for m, (o1, o2) in enumerate(OFFSET_PAIRS):
        put("w1", np.concatenate([w1[:, k_of(o1)], w1[:, k_of(o2)]]), m * C)
        put("w3", np.concatenate([w3[:, k_of(o1)], w3[:, k_of(o2)]]), m * C)
        both = np.concatenate([w2[:, :, k_of(o1)], w2[:, :, k_of(o2)]], axis=1)
        put("w2", np.concatenate([both, both]), m * P)
        put("b2", np.concatenate([b2[:, k_of(o1)], b2[:, k_of(o2)]])[:, None], m)
    last = k_of(LAST_OFFSET)
    put("w1", pair_diag(w1[:, last]), 4 * C)
    put("w3", pair_diag(w3[:, last]), 4 * C)
    for img in range(2):
        put("w2", np.concatenate([w2[:, :, last]] * 2), (4 + img) * P + 64 * img)
    put("b2", np.concatenate([b2[:, last]] * 2)[:, None], 4)
    wq, wk, wv = np.split(a["L0_attn_w_qkv"], 3, axis=1)
    put("wqkv", pair_diag(wq))
    put("wqkv", pair_diag(wk), P)
    put("wqkv", pair_diag(wv), 2 * P)
    put("wo", pair_diag(a["L0_attn_w_out"]))
    e1, e2, e3 = (a[f"L0_ffn_expert_w{k}"] for k in (1, 2, 3))
    eb1, eb2, eb3 = (a[f"L0_ffn_expert_b{k}"] for k in (1, 2, 3))
    for ep in range(E // 2):
        first = np.concatenate([e1[2 * ep], e1[2 * ep + 1]], axis=1)
        put("ew1", np.concatenate([first, first]), ep * P)
        put("ew2", e2[2 * ep], ep * P)
        lo, _ = COLS["ew2"]
        pack[64:, lo + ep * P + 64:lo + (ep + 1) * P] = e2[2 * ep + 1]
        put("ew3", np.concatenate([e3[2 * ep], e3[2 * ep + 1]]), ep * C)
        put("eb1", np.concatenate([eb1[2 * ep], eb1[2 * ep + 1]])[:, None], ep)
        put("eb2", np.concatenate([eb2[2 * ep], eb2[2 * ep + 1]])[:, None], ep)
    sel_at, eb3_at = COLS["gate_sel"][0], COLS["eb3"][0]
    for part in range(2):
        for img in range(2):
            for e in range(E):
                row = part * 2 * E + img * E + e
                j = 2 * (e // 2) + img
                at = sel_at + j * P + 64 * (e % 2)
                pack[row, at:at + 64] = 1.0
                pack[row, eb3_at + 64 * img:eb3_at + 64 * img + 64] = eb3[e]
    for img in range(2):
        put("rw1", np.concatenate([a["L0_ffn_router_w1"]] * 2), img * P + RH * img)
    put("rw2", pair_diag(a["L0_ffn_router_w2"]))
    put("ident", np.eye(P, dtype=f32))
    put("center", pair_diag(np.eye(C, dtype=f32) - f32(1.0 / C)))
    put("mean", pair_diag(np.full((C, 1), 1.0 / C, f32)))
    head = np.arange(P) // HD
    put("head_mask", (head[:, None] == head[None, :]).astype(f32))
    put("head_mask", (head[:, None] == np.arange(2 * HEADS)[None, :]).astype(f32), P)
    put("order", np.tile(np.arange(E, 0, -1, dtype=f32), (P, 2 * NT)))
    put("rb2", np.tile(a["L0_ffn_router_b2"], (P, 2 * NT)))
    put("cls", np.tile(np.concatenate([a["cls_tok"].reshape(C)] * 2)[:, None], (1, NCLS)))

    def column(name, v):
        put(name, np.concatenate([v, v])[:, None])

    column("b1", a["L0_tok_b1"])
    column("b3", a["L0_tok_b3"])
    column("norm1", a["L0_attn_w_norm1"])
    column("norm2", a["L0_attn_w_norm2"])
    column("bo", a["L0_attn_b_out"])
    column("rb1", a["L0_ffn_router_b1"])

    nc = bacc.Bacc("TRN2", target_bir_lowering=False, num_devices=1)
    ap_x = nc.dram_tensor("xpad", xpad.shape, F32, kind="ExternalInput").ap()
    ap_p = nc.dram_tensor("pack", pack.shape, F32, kind="ExternalInput").ap()
    ap_o = nc.dram_tensor("out", (B, TOKENS, C), F32, kind="ExternalOutput").ap()
    build(nc, ap_x, ap_p, ap_o)
    r = run_bass_kernel_spmd(nc, [{"xpad": xpad, "pack": pack}], core_ids=[0])
    return r.results[0]["out"]
```

```python
from contextlib import ExitStack

import numpy as np

import concourse.bass as bass
from concourse import mybir

F32 = mybir.dt.float32
F32R = mybir.dt.float32r
I32 = mybir.dt.int32
ALU = mybir.AluOpType
ACT = mybir.ActivationFunctionType
AX_X = mybir.AxisListType.X

B, C, H, W = 16, 64, 56, 56
HEADS, HD = 8, 8
E, RH = 6, 32
TOKENS = H * W + 1
P = 128
PW = W + 2
ROWS = 8
CHUNKS = H // ROWS
N = ROWS * W
WIDE = P + 2 * HEADS
TILE, NT = 112, 4
PAIRS = B // 2
NCLS = PAIRS
UNITS = 9
XC_LEN = 9 * PW + W
XR_LEN = 7 * PW + W
EPS_LN, EPS_RMS, EPS_ATT = 1e-5, 1e-6, 1e-6

OFFSET_PAIRS = [((0, 0), (0, 1)), ((1, 0), (1, 1)), ((2, 0), (2, 1)), ((0, 2), (1, 2))]
LAST_OFFSET = (2, 2)


def columns():
    widths = [
        ("w2", 6 * P), ("ew1", 3 * P), ("rw1", 2 * P), ("gate_sel", 6 * P), ("eb3", P),
        ("w1", 4 * C + P), ("w3", 4 * C + P), ("wqkv", 3 * P), ("wo", P), ("ew2", 3 * P), ("ew3", 3 * C),
        ("rw2", 2 * E), ("ident", P), ("center", P), ("mean", 2), ("head_mask", P + 2 * HEADS),
        ("order", NT * 2 * E), ("rb2", NT * 2 * E), ("cls", NCLS),
        ("b1", 1), ("b2", 5), ("b3", 1), ("norm1", 1), ("bo", 1), ("norm2", 1), ("rb1", 1), ("eb1", 3), ("eb2", 3),
    ]
    out, at = {}, 0
    for name, width in widths:
        out[name] = (at, at + width)
        at += width
    return out, at


COLS, PACK_W = columns()
SPLIT_W = COLS["eb3"][1]


def build(nc, xpad, pack, out):
    ctx = ExitStack()
    with ctx:
        def sb(name, shape, dt=F32):
            return ctx.enter_context(nc.sbuf_tensor(name, shape, dt))

        def sem(name):
            return ctx.enter_context(nc.semaphore(name))

        packed = sb("packed", [P, PACK_W])
        split_hi = sb("split_hi", [P, SPLIT_W], F32R)
        split_lo = sb("split_lo", [P, SPLIT_W], F32R)
        w3_half = sb("w3_half", [P, 4 * C + P])
        wqkv_n = sb("wqkv_n", [P, 3 * P])
        b2_half = sb("b2_half", [P, 5])
        exponent = sb("exponent", [TILE, 2 * NT])

        def cst(name, a=0, b=None):
            lo, hi = COLS[name]
            return packed[:, lo + a:(hi if b is None else lo + b)]

        def hi_of(name, a=0, b=None):
            lo, hi = COLS[name]
            return split_hi[:, lo + a:(hi if b is None else lo + b)]

        def lo_of(name, a=0, b=None):
            lo, hi = COLS[name]
            return split_lo[:, lo + a:(hi if b is None else lo + b)]

        xc = [sb(f"xc{m}", [P, 10 * PW]) for m in range(2)]
        xr = [sb(f"xr{m}", [P, ROWS * PW]) for m in range(2)]
        xp = sb("xp", [P, ROWS * PW])
        h1 = sb("h1", [P, N])
        h1s = [sb(f"h1s{m}", [P, N], F32R) for m in range(2)]
        th = [sb(f"th{k}", [P, N]) for k in range(3)]
        gated = [sb(f"gated{k}", [P, N]) for k in range(3)]
        h_new = sb("h_new", [P, N])
        hn_new = sb("hn_new", [P, N])
        q_new = sb("q_new", [P, N])
        sq_a = sb("sq_a", [P, N])
        xc_a = sb("xc_a", [P, N])
        u_a = sb("u_a", [P, N])
        var_u = sb("var_u", [TILE, 2 * NT])
        var_h = sb("var_h", [TILE, 2 * NT])
        rstd_u = sb("rstd_u", [TILE, 2 * NT])
        rstd_h = sb("rstd_h", [TILE, 2 * NT])
        rx_u = sb("rx_u", [TILE, NT * P])
        rx_h = sb("rx_h", [TILE, NT * P])
        eq = sb("eq", [P, N])
        eq1 = sb("eq1", [P, N])
        ek = sb("ek", [TILE, NT, P])
        ek1 = sb("ek1", [TILE, NT, P])
        k_tok = sb("k_tok", [TILE, NT, P])
        v_tok = sb("v_tok", [TILE, NT, P + 2])
        kv_sum = sb("kv_sum", [P, P + 2])
        kv_cls = sb("kv_cls", [P, P + 2])
        ring = [sb(f"ring_{n}", [P, CHUNKS * N]) for n in ("h", "hn", "q")]
        cur = [sb(f"cur_{n}", [P, N]) for n in ("h", "hn", "q")]
        cls_h = cst("cls")
        cls_hn = sb("cls_hn", [P, NCLS])
        cls_q = sb("cls_q", [P, NCLS])
        kv_m = sb("kv_m", [P, P + 2 * HEADS])
        k_m = sb("k_m", [P, P])
        cls_den = sb("cls_den", [P, 2])
        cls_att = sb("cls_att", [P, NCLS])
        den = sb("den", [TILE, NT * 2 * HEADS])
        zed = sb("zed", [TILE, NT * 2 * HEADS])
        att = sb("att", [TILE, NT * P])
        att_c = sb("att_c", [P, N])
        h2 = sb("h2", [P, N])
        sq_b = sb("sq_b", [P, N])
        ms_b = sb("ms_b", [TILE, 2 * NT])
        rms_b = sb("rms_b", [TILE, 2 * NT])
        rx_b = sb("rx_b", [TILE, NT * P])
        sum_b = sb("sum_b", [P, N])
        nrm_b = sb("nrm_b", [P, N])
        h3 = sb("h3", [P, N])
        h3_ffn = sb("h3_ffn", [P, N])
        sq_c = sb("sq_c", [P, N])
        xc_b = sb("xc_b", [P, N])
        var_b = sb("var_b", [TILE, 2 * NT])
        rstd_b = sb("rstd_b", [TILE, 2 * NT])
        rx_c = sb("rx_c", [TILE, NT * P])
        y = sb("y", [P, N])
        ys = [sb(f"ys{m}", [P, N], F32R) for m in range(2)]
        rh = sb("rh", [2 * RH, N])
        G = NT * 2
        gates_shape = [TILE, G * E]
        g_logit, g_shift, g_exp, g_p, g_e1, g_o1, g_rest, g_e2, g_o2, g_a, g_b, g_sum = (
            sb(f"g_{n}", gates_shape)
            for n in ("logit", "shift", "exp", "p", "e1", "o1", "rest", "e2", "o2", "a", "b", "sum"))
        g_w1, g_w2 = sb("g_w1", gates_shape), sb("g_w2", gates_shape)
        g_max, g_tot, g_inv, g_top, g_i1, g_top2, g_i2, g_dif, g_ed, g_one, g_r1, g_r2 = (
            sb(f"gs_{n}", [TILE, G])
            for n in ("max", "tot", "inv", "top", "i1", "top2", "i2", "dif", "ed", "one", "r1", "r2"))
        g_parts = sb("g_parts", [TILE, NT, 2, 2 * E], F32R)
        gates_c = sb("gates_c", [4 * E, N], F32R)
        f1 = [sb(f"f1_{k}", [P, N]) for k in range(2)]
        f2 = [sb(f"f2_{k}", [P, N]) for k in range(2)]
        gh = [sb(f"gh_{k}", [P, N]) for k in range(3)]
        res = sb("res", [P, N])
        out_t = sb("out_t", [TILE, NT * P])

        ps = ctx.enter_context(nc.psum_tensor("ps", [P, 8, 512], F32))
        S0, S1, L0, L1, M0, F5, F6, F7 = range(8)
        KV = (F7, F5)

        pack_loaded, x_loaded, cur_loaded = sem("pack_loaded"), sem("x_loaded"), sem("cur_loaded")
        ring_stored, out_stored = sem("ring_stored"), sem("out_stored")
        setup_dve, setup_act = sem("setup_dve"), sem("setup_act")
        (w1_done, s_done, w3_done, ctr_done, vara_done, rxu_done, rxh_done, q_done, kv_done, kvp_done,
         clsatt_done) = (
            sem(n) for n in ("w1_done", "s_done", "w3_done", "ctr_done", "vara_done", "rxu_done", "rxh_done",
                             "q_done", "kv_done", "kvp_done", "clsatt_done"))
        (attn_done, attc_done, wo_done, ms_done, rxb_done, ctrb_done, varb_done, rxc_done, router_done,
         logit_done, gt_done, fh1_done, fgb_done, fh2_done, fw3_done, outt_done) = (
            sem(n) for n in ("attn_done", "attc_done", "wo_done", "ms_done", "rxb_done", "ctrb_done",
                             "varb_done", "rxc_done", "router_done", "logit_done", "gt_done", "fh1_done",
                             "fgb_done", "fh2_done", "fw3_done", "outt_done"))
        (h1hi_set, th_set, h_set, sqa_set, eq_set, ek_set, v_set, attc_set, sqb_set, sqc_set, yhi_set, rh_set,
         gexp_set, ged_set, gatesc_set, f1_set, f2_set, outt_set) = (
            sem(n) for n in ("h1hi_set", "th_set", "h_set", "sqa_set", "eq_set", "ek_set", "v_set", "attc_set",
                             "sqb_set", "sqc_set", "yhi_set", "rh_set", "gexp_set", "ged_set", "gatesc_set",
                             "f1_set", "f2_set", "outt_set"))
        (h1_set, h1lo_set, gated_set, xca_set, var_set, rxu_set, rxh_set, hn_set, u_set, eq1_set, qf_set, ek1_set, kf_set,
         kvsum_set, kvm_set, clsden_set, clsatt_set) = (
            sem(n) for n in ("h1_set", "h1lo_set", "gated_set", "xca_set", "var_set", "rxu_set", "rxh_set", "hn_set", "u_set",
                             "eq1_set", "qf_set", "ek1_set", "kf_set", "kvsum_set", "kvm_set", "clsden_set",
                             "clsatt_set"))
        (den_set, zed_set, att_set, h2_set, msb_set, rxb_set, nrm_set, h3_set, xcb_set, varb_set, rxc_set, y_set,
         ylo_set, gate_step, gh_set, res_set) = (
            sem(n) for n in ("den_set", "zed_set", "att_set", "h2_set", "msb_set", "rxb_set", "nrm_set", "h3_set",
                             "xcb_set", "varb_set", "rxc_set", "y_set", "ylo_set", "gate_step", "gh_set",
                             "res_set"))
        rstdu_set, rstdh_set, rmsb_set, rstdb_set, sumb_set, h3f_set = (
            sem(n) for n in ("rstdu_set", "rstdh_set", "rmsb_set", "rstdb_set", "sumb_set", "h3f_set"))
        GATE_STEPS = 24
        SETUP_DVE = 7

        def x_view(unit):
            if unit == UNITS - 1:
                return xp[:, :].rearrange("p (r c) -> p r c", c=PW)[:, :, 0:W]
            m, img = unit // 2, unit % 2
            if m < 3:
                return xc[img][:, :].rearrange("p (r c) -> p r c", c=PW)[:, m:m + ROWS, 0:W]
            return xr[img][:, :].rearrange("p (r c) -> p r c", c=PW)[:, :, 0:W]

        def as_rows(ap):
            return ap.rearrange("p (r c) -> p r c", c=W)

        def bank(b, n=N, p0=0, p1=P):
            return ps[p0:p1, b, 0:n]

        def half(img):
            return slice(64 * img, 64 * img + 64)

        FULL, CLS = (NT, TILE), (1, NCLS)
        block = ctx.enter_context(nc.Block())

        @block.sync
        def _(sp):
            def prime(s, n):
                sp.sem_inc(s, n)

            prime(ring_stored, 48)
            prime(out_stored, 32)
            sp.dma_start(packed[:, :], pack).then_inc(pack_loaded, 16)

            def reg(v):
                return v if isinstance(v, int) else sp.snap(v)

            def settle():
                sp.wait_ge(pack_loaded, 16)

            def load_x(i, c, s):
                row, at, before = reg(i * P), reg(c * (ROWS * PW)), reg(UNITS * s)
                rows = [xpad[bass.ds(row + 64 * img, 64)] for img in range(2)]
                todo = []
                for img in range(2):
                    for part in range(2):
                        todo.append((xc[img][half(part), 0:XC_LEN], rows[img][:, bass.ds(at + part, XC_LEN)]))
                        todo.append((xr[img][half(part), 0:XR_LEN],
                                     rows[img][:, bass.ds(at + 2 + part * PW, XR_LEN)]))
                todo.append((xp[:, 0:XR_LEN], xpad[bass.ds(row, P)][:, bass.ds(at + 2 * PW + 2, XR_LEN)]))
                sp.wait_ge(gated_set, before)
                settle()
                for to, of in todo:
                    sp.dma_start(to, of).then_inc(x_loaded, 16)

            def load_cur(c, t):
                at, before, stored = reg(c * N), reg(t + 0), reg(48 * t + 48)
                sp.wait_ge(h3_set, before)
                sp.wait_ge(attn_done, before)
                sp.wait_ge(ring_stored, stored)
                settle()
                for to, of in zip(cur, ring):
                    sp.dma_start(to[:, :], of[:, bass.ds(at, N)]).then_inc(cur_loaded, 16)

            def store_ring(c, s, t):
                at, now = reg(c * N), reg(s + 1)
                loaded = None if t is None else reg(48 * t)
                if t is not None:
                    sp.wait_ge(cur_loaded, loaded)
                sp.wait_ge(h_set, now)
                sp.wait_ge(hn_set, now)
                sp.wait_ge(qf_set, now)
                settle()
                for to, of in zip(ring, (h_new, hn_new, q_new)):
                    sp.dma_start(to[:, bass.ds(at, N)], of[:, :]).then_inc(ring_stored, 16)

            def store_out(i, c, t):
                image, at, now = reg(i * 2), reg(c * N + 1), reg(t + 1)
                sp.wait_ge(outt_set, now)
                settle()
                for img in range(2):
                    dst = out[bass.ds(image + img, 1), bass.ds(at, N), :]
                    sp.dma_start(dst.rearrange("o (n p) c -> p (o n) c", p=TILE),
                                 out_t[:, :].rearrange("p (n m c) -> p n m c", m=2, c=C)[:, :, img, :]
                                 ).then_inc(out_stored, 16)

            def image(i, first=False, a=True):
                s = i * CHUNKS + 1
                t = s - CHUNKS
                if a:
                    load_x(i, 0, s)
                load_cur(0, t)
                store_ring(CHUNKS - 1, s - 1, None if first else t - 1)
                if not first:
                    store_out(i - 2, CHUNKS - 2, t - 2)
                if a:
                    load_x(i, 1, s + 1)
                load_cur(1, t + 1)
                if a:
                    store_ring(0, s, t)
                if not first:
                    store_out(i - 2, CHUNKS - 1, t - 1)
                with sp.Fori(2, CHUNKS) as c:
                    if a:
                        load_x(i, c, s + c)
                    load_cur(c, t + c)
                    if a:
                        store_ring(c - 1, s + c - 1, t + c - 1)
                    store_out(i - 1, c - 2, t + c - 2)

            load_x(0, 0, 1)
            with sp.Fori(1, CHUNKS) as c:
                load_x(0, c, c + 1)
                store_ring(c - 1, c, None)
            image(1, first=True)
            with sp.Fori(2, PAIRS) as i:
                image(i)
            image(PAIRS, a=False)
            last = PAIRS * CHUNKS
            store_out(PAIRS - 1, CHUNKS - 2, last - 1)
            store_out(PAIRS - 1, CHUNKS - 1, last)
            sp.wait_ge(outt_set, last + 2)
            cls_rows = out.rearrange("(i m) t c -> i m t c", m=2)[:, :, 0, :]
            sp.dma_start(cls_rows, out_t[0:NCLS, 0:P].rearrange("p (m c) -> p m c", m=2)).then_inc(out_stored, 16)
            sp.wait_ge(out_stored, 32 + 32 * last + 16)

        @block.tensor
        def _(pe):
            ident = cst("ident")

            def w1(s, part):
                if part == 0:
                    pe.wait_ge(x_loaded, 144 * s)
                    pe.wait_ge(h_set, s)
                for u in range(4 * part, 4 * part + 4):
                    m, img = u // 2, u % 2
                    pe.matmul(as_rows(bank(L0, p0=64 * img, p1=64 * img + 64)), cst("w1", m * C, (m + 1) * C),
                              x_view(u), start=(m == 0), stop=False)
                if part == 1:
                    pe.matmul(as_rows(bank(L0)), cst("w1", 4 * C), x_view(UNITS - 1), start=False,
                              stop=True).then_inc(w1_done, 1)

            def w2(s, u, f=None):
                if u < 2:
                    pe.wait_ge(h1lo_set, 2 * s + 1 + u)
                    if f is not None:
                        pe.wait_ge(f2_set if u else f1_set, E * f)
                else:
                    pe.wait_ge(th_set, UNITS * s + u - 1)
                b = S0 + u % 2
                if u == UNITS - 1:
                    todo = [(m, img, w) for m, img in ((4, 0), (5, 1)) for w in (hi_of, lo_of)]
                else:
                    todo = [(u // 2, u % 2, w) for w in (hi_of, lo_of)]
                for n, (m, img, w) in enumerate(todo):
                    mm = pe.matmul(bank(b), w("w2", m * P, (m + 1) * P), h1s[img][:, :],
                                   start=(n == 0), stop=(n == len(todo) - 1))
                mm.then_inc(s_done, 1)

            def w3(s, m):
                if m == 4:
                    pe.wait_ge(gated_set, UNITS * (s + 1))
                    pe.matmul(bank(L0), w3_half[:, 4 * C:], gated[(UNITS - 1) % 3][:, :], start=False,
                              stop=True).then_inc(w3_done, 1)
                    return
                for img in range(2):
                    u = 2 * m + img
                    pe.wait_ge(gated_set, UNITS * s + u + 1)
                    pe.matmul(bank(L0, p0=64 * img, p1=64 * img + 64), w3_half[:, m * C:(m + 1) * C],
                              gated[u % 3][:, :], start=(m == 0), stop=False).then_inc(w3_done, 1)

            def token_mean(b, src, geo, done):
                nt, tw = geo
                for k in range(nt):
                    mm = pe.matmul(ps[0:tw, b, 2 * k:2 * k + 2], src[:, k * tw:(k + 1) * tw], cst("mean"),
                                   start=True, stop=True)
                mm.then_inc(done, 1)

            def to_channels(b, src, geo):
                nt, tw = geo
                for k in range(nt):
                    mm = pe.transpose(bank(b)[:, k * tw:(k + 1) * tw], src[0:tw, k * P:(k + 1) * P],
                                      ident[0:tw, 0:tw])
                return mm

            def center_a(s, geo, h):
                n = geo[0] * geo[1]
                if s is not 0:
                    pe.wait_ge(h_set, s + 1)
                    pe.wait_ge(kvsum_set, s)
                pe.matmul(bank(L1, n), cst("center"), h[:, 0:n], start=True, stop=True).then_inc(ctr_done, 1)

            def var_mean_a(s, geo):
                pe.wait_ge(sqa_set, s + 1)
                pe.wait_ge(xca_set, s + 1)
                token_mean(L1, sq_a, geo, vara_done)

            def spread_u(s, geo):
                pe.wait_ge(rxu_set, s + 1)
                pe.wait_ge(var_set, 2 * s + 2)
                to_channels(L1, rx_u, geo).then_inc(rxu_done, 1)

            def spread_hn(s, geo):
                pe.wait_ge(rxh_set, s + 1)
                pe.wait_ge(qf_set, s + 1)
                to_channels(L1, rx_h, geo).then_inc(rxh_done, 1)

            def q_prod(s, geo):
                n = geo[0] * geo[1]
                pe.wait_ge(u_set, s + 1)
                pe.matmul(bank(L1, n), wqkv_n[:, 0:P], u_a[:, 0:n], start=True, stop=True).then_inc(q_done, 1)

            def kv_prod(s, geo, t=None, f=None):
                nt, tw = geo
                pe.wait_ge(u_set, s + 1)
                if s is not 0:
                    pe.wait_ge(kf_set, 2 * s)
                if t is not None:
                    pe.wait_ge(y_set, t + 1)
                if f is not None:
                    pe.wait_ge(gatesc_set, f + 1)
                for k in range(nt):
                    at = 2 * P * (k % 2)
                    mm = pe.matmul(ps[0:tw, KV[k // 2], at:at + 2 * P], u_a[:, k * tw:(k + 1) * tw],
                                   wqkv_n[:, P:3 * P], start=True, stop=True)
                mm.then_inc(kv_done, 1)

            def kv_outer(s, geo):
                nt, tw = geo if geo is FULL else (1, 1)
                pe.wait_ge(kf_set, 2 * s + 2)
                pe.wait_ge(v_set, s + 1)
                pe.wait_ge(hn_set, s + 1)
                for k in range(nt):
                    mm = pe.matmul(bank(L1, P + 2), k_tok[0:tw, k, :], v_tok[0:tw, k, :],
                                   start=(k == 0), stop=(k == nt - 1))
                mm.then_inc(kvp_done, 1)

            def cls_attention(i):
                pe.wait_ge(kvm_set, i + 1)
                pe.matmul(ps[:, L1, 0:1], kv_m[:, 0:P], cls_q[:, 0:1], start=True, stop=True)
                pe.matmul(ps[:, L1, 1:2], k_m[:, :], cls_q[:, 0:1], start=True, stop=True).then_inc(clsatt_done, 1)
                pe.wait_ge(clsatt_set, i + 1)

            def attention(t, s, g):
                pe.wait_ge(cur_loaded, 48 * t)
                if g is not None:
                    pe.wait_ge(res_set, g + 1)
                if s is not None:
                    pe.wait_ge(kf_set, 2 * s)
                pe.wait_ge(y_set, t)
                for k in range(NT):
                    at = (P + 2 * HEADS) * (k % 2)
                    mm = pe.matmul(ps[0:TILE, M0 + k // 2, at:at + P + 2 * HEADS],
                                   cur[2][:, k * TILE:(k + 1) * TILE], kv_m[:, :], start=True, stop=True)
                mm.then_inc(attn_done, 1)

            def att_channels(t, g):
                pe.wait_ge(att_set, 2 * t + 2)
                if g is not None:
                    pe.wait_ge(outt_set, g + 1)
                to_channels(F6, att, FULL).then_inc(attc_done, 1)

            def out_proj(t, geo):
                n = geo[0] * geo[1]
                pe.wait_ge(attc_set, t + 1)
                if geo is CLS:
                    pe.wait_ge(res_set, t - 1)
                pe.matmul(bank(M0, n), cst("wo"), att_c[:, 0:n], start=True, stop=True).then_inc(wo_done, 1)

            def mean_sq_b(t, geo):
                pe.wait_ge(sqb_set, t + 1)
                token_mean(F5, sq_b, geo, ms_done)

            def spread_b(t, geo):
                pe.wait_ge(rxb_set, t + 1)
                to_channels(F5, rx_b, geo).then_inc(rxb_done, 1)

            def center_b(t, geo):
                n = geo[0] * geo[1]
                pe.wait_ge(h3_set, t + 1)
                pe.matmul(bank(M0, n), cst("center"), h3[:, 0:n], start=True, stop=True).then_inc(ctrb_done, 1)

            def var_mean_b(t, geo):
                pe.wait_ge(sqc_set, t + 1)
                token_mean(F5, sq_c, geo, varb_done)

            def spread_c(t, geo):
                pe.wait_ge(rxc_set, t + 1)
                to_channels(F5, rx_c, geo).then_inc(rxc_done, 1)

            def router(t, geo, s):
                n = geo[0] * geo[1]
                if s is not None:
                    pe.wait_ge(kf_set, 2 * s)
                pe.wait_ge(gatesc_set, t)
                pe.wait_ge(yhi_set, 2 * t + 2)
                pe.wait_ge(ylo_set, 2 * t + 2)
                k = 0
                for img in range(2):
                    for w in (hi_of, lo_of):
                        mm = pe.matmul(bank(F7, n), w("rw1", img * P, (img + 1) * P), ys[img][:, 0:n],
                                       start=(k == 0), stop=(k == 3))
                        k += 1
                mm.then_inc(router_done, 1)

            def logits(t, geo):
                nt, tw = geo
                pe.wait_ge(rh_set, t + 1)
                for k in range(nt):
                    mm = pe.matmul(ps[0:tw, F7, 2 * E * k:2 * E * (k + 1)], rh[:, k * tw:(k + 1) * tw],
                                   cst("rw2")[0:2 * RH, :], start=True, stop=True)
                mm.then_inc(logit_done, 1)

            def gates_channels(t, geo):
                nt, tw = geo
                pe.wait_ge(gate_step, GATE_STEPS * (t + 1))
                for k in range(nt):
                    mm = pe.transpose(ps[0:4 * E, F7, k * tw:(k + 1) * tw],
                                      g_parts[0:tw, k].rearrange("p a e -> p (a e)").bitcast(F32),
                                      ident[0:tw, 0:tw])
                mm.then_inc(gt_done, 1)

            def expert_h1(t, geo, j, s=None):
                n = geo[0] * geo[1]
                ep, img = j // 2, j % 2
                pe.wait_ge(f1_set, E * t + j)
                if j == 0 and s is not None:
                    pe.wait_ge(th_set, UNITS * (s + 1))
                for w in (hi_of, lo_of):
                    mm = pe.matmul(bank(S0, n), w("ew1", ep * P, (ep + 1) * P), ys[img][:, 0:n],
                                   start=(w is hi_of), stop=(w is lo_of))
                mm.then_inc(fh1_done, 1)

            def expert_gate(t, geo, j, tb=None):
                n = geo[0] * geo[1]
                if j == 0:
                    pe.wait_ge(gatesc_set, t + 1)
                    pe.wait_ge(outt_set, t)
                    if tb is not None:
                        pe.wait_ge(attc_set, tb + 1)
                else:
                    pe.wait_ge(gh_set, E * t + j)
                pe.matmul(bank(F6, n), hi_of("gate_sel", j * P, (j + 1) * P)[0:4 * E], gates_c[:, 0:n],
                          start=True, stop=True).then_inc(fgb_done, 1)

            def expert_h2(t, geo, j):
                n = geo[0] * geo[1]
                ep = j // 2
                pe.wait_ge(f1_set, E * t + j + 1)
                pe.wait_ge(f2_set, E * t + j)
                pe.matmul(bank(S1, n), cst("ew2", ep * P, (ep + 1) * P), f1[j % 2][:, 0:n],
                          start=True, stop=True).then_inc(fh2_done, 1)

            def expert_bias(t, geo, tb):
                n = geo[0] * geo[1]
                pe.wait_ge(gatesc_set, t + 1)
                pe.wait_ge(res_set, t)
                if tb is not None:
                    pe.wait_ge(sqc_set, tb + 1)
                    pe.wait_ge(xcb_set, tb + 1)
                pe.matmul(bank(M0, n), hi_of("eb3")[0:4 * E], gates_c[:, 0:n], start=True, stop=False)
                pe.matmul(bank(M0, n), lo_of("eb3")[0:4 * E], gates_c[:, 0:n], start=False, stop=False)

            def expert_out(t, geo, ep):
                n = geo[0] * geo[1]
                for img in range(2):
                    j = 2 * ep + img
                    pe.wait_ge(gh_set, E * t + j + 1)
                    pe.matmul(bank(M0, n, 64 * img, 64 * img + 64), cst("ew3", ep * C, (ep + 1) * C),
                              gh[j % 3][:, 0:n], start=False, stop=(j >= E - 2)).then_inc(fw3_done, 1)

            def out_tokens(t, geo):
                nt, tw = geo
                pe.wait_ge(res_set, t + 1)
                for k in range(nt):
                    mm = pe.transpose(ps[0:tw, F6, k * P:(k + 1) * P], res[:, k * tw:(k + 1) * tw], ident)
                mm.then_inc(outt_done, 1)

            def step(s, t, f, g, geo_t=FULL, geo_f=FULL, geo_g=FULL):
                a, b, x, z = s is not None, t is not None, f is not None, g is not None
                if a: w1(s, 0); w1(s, 1)
                if z: expert_out(g, geo_g, 2)
                if x: router(f, geo_f, s)
                if b and geo_t is FULL: attention(t, s, g)
                if a: w2(s, 0, f); w2(s, 1, f)
                if x: logits(f, geo_f)
                if a: w2(s, 2)
                if z: out_tokens(g, geo_g)
                if a: w2(s, 3); w3(s, 0); w2(s, 4); w2(s, 5)
                if b and geo_t is FULL: att_channels(t, g)
                if a: w3(s, 1); w2(s, 6)
                if b: out_proj(t, geo_t)
                if a: w2(s, 7); w2(s, 8); w3(s, 2)
                if b: mean_sq_b(t, geo_t)
                if x: expert_h1(f, geo_f, 0, s)
                if a: w3(s, 3); w3(s, 4)
                if x: expert_h1(f, geo_f, 1); expert_h2(f, geo_f, 0)
                if a: center_a(s, FULL, h_new)
                if b: spread_b(t, geo_t)
                if x: expert_h2(f, geo_f, 1); expert_h1(f, geo_f, 2)
                if a: var_mean_a(s, FULL)
                if b: center_b(t, geo_t)
                if x: gates_channels(f, geo_f); expert_h1(f, geo_f, 3); expert_h2(f, geo_f, 2)
                if x: expert_gate(f, geo_f, 0, t)
                if b: var_mean_b(t, geo_t)
                if a: spread_u(s, FULL)
                if x: expert_gate(f, geo_f, 1); expert_bias(f, geo_f, t); expert_h1(f, geo_f, 4)
                if a: q_prod(s, FULL)
                if x: expert_out(f, geo_f, 0); expert_gate(f, geo_f, 2)
                if b: spread_c(t, geo_t)
                if x: expert_h2(f, geo_f, 3); expert_h1(f, geo_f, 5)
                if a: kv_prod(s, FULL, t, f)
                if x: expert_gate(f, geo_f, 3)
                if a: spread_hn(s, FULL)
                if x: expert_h2(f, geo_f, 4); expert_out(f, geo_f, 1); expert_gate(f, geo_f, 4)
                if x: expert_h2(f, geo_f, 5)
                if a: kv_outer(s, FULL)
                if x: expert_gate(f, geo_f, 5)

            pe.wait_ge(pack_loaded, 16)
            pe.wait_ge(setup_dve, SETUP_DVE)
            for s_, n_ in ((attn_done, 1), (w3_done, UNITS)):
                pe.sem_inc(s_, n_)
            prime_pe = [w1_done, wo_done, ms_done, rxb_done, ctrb_done, varb_done, rxc_done, router_done,
                        logit_done, gt_done, attc_done, outt_done]
            for s_ in prime_pe:
                pe.sem_inc(s_, 1)
            pe.sem_inc(s_done, UNITS)
            for s_ in (fh1_done, fgb_done, fh2_done, fw3_done):
                pe.sem_inc(s_, E)
            center_a(0, CLS, cls_h)
            var_mean_a(0, CLS)
            spread_u(0, CLS)
            q_prod(0, CLS)
            kv_prod(0, CLS)
            spread_hn(0, CLS)
            kv_outer(0, CLS)
            with pe.Fori(0, CHUNKS) as c:
                step(c + 1, None, None, None)
            cls_attention(0)
            step(CHUNKS + 1, 1, None, None)
            step(CHUNKS + 2, 2, 1, None)
            with pe.Fori(2, CHUNKS) as c:
                step(c + (CHUNKS + 1), c + 1, c + 0, c - 1)
            cls_attention(1)
            with pe.Fori(2, PAIRS) as i:
                with pe.Fori(0, CHUNKS) as c:
                    s = i * CHUNKS + c + 1
                    step(s, s - CHUNKS, s - (CHUNKS + 1), s - (CHUNKS + 2))
                cls_attention(i)
            with pe.Fori(0, CHUNKS) as c:
                t = c + ((PAIRS - 1) * CHUNKS + 1)
                step(None, t, t - 1, t - 2)
            last = PAIRS * CHUNKS
            step(None, last + 1, last, last - 1, CLS, FULL, FULL)
            step(None, None, last + 1, last, CLS, CLS, FULL)
            step(None, None, None, last + 1, CLS, CLS, CLS)

        @block.scalar
        def _(act):
            def hidden(s):
                act.wait_ge(w1_done, s + 1)
                act.wait_ge(h1lo_set, 2 * s)
                act.activation(h1[:, :], bank(L0), ACT.Relu, bias=cst("b1")).then_inc(h1_set, 1)

            def hidden_hi(s, img):
                act.wait_ge(w1_done, s + 1)
                act.wait_ge(s_done, UNITS * s)
                act.activation(h1s[img][half(img), :], bank(L0, p0=64 * img, p1=64 * img + 64), ACT.Relu,
                               bias=cst("b1")[half(img)]).then_inc(h1hi_set, 1)

            def gate_tanh(s, u):
                m = u // 2
                act.wait_ge(s_done, UNITS * s + u + 1)
                act.wait_ge(gated_set, UNITS * s + u - 2)
                act.activation(th[u % 3][:, :], bank(S0 + u % 2), ACT.Tanh, bias=b2_half[:, m:m + 1],
                               scale=0.5).then_inc(th_set, 1)

            def unfold_out(s):
                act.wait_ge(w3_done, UNITS * (s + 1))
                act.wait_ge(ring_stored, 48 * s)
                act.activation(h_new[:, :], bank(L0), ACT.Identity, bias=cst("b3")).then_inc(h_set, 1)

            def square_a(s, geo):
                n = geo[0] * geo[1]
                act.wait_ge(ctr_done, s + 1)
                act.activation(sq_a[:, 0:n], bank(L1, n), ACT.Square).then_inc(sqa_set, 1)

            def center_a(s, geo):
                n = geo[0] * geo[1]
                act.wait_ge(ctr_done, s + 1)
                act.activation(xc_a[:, 0:n], bank(L1, n), ACT.Copy).then_inc(xca_set, 1)

            def exp_q(s, geo):
                n = geo[0] * geo[1]
                act.wait_ge(q_done, s + 1)
                act.activation(eq[:, 0:n], bank(L1, n), ACT.Exp).then_inc(eq_set, 1)

            def exp_k(s, geo):
                nt, tw = geo
                act.wait_ge(kv_done, s + 1)
                for b in range((nt + 1) // 2):
                    k = min(2, nt - 2 * b)
                    src = ps[0:tw, KV[b], 0:2 * P * k].rearrange("p (k c) -> p k c", k=k)
                    act.activation(ek[0:tw, 2 * b:2 * b + k, :], src[:, :, 0:P], ACT.Exp).then_inc(ek_set, 1)
                    op = act.activation(v_tok[0:tw, 2 * b:2 * b + k, 0:P], src[:, :, P:2 * P], ACT.Copy)
                    if b == (nt + 1) // 2 - 1:
                        op.then_inc(v_set, 1)
                if nt == 1:
                    act.sem_inc(ek_set, 1)

            def cls_att_copy(t):
                act.wait_ge(clsatt_set, PAIRS)
                act.wait_ge(wo_done, t)
                act.activation(att_c[:, 0:NCLS], cls_att[:, :], ACT.Copy).then_inc(attc_set, 1)

            def att_copy(t):
                act.wait_ge(attc_done, t + 1)
                act.activation(att_c[:, :], bank(F6), ACT.Copy).then_inc(attc_set, 1)

            def square_b(t, geo):
                n = geo[0] * geo[1]
                act.wait_ge(h2_set, t + 1)
                act.activation(sq_b[:, 0:n], h2[:, 0:n], ACT.Square).then_inc(sqb_set, 1)

            def square_c(t, geo):
                n = geo[0] * geo[1]
                act.wait_ge(ctrb_done, t + 1)
                act.activation(sq_c[:, 0:n], bank(M0, n), ACT.Square).then_inc(sqc_set, 1)

            def center_b(t, geo):
                n = geo[0] * geo[1]
                act.wait_ge(ctrb_done, t + 1)
                act.activation(xc_b[:, 0:n], bank(M0, n), ACT.Copy).then_inc(xcb_set, 1)

            def y_hi(t, geo, f):
                n = geo[0] * geo[1]
                act.wait_ge(y_set, t + 1)
                if f is not None:
                    act.wait_ge(fh1_done, E * (f + 1))
                for img in range(2):
                    act.activation(ys[img][half(img), 0:n], y[half(img), 0:n], ACT.Copy).then_inc(yhi_set, 1)

            def router_relu(t, geo):
                n = geo[0] * geo[1]
                act.wait_ge(router_done, t + 1)
                act.activation(rh[:, 0:n], ps[0:2 * RH, F7, 0:n], ACT.Relu,
                               bias=cst("rb1")[0:2 * RH]).then_inc(rh_set, 1)

            def gate_exp(t, geo):
                nt, tw = geo
                w = 2 * nt * E
                act.wait_ge(gate_step, GATE_STEPS * t + 3)
                act.activation(g_exp[0:tw, 0:w], g_shift[0:tw, 0:w], ACT.Exp).then_inc(gexp_set, 1)

            def gate_exp_top(t, geo):
                nt, tw = geo
                act.wait_ge(gate_step, GATE_STEPS * t + 15)
                act.activation(g_ed[0:tw, 0:2 * nt], g_dif[0:tw, 0:2 * nt], ACT.Exp).then_inc(ged_set, 1)

            def gates_copy(t, geo):
                n = geo[0] * geo[1]
                act.wait_ge(gt_done, t + 1)
                act.wait_ge(fgb_done, E * t)
                act.activation(gates_c[:, 0:n], ps[0:4 * E, F7, 0:n], ACT.Copy).then_inc(gatesc_set, 1)

            def relu1(t, geo, j):
                n = geo[0] * geo[1]
                act.wait_ge(fh1_done, E * t + j + 1)
                act.wait_ge(fh2_done, E * t + j - 1)
                act.activation(f1[j % 2][:, 0:n], bank(S0, n), ACT.Relu,
                               bias=cst("eb1")[:, j // 2:j // 2 + 1]).then_inc(f1_set, 1)

            def relu2(t, geo, j):
                n = geo[0] * geo[1]
                act.wait_ge(fh2_done, E * t + j + 1)
                act.wait_ge(gh_set, E * t + j - 1)
                act.activation(f2[j % 2][:, 0:n], bank(S1, n), ACT.Relu,
                               bias=cst("eb2")[:, j // 2:j // 2 + 1]).then_inc(f2_set, 1)

            def out_copy(t, geo):
                nt, tw = geo
                act.wait_ge(outt_done, t + 1)
                act.wait_ge(out_stored, 32 * t)
                act.activation(out_t[0:tw, 0:nt * P], ps[0:tw, F6, 0:nt * P], ACT.Copy).then_inc(outt_set, 1)

            def step(s, t, f, g, geo_t=FULL, geo_f=FULL, geo_g=FULL):
                a, b, x, z = s is not None, t is not None, f is not None, g is not None
                if a: hidden_hi(s, 0); hidden(s); hidden_hi(s, 1)
                if x: router_relu(f, geo_f)
                if a: gate_tanh(s, 0); gate_tanh(s, 1); gate_tanh(s, 2)
                if z: out_copy(g, geo_g)
                if a: gate_tanh(s, 3); gate_tanh(s, 4); gate_tanh(s, 5)
                if b and geo_t is FULL: att_copy(t)
                if b and geo_t is CLS: cls_att_copy(t)
                if a: gate_tanh(s, 6)
                if x: gate_exp(f, geo_f)
                if a: gate_tanh(s, 7)
                if b: square_b(t, geo_t)
                if a: gate_tanh(s, 8)
                if x: relu1(f, geo_f, 0)
                if a: unfold_out(s)
                if x: relu1(f, geo_f, 1); gate_exp_top(f, geo_f); relu2(f, geo_f, 0)
                if a: square_a(s, FULL); center_a(s, FULL)
                if x: relu2(f, geo_f, 1); relu1(f, geo_f, 2)
                if b: square_c(t, geo_t)
                if x: gates_copy(f, geo_f)
                if b: center_b(t, geo_t)
                if x: relu1(f, geo_f, 3); relu2(f, geo_f, 2); relu1(f, geo_f, 4)
                if a: exp_q(s, FULL)
                if x: relu2(f, geo_f, 3); relu1(f, geo_f, 5)
                if b: y_hi(t, geo_t, f)
                if a: exp_k(s, FULL)
                if x: relu2(f, geo_f, 4); relu2(f, geo_f, 5)

            act.wait_ge(pack_loaded, 16)
            act.activation(b2_half[:, :], cst("b2"), ACT.Copy, scale=0.5).then_inc(setup_act, 1)
            act.activation(w3_half[:, :], cst("w3"), ACT.Copy, scale=0.5).then_inc(setup_act, 1)
            act.wait_ge(setup_act, 2)
            act.sem_inc(th_set, UNITS)
            act.sem_inc(h1_set, 1)
            act.sem_inc(h1hi_set, 2)
            act.sem_inc(xcb_set, 1)
            act.sem_inc(h_set, 1)
            for s_ in (attc_set, sqb_set, sqc_set, rh_set, gexp_set, ged_set, gatesc_set, outt_set):
                act.sem_inc(s_, 1)
            act.sem_inc(yhi_set, 2)
            act.sem_inc(f1_set, E)
            act.sem_inc(f2_set, E)
            act.wait_ge(setup_dve, SETUP_DVE)
            square_a(0, CLS)
            center_a(0, CLS)
            exp_q(0, CLS)
            exp_k(0, CLS)
            with act.Fori(0, CHUNKS) as c:
                step(c + 1, None, None, None)
            step(CHUNKS + 1, 1, None, None)
            step(CHUNKS + 2, 2, 1, None)
            with act.Fori(2, CHUNKS) as c:
                step(c + (CHUNKS + 1), c + 1, c + 0, c - 1)
            with act.Fori(2, PAIRS) as i:
                with act.Fori(0, CHUNKS) as c:
                    s = i * CHUNKS + c + 1
                    step(s, s - CHUNKS, s - (CHUNKS + 1), s - (CHUNKS + 2))
            with act.Fori(0, CHUNKS) as c:
                t = c + ((PAIRS - 1) * CHUNKS + 1)
                step(None, t, t - 1, t - 2)
            last = PAIRS * CHUNKS
            step(None, last + 1, last, last - 1, CLS, FULL, FULL)
            step(None, None, last + 1, last, CLS, CLS, FULL)
            step(None, None, None, last + 1, CLS, CLS, CLS)

        @block.gpsimd
        def _(pool):
            def power(dst, src, n, tw):
                return pool.tensor_tensor(dst[0:tw, 0:n], src[0:tw, 0:n], exponent[0:tw, 0:n], ALU.pow)

            def rstd_u_(s, geo):
                nt, tw = geo
                pool.wait_ge(var_set, 2 * s + 1)
                power(rstd_u, var_u, 2 * nt, tw).then_inc(rstdu_set, 1)

            def rstd_h_(s, geo):
                nt, tw = geo
                pool.wait_ge(var_set, 2 * s + 2)
                power(rstd_h, var_h, 2 * nt, tw).then_inc(rstdh_set, 1)

            def sum_b_(t, f, geo, h):
                n = geo[0] * geo[1]
                if f is not None:
                    pool.wait_ge(h3f_set, f + 1)
                pool.wait_ge(h2_set, t + 1)
                pool.wait_ge(h3_set, t)
                pool.tensor_tensor(sum_b[:, 0:n], h[:, 0:n], h2[:, 0:n], ALU.add).then_inc(sumb_set, 1)

            def rms_b_(t, geo):
                nt, tw = geo
                pool.wait_ge(msb_set, t + 1)
                power(rms_b, ms_b, 2 * nt, tw).then_inc(rmsb_set, 1)

            def rstd_b_(t, geo):
                nt, tw = geo
                pool.wait_ge(varb_set, t + 1)
                power(rstd_b, var_b, 2 * nt, tw).then_inc(rstdb_set, 1)

            def y_lo(t, s, geo):
                n = geo[0] * geo[1]
                pool.wait_ge(rstdb_set, t + 1)
                if s is not None:
                    pool.wait_ge(rstdh_set, s + 1)
                pool.wait_ge(y_set, t + 1)
                for img in range(2):
                    pool.wait_ge(yhi_set, 2 * t + 1 + img)
                    pool.tensor_tensor(ys[img][half(1 - img), 0:n], y[half(img), 0:n],
                                       ys[img][half(img), 0:n].bitcast(F32), ALU.subtract).then_inc(ylo_set, 1)
                    pool.wait_ge(ylo_set, 2 * t + 1 + img)

            def keep_h3(f, geo):
                n = geo[0] * geo[1]
                pool.wait_ge(nrm_set, f + 1)
                pool.wait_ge(sumb_set, f + 1)
                pool.wait_ge(res_set, f)
                pool.tensor_tensor(h3_ffn[:, 0:n], nrm_b[:, 0:n], sum_b[:, 0:n], ALU.add).then_inc(h3f_set, 1)

            def step(s, t, f, g, geo_t=FULL, geo_f=FULL, geo_g=FULL, h=cur[0]):
                a, b, x, z = s is not None, t is not None, f is not None, g is not None
                if x: keep_h3(f, geo_f)
                if b: sum_b_(t, f, geo_t, h); rms_b_(t, geo_t)
                if a: rstd_u_(s, FULL)
                if b: rstd_b_(t, geo_t)
                if a: rstd_h_(s, FULL)
                if b: y_lo(t, s, geo_t)

            pool.wait_ge(setup_dve, SETUP_DVE)
            for s_ in (sumb_set, rmsb_set, rstdb_set, h3f_set):
                pool.sem_inc(s_, 1)
            pool.sem_inc(ylo_set, 2)
            rstd_u_(0, CLS)
            rstd_h_(0, CLS)
            with pool.Fori(0, CHUNKS) as c:
                step(c + 1, None, None, None)
            step(CHUNKS + 1, 1, None, None)
            step(CHUNKS + 2, 2, 1, None)
            with pool.Fori(2, CHUNKS) as c:
                step(c + (CHUNKS + 1), c + 1, c + 0, c - 1)
            with pool.Fori(2, PAIRS) as i:
                with pool.Fori(0, CHUNKS) as c:
                    s = i * CHUNKS + c + 1
                    step(s, s - CHUNKS, s - (CHUNKS + 1), s - (CHUNKS + 2))
            with pool.Fori(0, CHUNKS) as c:
                t = c + ((PAIRS - 1) * CHUNKS + 1)
                step(None, t, t - 1, t - 2)
            last = PAIRS * CHUNKS
            step(None, last + 1, last, last - 1, CLS, FULL, FULL, cls_h)
            step(None, None, last + 1, last, CLS, CLS, FULL)
            step(None, None, None, last + 1, CLS, CLS, CLS)

        @block.vector
        def _(dve):
            def hidden_lo(s, img):
                dve.wait_ge(h1_set, s + 1)
                dve.wait_ge(h1hi_set, 2 * s + 1 + img)
                dve.tensor_tensor(h1s[img][half(1 - img), :], h1[half(img), :],
                                  h1s[img][half(img), :].bitcast(F32), ALU.subtract).then_inc(h1lo_set, 1)

            def gate_pixels(s, u):
                dve.wait_ge(th_set, UNITS * s + u + 1)
                dve.wait_ge(w3_done, UNITS * s + u - 2)
                dve.scalar_tensor_tensor(as_rows(gated[u % 3][:, :]), as_rows(th[u % 3][:, :]), 1.0, x_view(u),
                                         ALU.add, ALU.mult).then_inc(gated_set, 1)

            def deviations_a(s, geo):
                nt, tw = geo
                n = 2 * nt
                dve.wait_ge(vara_done, s + 1)
                dve.tensor_scalar(var_u[0:tw, 0:n], ps[0:tw, L1, 0:n], 1.0 + EPS_RMS, EPS_LN * EPS_RMS,
                                  ALU.mult, ALU.add).then_inc(var_set, 1)
                dve.tensor_scalar(var_h[0:tw, 0:n], ps[0:tw, L1, 0:n], EPS_LN, None, ALU.add).then_inc(var_set, 1)

            def spread_copy(dst, src, nt, tw, done):
                return dve.tensor_copy(dst.rearrange("p (g c) -> p g c", c=C),
                                       src.unsqueeze(2).to_broadcast([tw, 2 * nt, C])).then_inc(done, 1)

            def spread_u(s, geo):
                nt, tw = geo
                dve.wait_ge(rstdu_set, s + 1)
                spread_copy(rx_u[0:tw, 0:nt * P], rstd_u[0:tw, 0:2 * nt], nt, tw, rxu_set)

            def spread_hn(s, geo):
                nt, tw = geo
                dve.wait_ge(rstdh_set, s + 1)
                spread_copy(rx_h[0:tw, 0:nt * P], rstd_h[0:tw, 0:2 * nt], nt, tw, rxh_set)

            def normed_u(s, geo):
                n = geo[0] * geo[1]
                dve.wait_ge(rxu_done, s + 1)
                dve.wait_ge(xca_set, s + 1)
                dve.tensor_tensor(u_a[:, 0:n], xc_a[:, 0:n], bank(L1, n), ALU.mult).then_inc(u_set, 1)

            def normed_hn(s, geo, hn):
                n = geo[0] * geo[1]
                dve.wait_ge(rxh_done, s + 1)
                if s is not 0:
                    dve.wait_ge(ring_stored, 48 * s)
                dve.tensor_tensor(hn[:, 0:n], xc_a[:, 0:n], bank(L1, n), ALU.mult).then_inc(hn_set, 1)

            def elu_q_min(s, geo):
                n = geo[0] * geo[1]
                dve.wait_ge(eq_set, s + 1)
                dve.tensor_scalar(eq1[:, 0:n], eq[:, 0:n], 1.0, None, ALU.min).then_inc(eq1_set, 1)

            def elu_q(s, geo, q):
                n = geo[0] * geo[1]
                dve.wait_ge(eq1_set, s + 1)
                if s is not 0:
                    dve.wait_ge(ring_stored, 48 * s)
                dve.scalar_tensor_tensor(q[:, 0:n], bank(L1, n), 1.0, eq1[:, 0:n], ALU.add, ALU.max).then_inc(qf_set, 1)

            def elu_k_min(s, geo):
                nt, tw = geo
                dve.wait_ge(ek_set, 2 * s + 2)
                dve.tensor_scalar(ek1[0:tw, 0:nt, :], ek[0:tw, 0:nt, :], 1.0, None, ALU.min).then_inc(ek1_set, 1)

            def elu_k(s, geo):
                nt, tw = geo
                dve.wait_ge(ek1_set, s + 1)
                dve.wait_ge(v_set, s + 1)
                for b in range((nt + 1) // 2):
                    k = min(2, nt - 2 * b)
                    src = ps[0:tw, KV[b], 0:2 * P * k].rearrange("p (k c) -> p k c", k=k)
                    dve.scalar_tensor_tensor(k_tok[0:tw, 2 * b:2 * b + k, :], src[:, :, 0:P], 1.0,
                                             ek1[0:tw, 2 * b:2 * b + k, :], ALU.add, ALU.max).then_inc(kf_set, 1)
                if nt == 1:
                    dve.sem_inc(kf_set, 1)

            def sum_kv(s):
                dve.wait_ge(kvp_done, s + 1)
                if s is 0:
                    dve.tensor_copy(kv_cls[:, :], bank(L1, P + 2)).then_inc(kvsum_set, 1)
                else:
                    dve.wait_ge(kvsum_set, s)
                    dve.tensor_tensor(kv_sum[:, :], kv_sum[:, :], bank(L1, P + 2), ALU.add).then_inc(kvsum_set, 1)

            def image_end(i, s, t):
                dve.wait_ge(kvsum_set, s)
                if t is not None:
                    dve.wait_ge(attn_done, t)
                    dve.wait_ge(clsatt_set, i)
                lo, _ = COLS["head_mask"]
                dve.tensor_tensor(kv_m[:, 0:P], kv_sum[:, 0:P], packed[:, lo:lo + P], ALU.mult)
                dve.tensor_scalar(kv_m[:, P:], packed[:, lo + P:lo + P + 2 * HEADS], kv_sum[:, P:P + 1], None,
                                  ALU.mult)
                dve.tensor_scalar(k_m[:, :], packed[:, lo:lo + P], kv_sum[:, P:P + 1], None,
                                  ALU.mult).then_inc(kvm_set, 1)
                dve.wait_ge(kvm_set, i + 1)
                dve.tensor_copy(kv_sum[:, :], kv_cls[:, :]).then_inc(clsden_set, 1)
                dve.wait_ge(clsatt_done, i + 1)
                dve.tensor_scalar(cls_den[:, 0:1], ps[:, L1, 1:2], EPS_ATT, None, ALU.add).then_inc(clsden_set, 1)
                dve.wait_ge(clsden_set, 3 * i + 2)
                dve.reciprocal(cls_den[:, 1:2], cls_den[:, 0:1]).then_inc(clsden_set, 1)
                dve.wait_ge(clsden_set, 3 * i + 3)
                dve.tensor_tensor(cls_att[:, bass.ds(i, 1)], cls_den[:, 1:2], ps[:, L1, 0:1],
                                  ALU.mult).then_inc(clsatt_set, 1)

            def denominators(t):
                dve.wait_ge(attn_done, t + 1)
                for b in range(2):
                    src = ps[0:TILE, M0 + b, 0:2 * WIDE].rearrange("p (k c) -> p k c", k=2)
                    dve.tensor_scalar(den[:, 32 * b:32 * b + 32].rearrange("p (k c) -> p k c", k=2),
                                      src[:, :, P:WIDE], EPS_ATT, None, ALU.add).then_inc(den_set, 1)

            def inverses(t):
                dve.wait_ge(den_set, 2 * t + 2)
                dve.reciprocal(zed[:, :], den[:, :]).then_inc(zed_set, 1)

            def attended(t):
                dve.wait_ge(zed_set, t + 1)
                for k in range(NT):
                    src = ps[0:TILE, M0 + k // 2, WIDE * (k % 2):WIDE * (k % 2) + P]
                    op = dve.tensor_tensor(att[:, k * P:(k + 1) * P].rearrange("p (h c) -> p h c", c=HD),
                                           zed[:, 16 * k:16 * k + 16].unsqueeze(2).to_broadcast([TILE, 16, HD]),
                                           src.rearrange("p (h c) -> p h c", c=HD), ALU.mult)
                    if k % 2 == 1:
                        op.then_inc(att_set, 1)

            def residual(t, geo, hn):
                n = geo[0] * geo[1]
                dve.wait_ge(wo_done, t + 1)
                dve.wait_ge(sumb_set, t)
                dve.scalar_tensor_tensor(h2[:, 0:n], bank(M0, n), cst("bo"), hn[:, 0:n], ALU.add,
                                         ALU.add).then_inc(h2_set, 1)

            def mean_sq_b(t, geo):
                nt, tw = geo
                dve.wait_ge(ms_done, t + 1)
                dve.tensor_scalar(ms_b[0:tw, 0:2 * nt], ps[0:tw, F5, 0:2 * nt], EPS_RMS, None,
                                  ALU.add).then_inc(msb_set, 1)

            def spread_b(t, geo):
                nt, tw = geo
                dve.wait_ge(rmsb_set, t + 1)
                spread_copy(rx_b[0:tw, 0:nt * P], rms_b[0:tw, 0:2 * nt], nt, tw, rxb_set)

            def rms_normed(t, geo, f):
                n = geo[0] * geo[1]
                dve.wait_ge(rxb_done, t + 1)
                if f is not None:
                    dve.wait_ge(h3f_set, f + 1)
                dve.scalar_tensor_tensor(nrm_b[:, 0:n], h2[:, 0:n], cst("norm2"), bank(F5, n), ALU.mult,
                                         ALU.mult).then_inc(nrm_set, 1)

            def block_out(t, geo):
                n = geo[0] * geo[1]
                dve.wait_ge(nrm_set, t + 1)
                dve.wait_ge(sumb_set, t + 1)
                dve.tensor_tensor(h3[:, 0:n], nrm_b[:, 0:n], sum_b[:, 0:n], ALU.add).then_inc(h3_set, 1)

            def variance_b(t, geo):
                nt, tw = geo
                dve.wait_ge(varb_done, t + 1)
                dve.tensor_scalar(var_b[0:tw, 0:2 * nt], ps[0:tw, F5, 0:2 * nt], EPS_LN, None,
                                  ALU.add).then_inc(varb_set, 1)

            def spread_c(t, geo):
                nt, tw = geo
                dve.wait_ge(rstdb_set, t + 1)
                spread_copy(rx_c[0:tw, 0:nt * P], rstd_b[0:tw, 0:2 * nt], nt, tw, rxc_set)

            def normed_b(t, geo):
                n = geo[0] * geo[1]
                dve.wait_ge(rxc_done, t + 1)
                dve.wait_ge(xcb_set, t + 1)
                dve.wait_ge(ylo_set, 2 * t)
                dve.tensor_tensor(y[:, 0:n], xc_b[:, 0:n], bank(F5, n), ALU.mult).then_inc(y_set, 1)

            def gates_part(t, geo, part):
                nt, tw = geo
                g, w = 2 * nt, 2 * nt * E

                def flat(x):
                    return x[0:tw, 0:w]

                def grp(x):
                    return x[0:tw, 0:w].rearrange("p (g e) -> p g e", e=E)

                def one(x):
                    return x[0:tw, 0:g]

                def wide(x):
                    return x[0:tw, 0:g].unsqueeze(2).to_broadcast([tw, g, E])

                def after(k):
                    dve.wait_ge(gate_step, GATE_STEPS * t + k)

                if part == 0:
                    dve.wait_ge(logit_done, t + 1)
                    dve.tensor_tensor(flat(g_logit), ps[0:tw, F7, 0:w], cst("rb2")[0:tw, 0:w],
                                      ALU.add).then_inc(gate_step, 1)
                    after(1)
                    dve.tensor_reduce(one(g_max), grp(g_logit), AX_X, ALU.max).then_inc(gate_step, 1)
                    after(2)
                    dve.tensor_tensor(grp(g_shift), grp(g_logit), wide(g_max), ALU.subtract).then_inc(gate_step, 1)
                if part == 1:
                    dve.wait_ge(gexp_set, t + 1)
                    dve.tensor_reduce(one(g_tot), grp(g_exp), AX_X, ALU.add).then_inc(gate_step, 1)
                    after(4)
                    dve.reciprocal(one(g_inv), one(g_tot)).then_inc(gate_step, 1)
                if part == 2:
                    after(5)
                    dve.tensor_tensor(grp(g_p), grp(g_exp), wide(g_inv), ALU.mult).then_inc(gate_step, 1)
                    after(6)
                    dve.tensor_reduce(one(g_top), grp(g_p), AX_X, ALU.max).then_inc(gate_step, 1)
                if part == 3:
                    after(7)
                    dve.tensor_tensor(grp(g_e1), grp(g_p), wide(g_top), ALU.is_equal).then_inc(gate_step, 1)
                    after(8)
                    dve.tensor_tensor(flat(g_w1), flat(g_e1), cst("order")[0:tw, 0:w], ALU.mult).then_inc(gate_step, 1)
                if part == 4:
                    after(9)
                    dve.tensor_reduce(one(g_i1), grp(g_w1), AX_X, ALU.max).then_inc(gate_step, 1)
                    after(10)
                    dve.tensor_tensor(grp(g_o1), grp(g_w1), wide(g_i1), ALU.is_equal).then_inc(gate_step, 1)
                if part == 5:
                    after(11)
                    dve.scalar_tensor_tensor(flat(g_rest), flat(g_o1), -4.0, flat(g_p), ALU.mult,
                                             ALU.add).then_inc(gate_step, 1)
                    after(12)
                    dve.tensor_reduce(one(g_top2), grp(g_rest), AX_X, ALU.max).then_inc(gate_step, 1)
                if part == 6:
                    after(13)
                    dve.tensor_tensor(grp(g_e2), grp(g_rest), wide(g_top2), ALU.is_equal).then_inc(gate_step, 1)
                    dve.tensor_tensor(one(g_dif), one(g_top2), one(g_top), ALU.subtract).then_inc(gate_step, 1)
                    after(14)
                    dve.tensor_tensor(flat(g_w2), flat(g_e2), cst("order")[0:tw, 0:w], ALU.mult).then_inc(gate_step, 1)
                if part == 7:
                    after(16)
                    dve.tensor_reduce(one(g_i2), grp(g_w2), AX_X, ALU.max).then_inc(gate_step, 1)
                    after(17)
                    dve.tensor_tensor(grp(g_o2), grp(g_w2), wide(g_i2), ALU.is_equal).then_inc(gate_step, 1)
                if part == 8:
                    dve.wait_ge(ged_set, t + 1)
                    dve.tensor_scalar(one(g_one), one(g_ed), 1.0, None, ALU.add).then_inc(gate_step, 1)
                    after(19)
                    dve.reciprocal(one(g_r1), one(g_one)).then_inc(gate_step, 1)
                if part == 9:
                    after(20)
                    dve.tensor_tensor(one(g_r2), one(g_r1), one(g_ed), ALU.mult)
                    dve.tensor_tensor(grp(g_a), grp(g_o1), wide(g_r1), ALU.mult).then_inc(gate_step, 1)
                    after(21)
                    dve.tensor_tensor(grp(g_b), grp(g_o2), wide(g_r2), ALU.mult).then_inc(gate_step, 1)
                if part == 10:
                    after(22)
                    dve.tensor_tensor(flat(g_sum), flat(g_a), flat(g_b), ALU.add)
                    by_tile = g_sum[0:tw, 0:w].rearrange("p (n e) -> p n e", n=nt)
                    dve.tensor_tensor(g_parts[0:tw, 0:nt, 0, :], g_a[0:tw, 0:w].rearrange("p (n e) -> p n e", n=nt),
                                      g_b[0:tw, 0:w].rearrange("p (n e) -> p n e", n=nt), ALU.add).then_inc(gate_step, 1)
                    after(23)
                    dve.tensor_tensor(g_parts[0:tw, 0:nt, 1, :], by_tile, g_parts[0:tw, 0:nt, 0, :].bitcast(F32),
                                      ALU.subtract).then_inc(gate_step, 1)

            def gate_hidden(t, geo, j):
                n = geo[0] * geo[1]
                dve.wait_ge(f2_set, E * t + j + 1)
                dve.wait_ge(fgb_done, E * t + j + 1)
                dve.wait_ge(fw3_done, E * t + j - 2)
                dve.tensor_tensor(gh[j % 3][:, 0:n], f2[j % 2][:, 0:n], bank(F6, n), ALU.mult).then_inc(gh_set, 1)

            def result(t, geo):
                n = geo[0] * geo[1]
                dve.wait_ge(fw3_done, E * (t + 1))
                dve.wait_ge(outt_done, t)
                dve.wait_ge(h3f_set, t + 1)
                dve.tensor_tensor(res[:, 0:n], h3_ffn[:, 0:n], bank(M0, n), ALU.add).then_inc(res_set, 1)

            def step(s, t, f, g, geo_t=FULL, geo_f=FULL, geo_g=FULL, hn=cur[1]):
                a, b, x, z = s is not None, t is not None, f is not None, g is not None
                if z: gate_hidden(g, geo_g, 5); result(g, geo_g)
                if a: hidden_lo(s, 0); hidden_lo(s, 1)
                if b and geo_t is FULL: denominators(t); inverses(t)
                if a: gate_pixels(s, 0); gate_pixels(s, 1)
                if b and geo_t is FULL: attended(t)
                if a: gate_pixels(s, 2); gate_pixels(s, 3)
                if x: gates_part(f, geo_f, 0)
                if a: gate_pixels(s, 4); gate_pixels(s, 5)
                if b: residual(t, geo_t, hn)
                if x: gates_part(f, geo_f, 1)
                if a: gate_pixels(s, 6)
                if x: gates_part(f, geo_f, 2)
                if a: gate_pixels(s, 7); gate_pixels(s, 8)
                if x: gates_part(f, geo_f, 3)
                if b: mean_sq_b(t, geo_t)
                if x: gates_part(f, geo_f, 4); gates_part(f, geo_f, 5); gates_part(f, geo_f, 6)
                if x: gates_part(f, geo_f, 7)
                if b: spread_b(t, geo_t)
                if x: gates_part(f, geo_f, 8); gates_part(f, geo_f, 9)
                if b: rms_normed(t, geo_t, f); block_out(t, geo_t)
                if x: gates_part(f, geo_f, 10)
                if a: deviations_a(s, FULL); spread_u(s, FULL)
                if x: gate_hidden(f, geo_f, 0)
                if b: variance_b(t, geo_t)
                if a: normed_u(s, FULL)
                if x: gate_hidden(f, geo_f, 1)
                if b: spread_c(t, geo_t); normed_b(t, geo_t)
                if a: elu_q_min(s, FULL)
                if x: gate_hidden(f, geo_f, 2)
                if a: spread_hn(s, FULL); elu_q(s, FULL, q_new)
                if x: gate_hidden(f, geo_f, 3)
                if a: normed_hn(s, FULL, hn_new); elu_k_min(s, FULL); elu_k(s, FULL)
                if x: gate_hidden(f, geo_f, 4)
                if a: sum_kv(s)

            dve.wait_ge(pack_loaded, 16)
            dve.tensor_copy(split_hi[:, :], packed[:, 0:SPLIT_W]).then_inc(setup_dve, 1)
            dve.wait_ge(setup_dve, 1)
            dve.tensor_tensor(split_lo[:, :], packed[:, 0:SPLIT_W], split_hi[:, :].bitcast(F32),
                              ALU.subtract).then_inc(setup_dve, 1)
            dve.tensor_scalar(wqkv_n[:, :], cst("wqkv"), cst("norm1"), None, ALU.mult).then_inc(setup_dve, 1)
            dve.memset(exponent[:, :], -0.5).then_inc(setup_dve, 1)
            dve.memset(v_tok[:, :, :], 1.0).then_inc(setup_dve, 1)
            dve.wait_ge(setup_act, 2)
            dve.sem_inc(setup_dve, 2)
            dve.sem_inc(gated_set, UNITS)
            for s_ in (den_set, den_set, zed_set, att_set, att_set, h2_set, msb_set, rxb_set, nrm_set, h3_set,
                       varb_set, rxc_set, y_set, res_set):
                dve.sem_inc(s_, 1)
            dve.sem_inc(h1lo_set, 2)
            dve.sem_inc(gate_step, GATE_STEPS)
            dve.sem_inc(gh_set, E)
            deviations_a(0, CLS)
            spread_u(0, CLS)
            normed_u(0, CLS)
            elu_q_min(0, CLS)
            elu_q(0, CLS, cls_q)
            spread_hn(0, CLS)
            normed_hn(0, CLS, cls_hn)
            elu_k_min(0, CLS)
            elu_k(0, CLS)
            sum_kv(0)
            dve.wait_ge(kvsum_set, 1)
            dve.tensor_copy(kv_sum[:, :], kv_cls[:, :]).then_inc(setup_dve, 1)
            dve.wait_ge(setup_dve, SETUP_DVE + 1)
            with dve.Fori(0, CHUNKS) as c:
                step(c + 1, None, None, None)
            image_end(0, CHUNKS + 1, None)
            step(CHUNKS + 1, 1, None, None)
            step(CHUNKS + 2, 2, 1, None)
            with dve.Fori(2, CHUNKS) as c:
                step(c + (CHUNKS + 1), c + 1, c + 0, c - 1)
            image_end(1, 2 * CHUNKS + 1, CHUNKS + 1)
            with dve.Fori(2, PAIRS) as i:
                with dve.Fori(0, CHUNKS) as c:
                    s = i * CHUNKS + c + 1
                    step(s, s - CHUNKS, s - (CHUNKS + 1), s - (CHUNKS + 2))
                image_end(i, i * CHUNKS + CHUNKS + 1, i * CHUNKS + 1)
            with dve.Fori(0, CHUNKS) as c:
                t = c + ((PAIRS - 1) * CHUNKS + 1)
                step(None, t, t - 1, t - 2)
            last = PAIRS * CHUNKS
            step(None, last + 1, last, last - 1, CLS, FULL, FULL, cls_hn)
            step(None, None, last + 1, last, CLS, CLS, FULL)
            step(None, None, None, last + 1, CLS, CLS, CLS)



def kernel(**inputs):
    import concourse.bacc as bacc
    from concourse.bass_utils import run_bass_kernel_spmd

    a = {k: np.asarray(v) for k, v in inputs.items()}
    f32 = np.float32
    xpad = np.ascontiguousarray(np.pad(a["x"], ((0, 0), (0, 0), (1, 1), (1, 1))).reshape(B * C, PW * PW))

    def pair_diag(w):
        z = np.zeros((2 * w.shape[0], 2 * w.shape[1]), f32)
        z[:w.shape[0], :w.shape[1]] = w
        z[w.shape[0]:, w.shape[1]:] = w
        return z

    pack = np.zeros((P, PACK_W), f32)

    def put(name, v, at=0):
        lo, _ = COLS[name]
        pack[0:v.shape[0], lo + at:lo + at + v.shape[1]] = v

    w1, w2, w3 = a["L0_tok_W1"].reshape(C, 9, C), a["L0_tok_W2"].reshape(C, C, 9), a["L0_tok_W3"].reshape(C, 9, C)
    b2 = a["L0_tok_b2"].reshape(C, 9)

    def k_of(offset):
        return 3 * offset[0] + offset[1]

    for m, (o1, o2) in enumerate(OFFSET_PAIRS):
        put("w1", np.concatenate([w1[:, k_of(o1)], w1[:, k_of(o2)]]), m * C)
        put("w3", np.concatenate([w3[:, k_of(o1)], w3[:, k_of(o2)]]), m * C)
        both = np.concatenate([w2[:, :, k_of(o1)], w2[:, :, k_of(o2)]], axis=1)
        put("w2", np.concatenate([both, both]), m * P)
        put("b2", np.concatenate([b2[:, k_of(o1)], b2[:, k_of(o2)]])[:, None], m)
    last = k_of(LAST_OFFSET)
    put("w1", pair_diag(w1[:, last]), 4 * C)
    put("w3", pair_diag(w3[:, last]), 4 * C)
    for img in range(2):
        put("w2", np.concatenate([w2[:, :, last]] * 2), (4 + img) * P + 64 * img)
    put("b2", np.concatenate([b2[:, last]] * 2)[:, None], 4)
    wq, wk, wv = np.split(a["L0_attn_w_qkv"], 3, axis=1)
    put("wqkv", pair_diag(wq))
    put("wqkv", pair_diag(wk), P)
    put("wqkv", pair_diag(wv), 2 * P)
    put("wo", pair_diag(a["L0_attn_w_out"]))
    e1, e2, e3 = (a[f"L0_ffn_expert_w{k}"] for k in (1, 2, 3))
    eb1, eb2, eb3 = (a[f"L0_ffn_expert_b{k}"] for k in (1, 2, 3))
    for ep in range(E // 2):
        first = np.concatenate([e1[2 * ep], e1[2 * ep + 1]], axis=1)
        put("ew1", np.concatenate([first, first]), ep * P)
        put("ew2", e2[2 * ep], ep * P)
        lo, _ = COLS["ew2"]
        pack[64:, lo + ep * P + 64:lo + (ep + 1) * P] = e2[2 * ep + 1]
        put("ew3", np.concatenate([e3[2 * ep], e3[2 * ep + 1]]), ep * C)
        put("eb1", np.concatenate([eb1[2 * ep], eb1[2 * ep + 1]])[:, None], ep)
        put("eb2", np.concatenate([eb2[2 * ep], eb2[2 * ep + 1]])[:, None], ep)
    sel_at, eb3_at = COLS["gate_sel"][0], COLS["eb3"][0]
    for part in range(2):
        for img in range(2):
            for e in range(E):
                row = part * 2 * E + img * E + e
                j = 2 * (e // 2) + img
                at = sel_at + j * P + 64 * (e % 2)
                pack[row, at:at + 64] = 1.0
                pack[row, eb3_at + 64 * img:eb3_at + 64 * img + 64] = eb3[e]
    for img in range(2):
        put("rw1", np.concatenate([a["L0_ffn_router_w1"]] * 2), img * P + RH * img)
    put("rw2", pair_diag(a["L0_ffn_router_w2"]))
    put("ident", np.eye(P, dtype=f32))
    put("center", pair_diag(np.eye(C, dtype=f32) - f32(1.0 / C)))
    put("mean", pair_diag(np.full((C, 1), 1.0 / C, f32)))
    head = np.arange(P) // HD
    put("head_mask", (head[:, None] == head[None, :]).astype(f32))
    put("head_mask", (head[:, None] == np.arange(2 * HEADS)[None, :]).astype(f32), P)
    put("order", np.tile(np.arange(E, 0, -1, dtype=f32), (P, 2 * NT)))
    put("rb2", np.tile(a["L0_ffn_router_b2"], (P, 2 * NT)))
    put("cls", np.tile(np.concatenate([a["cls_tok"].reshape(C)] * 2)[:, None], (1, NCLS)))

    def column(name, v):
        put(name, np.concatenate([v, v])[:, None])

    column("b1", a["L0_tok_b1"])
    column("b3", a["L0_tok_b3"])
    column("norm1", a["L0_attn_w_norm1"])
    column("norm2", a["L0_attn_w_norm2"])
    column("bo", a["L0_attn_b_out"])
    column("rb1", a["L0_ffn_router_b1"])

    nc = bacc.Bacc("TRN2", target_bir_lowering=False, num_devices=1)
    ap_x = nc.dram_tensor("xpad", xpad.shape, F32, kind="ExternalInput").ap()
    ap_p = nc.dram_tensor("pack", pack.shape, F32, kind="ExternalInput").ap()
    ap_o = nc.dram_tensor("out", (B, TOKENS, C), F32, kind="ExternalOutput").ap()
    build(nc, ap_x, ap_p, ap_o)
    r = run_bass_kernel_spmd(nc, [{"xpad": xpad, "pack": pack}], core_ids=[0])
    return r.results[0]["out"]
```

```python
from contextlib import ExitStack

import numpy as np

import concourse.bass as bass
from concourse import mybir

F32 = mybir.dt.float32
F32R = mybir.dt.float32r
ALU = mybir.AluOpType
ACT = mybir.ActivationFunctionType
AX_X = mybir.AxisListType.X

B, C, H, W = 16, 64, 56, 56
HEADS, HD = 8, 8
E, RH = 6, 32
TOKENS = H * W + 1
P = 128
PW = W + 2
ROWS = 8
CHUNKS = H // ROWS
N = ROWS * W
WIDE = P + 2 * HEADS
TILE, NT = 112, 4
PAIRS = B // 2
NCLS = PAIRS
UNITS = 9
XC_W, XR_W = 10 * PW, ROWS * PW
XC_AT, XR_AT, XP_AT = (0, XC_W), (2 * XC_W, 2 * XC_W + XR_W), 2 * XC_W + 2 * XR_W
X_W = 2 * XC_W + 3 * XR_W
X_LOADS = 3
EPS_LN, EPS_RMS, EPS_ATT = 1e-5, 1e-6, 1e-6

OFFSET_PAIRS = [((0, 0), (0, 1)), ((1, 0), (1, 1)), ((2, 0), (2, 1)), ((0, 2), (1, 2))]
LAST_OFFSET = (2, 2)


def columns():
    widths = [
        ("w1", 4 * C + P), ("ident", P), ("center", P), ("cls", NCLS),
        ("b1", 1), ("b2", 5), ("b3", 1), ("norm1", 1), ("bo", 1), ("norm2", 1), ("rb1", 1), ("eb1", 3), ("eb2", 3),
        ("wqkv", 3 * P),
        ("w2", 6 * P), ("w3", 4 * C + P),
        ("ew1", 3 * P), ("rw1", 2 * P), ("gate_sel", 6 * P), ("eb3", P),
        ("wo", P), ("ew2", 3 * P), ("ew3", 3 * C), ("rw2", 2 * E), ("head_mask", P + 2 * HEADS),
        ("order", NT * 2 * E), ("rb2", NT * 2 * E),
    ]
    out, at = {}, 0
    for name, width in widths:
        out[name] = (at, at + width)
        at += width
    return out, at


COLS, PACK_W = columns()
PARTS = [(0, COLS["w2"][0]), (COLS["w2"][0], COLS["ew1"][0]), (COLS["ew1"][0], PACK_W)]
W2_AT, W2_END = COLS["w2"]
EW1_AT, EB3_END = COLS["ew1"][0], COLS["eb3"][1]
SPLIT_W = 6 * P + EB3_END - EW1_AT


def build(nc, x, pack, out):
    ctx = ExitStack()
    with ctx:
        def sb(name, shape, dt=F32):
            return ctx.enter_context(nc.sbuf_tensor(name, shape, dt))

        def sem(name):
            return ctx.enter_context(nc.semaphore(name))

        packed = sb("packed", [P, PACK_W])
        split_hi = sb("split_hi", [P, SPLIT_W], F32R)
        split_lo = sb("split_lo", [P, SPLIT_W], F32R)
        w3_half = sb("w3_half", [P, 4 * C + P])
        wqkv_n = sb("wqkv_n", [P, 3 * P])
        b2_half = sb("b2_half", [P, 5])
        exponent = sb("exponent", [TILE, 2 * NT])

        def cst(name, a=0, b=None):
            lo, hi = COLS[name]
            return packed[:, lo + a:(hi if b is None else lo + b)]

        def split_at(name):
            lo, hi = COLS[name]
            base = W2_AT if name == "w2" else EW1_AT - 6 * P
            return lo - base, hi - base

        def hi_of(name, a=0, b=None):
            lo, hi = split_at(name)
            return split_hi[:, lo + a:(hi if b is None else lo + b)]

        def lo_of(name, a=0, b=None):
            lo, hi = split_at(name)
            return split_lo[:, lo + a:(hi if b is None else lo + b)]

        x_tile = sb("x_tile", [P, X_W])
        h1 = sb("h1", [P, N])
        h1s = [sb(f"h1s{m}", [P, N], F32R) for m in range(2)]
        th = [sb(f"th{k}", [P, N]) for k in range(3)]
        gated = [sb(f"gated{k}", [P, N]) for k in range(3)]
        new = sb("new", [P, 3, N])
        h_new, hn_new, q_new = (new[:, k, :] for k in range(3))
        sq_a = sb("sq_a", [P, N])
        xc_a = sb("xc_a", [P, N])
        u_a = sb("u_a", [P, N])
        sums_a = sb("sums_a", [TILE, 2 * NT])
        sums_b = sb("sums_b", [TILE, 2 * NT])
        var_u = sb("var_u", [TILE, 2 * NT])
        var_h = sb("var_h", [TILE, 2 * NT])
        rstd_u = sb("rstd_u", [TILE, 2 * NT])
        rstd_h = sb("rstd_h", [TILE, 2 * NT])
        rx_u = sb("rx_u", [TILE, NT * P])
        rx_h = sb("rx_h", [TILE, NT * P])
        eq = sb("eq", [P, N])
        eq1 = sb("eq1", [P, N])
        ek = sb("ek", [TILE, NT, P])
        ek1 = sb("ek1", [TILE, NT, P])
        k_tok = sb("k_tok", [TILE, NT, P])
        v_tok = sb("v_tok", [TILE, NT, P + 2])
        kv_sum = sb("kv_sum", [P, P + 2])
        kv_cls = sb("kv_cls", [P, P + 2])
        ring = sb("ring", [P, CHUNKS * 3 * N])
        current = sb("current", [P, 3, N])
        cur = [current[:, k, :] for k in range(3)]
        cls_h = cst("cls")
        cls_hn = sb("cls_hn", [P, NCLS])
        cls_q = sb("cls_q", [P, NCLS])
        kv_m = sb("kv_m", [P, P + 2 * HEADS])
        k_m = sb("k_m", [P, P])
        cls_den = sb("cls_den", [P, 2])
        cls_att = sb("cls_att", [P, NCLS])
        den = sb("den", [TILE, NT * 2 * HEADS])
        zed = sb("zed", [TILE, NT * 2 * HEADS])
        att = sb("att", [TILE, NT * P])
        att_c = sb("att_c", [P, N])
        h2 = sb("h2", [P, N])
        sq_b = sb("sq_b", [P, N])
        ms_b = sb("ms_b", [TILE, 2 * NT])
        rms_b = sb("rms_b", [TILE, 2 * NT])
        rx_b = sb("rx_b", [TILE, NT * P])
        sum_b = sb("sum_b", [P, N])
        nrm_b = sb("nrm_b", [P, N])
        h3 = sb("h3", [P, N])
        h3_ffn = sb("h3_ffn", [P, N])
        sq_c = sb("sq_c", [P, N])
        xc_b = sb("xc_b", [P, N])
        var_b = sb("var_b", [TILE, 2 * NT])
        rstd_b = sb("rstd_b", [TILE, 2 * NT])
        rx_c = sb("rx_c", [TILE, NT * P])
        y = sb("y", [P, N])
        ys = [sb(f"ys{m}", [P, N], F32R) for m in range(2)]
        rh = sb("rh", [2 * RH, N])
        G = NT * 2
        gates_shape = [TILE, G * E]
        g_logit, g_shift, g_exp, g_p, g_e1, g_o1, g_rest, g_e2, g_o2, g_a, g_b, g_sum = (
            sb(f"g_{n}", gates_shape)
            for n in ("logit", "shift", "exp", "p", "e1", "o1", "rest", "e2", "o2", "a", "b", "sum"))
        g_w1, g_w2 = sb("g_w1", gates_shape), sb("g_w2", gates_shape)
        g_max, g_tot, g_inv, g_top, g_i1, g_top2, g_i2, g_dif, g_ed, g_one, g_r1, g_r2 = (
            sb(f"gs_{n}", [TILE, G])
            for n in ("max", "tot", "inv", "top", "i1", "top2", "i2", "dif", "ed", "one", "r1", "r2"))
        g_parts = sb("g_parts", [TILE, NT, 2, 2 * E], F32R)
        gates_c = sb("gates_c", [4 * E, N], F32R)
        f1 = [sb(f"f1_{k}", [P, N]) for k in range(2)]
        f2 = [sb(f"f2_{k}", [P, N]) for k in range(2)]
        gh = [sb(f"gh_{k}", [P, N]) for k in range(3)]
        res = sb("res", [P, N])
        out_t = sb("out_t", [TILE, NT * P])

        ps = ctx.enter_context(nc.psum_tensor("ps", [P, 8, 512], F32))
        S0, S1, L0, L1, M0, F5, F6, F7 = range(8)
        KV = (F7, F5)

        pack_loaded = [sem(f"pack_loaded{k}") for k in range(3)]
        x_loaded, cur_loaded = sem("x_loaded"), sem("cur_loaded")
        ring_stored, out_stored = sem("ring_stored"), sem("out_stored")
        setup_dve, setup_act = sem("setup_dve"), sem("setup_act")
        (w1_done, s_done, w3_done, ctr_done, vara_done, rxu_done, rxh_done, q_done, kv_done, kvp_done,
         clsatt_done) = (
            sem(n) for n in ("w1_done", "s_done", "w3_done", "ctr_done", "vara_done", "rxu_done", "rxh_done",
                             "q_done", "kv_done", "kvp_done", "clsatt_done"))
        (attn_done, attc_done, wo_done, ms_done, rxb_done, ctrb_done, varb_done, rxc_done, router_done,
         logit_done, gt_done, fh1_done, fgb_done, fh2_done, fw3_done, outt_done) = (
            sem(n) for n in ("attn_done", "attc_done", "wo_done", "ms_done", "rxb_done", "ctrb_done",
                             "varb_done", "rxc_done", "router_done", "logit_done", "gt_done", "fh1_done",
                             "fgb_done", "fh2_done", "fw3_done", "outt_done"))
        (h1hi_set, th_set, h_set, sqa_set, eq_set, ek_set, v_set, attc_set, sqb_set, sqc_set, yhi_set, rh_set,
         gexp_set, ged_set, gatesc_set, f1_set, f2_set, outt_set) = (
            sem(n) for n in ("h1hi_set", "th_set", "h_set", "sqa_set", "eq_set", "ek_set", "v_set", "attc_set",
                             "sqb_set", "sqc_set", "yhi_set", "rh_set", "gexp_set", "ged_set", "gatesc_set",
                             "f1_set", "f2_set", "outt_set"))
        (h1_set, h1lo_set, gated_set, xca_set, var_set, rxu_set, rxh_set, hn_set, u_set, eq1_set, qf_set,
         ek1_set, kf_set,
         kvsum_set, kvm_set, kvnew_set, suma_set, clsden_set, clsatt_set) = (
            sem(n) for n in ("h1_set", "h1lo_set", "gated_set", "xca_set", "var_set", "rxu_set", "rxh_set",
                             "hn_set", "u_set", "eq1_set", "qf_set", "ek1_set", "kf_set", "kvsum_set",
                             "kvm_set", "kvnew_set", "suma_set", "clsden_set",
                             "clsatt_set"))
        summs_set, sumvar_set = sem("summs_set"), sem("sumvar_set")
        (den_set, zed_set, att_set, h2_set, msb_set, rxb_set, nrm_set, h3_set, xcb_set, varb_set, rxc_set, y_set,
         ylo_set, gate_step, gh_set, res_set) = (
            sem(n) for n in ("den_set", "zed_set", "att_set", "h2_set", "msb_set", "rxb_set", "nrm_set", "h3_set",
                             "xcb_set", "varb_set", "rxc_set", "y_set", "ylo_set", "gate_step", "gh_set",
                             "res_set"))
        rstdu_set, rstdh_set, rmsb_set, rstdb_set, sumb_set, h3f_set = (
            sem(n) for n in ("rstdu_set", "rstdh_set", "rmsb_set", "rstdb_set", "sumb_set", "h3f_set"))
        GATE_STEPS = 24
        SETUP_DVE = 9

        def x_view(unit):
            m, img = unit // 2, unit % 2
            if unit == UNITS - 1:
                at = XP_AT
            elif m < 3:
                at = XC_AT[img] + m * PW
            else:
                at = XR_AT[img]
            return x_tile[:, at:at + ROWS * PW].rearrange("p (r c) -> p r c", c=PW)[:, :, 0:W]

        def as_rows(ap):
            return ap.rearrange("p (r c) -> p r c", c=W)

        def bank(b, n=N, p0=0, p1=P):
            return ps[p0:p1, b, 0:n]

        def half(img):
            return slice(64 * img, 64 * img + 64)

        def is_step_0(s):
            return isinstance(s, int) and s == 0

        FULL, CLS = (NT, TILE), (1, NCLS)
        block = ctx.enter_context(nc.Block())

        @block.sync
        def _(sp):
            def prime(s, n):
                sp.sem_inc(s, n)

            prime(ring_stored, 16)
            prime(out_stored, 16)

            def reg(v):
                return v if isinstance(v, int) else sp.snap(v)

            def settle():
                sp.wait_ge(pack_loaded[0], 16)

            def load_x(i, c, s):
                row, at = reg(i * P), reg(c * X_W)
                steps = [reg(UNITS * s - UNITS + u) for u in (6, 8, UNITS)]
                rows = x[bass.ds(row, P)]
                cuts = (0, 2 * XC_W, XP_AT, X_W)
                for k, gated_before in enumerate(steps):
                    sp.wait_ge(gated_set, gated_before)
                    settle()
                    sp.dma_start(x_tile[:, cuts[k]:cuts[k + 1]],
                                 rows[:, bass.ds(at + cuts[k], cuts[k + 1] - cuts[k])]).then_inc(x_loaded, 16)

            def load_cur(c, t, cls=0):
                at, before, stored = reg(c * (3 * N)), reg(t + 0), reg(16 * (t - cls) + 16)
                sp.wait_ge(h3_set, before)
                sp.wait_ge(attn_done, before)
                sp.wait_ge(ring_stored, stored)
                settle()
                sp.dma_start(current[:, :, :].rearrange("p k n -> p (k n)"),
                             ring[:, bass.ds(at, 3 * N)]).then_inc(cur_loaded, 16)

            def store_ring(c, s, t):
                at, now = reg(c * (3 * N)), reg(s + 1)
                loaded = None if t is None else reg(16 * t)
                if t is not None:
                    sp.wait_ge(cur_loaded, loaded)
                sp.wait_ge(h_set, now)
                sp.wait_ge(hn_set, now)
                sp.wait_ge(qf_set, now)
                settle()
                sp.dma_start(ring[:, bass.ds(at, 3 * N)],
                             new[:, :, :].rearrange("p k n -> p (k n)")).then_inc(ring_stored, 16)

            def store_out(i, c, t):
                image, at, now = reg(i * 2), reg(c * N + 1), reg(t + 1)
                sp.wait_ge(outt_set, now)
                settle()
                dst = out[bass.ds(image, 2), bass.ds(at, N), :]
                sp.dma_start(dst.rearrange("m (p k) c -> p m (k c)", k=NT),
                             out_t[:, :].rearrange("p (m x) -> p m x", m=2)).then_inc(out_stored, 16)

            def image(i, first=False):
                s = i * CHUNKS + 1
                t = s - CHUNKS
                load_x(i, 0, s)
                load_cur(0, t)
                store_ring(CHUNKS - 1, s - 1, None if first else t - 1)
                if not first:
                    store_out(i - 2, CHUNKS - 2, t - 2)
                load_x(i, 1, s + 1)
                load_cur(1, t + 1)
                store_ring(0, s, t)
                if not first:
                    store_out(i - 2, CHUNKS - 1, t - 1)
                with sp.Fori(2, CHUNKS) as c:
                    load_x(i, c, s + c)
                    load_cur(c, t + c)
                    store_ring(c - 1, s + c - 1, t + c - 1)
                    store_out(i - 1, c - 2, t + c - 2)

            def load_pack(k):
                lo, hi = PARTS[k]
                sp.dma_start(packed[:, lo:hi], pack[:, lo:hi]).then_inc(pack_loaded[k], 16)

            load_pack(0)
            load_x(0, 0, 1)
            load_pack(1)
            load_pack(2)
            load_x(0, 1, 2)
            with sp.Fori(2, CHUNKS) as c:
                store_ring(c - 2, c - 1, None)
                load_x(0, c, c + 1)
            store_ring(CHUNKS - 2, CHUNKS - 1, None)
            image(1, first=True)
            with sp.Fori(2, PAIRS) as i:
                image(i)
            cls = (PAIRS - 1) * CHUNKS + 1
            store_ring(CHUNKS - 1, PAIRS * CHUNKS, cls - 1)
            store_out(PAIRS - 2, CHUNKS - 2, cls - 2)
            sp.sem_inc(cur_loaded, 16)
            load_cur(0, cls + 1, 1)
            store_out(PAIRS - 2, CHUNKS - 1, cls - 1)
            load_cur(1, cls + 2, 1)
            sp.wait_ge(outt_set, cls + 1)
            cls_rows = out.rearrange("(i m) t c -> i m t c", m=2)[:, :, 0, :]
            sp.dma_start(cls_rows, out_t[0:NCLS, 0:P].rearrange("p (m c) -> p m c", m=2)).then_inc(out_stored, 16)
            with sp.Fori(2, CHUNKS) as c:
                load_cur(c, c + (cls + 1), 1)
                store_out(PAIRS - 1, c - 2, c + (cls - 1))
            store_out(PAIRS - 1, CHUNKS - 2, cls + CHUNKS - 1)
            store_out(PAIRS - 1, CHUNKS - 1, cls + CHUNKS)
            last = PAIRS * CHUNKS
            sp.wait_ge(out_stored, 16 + 16 * last + 16)

        @block.tensor
        def _(pe):
            ident = cst("ident")

            def w1(s, part):
                if part == 0:
                    pe.wait_ge(x_loaded, 16 * X_LOADS * s)
                    pe.wait_ge(h_set, s)
                for u in range(4 * part, 4 * part + 4):
                    m, img = u // 2, u % 2
                    pe.matmul(as_rows(bank(L0, p0=64 * img, p1=64 * img + 64)), cst("w1", m * C, (m + 1) * C),
                              x_view(u), start=(m == 0), stop=False)
                if part == 1:
                    pe.matmul(as_rows(bank(L0)), cst("w1", 4 * C), x_view(UNITS - 1), start=False,
                              stop=True).then_inc(w1_done, 1)

            def w2(s, u, f=None, cls=None):
                if u < 2:
                    pe.wait_ge(h1lo_set, 2 * s + 1 + u)
                    if f is not None:
                        pe.wait_ge(f2_set if u else f1_set, E * f)
                    if cls is not None:
                        pe.wait_ge(clsatt_set, cls)
                else:
                    pe.wait_ge(th_set, UNITS * s + u - 1)
                b = S0 + u % 2
                if u == UNITS - 1:
                    todo = [(m, img, w) for m, img in ((4, 0), (5, 1)) for w in (hi_of, lo_of)]
                else:
                    todo = [(u // 2, u % 2, w) for w in (hi_of, lo_of)]
                for n, (m, img, w) in enumerate(todo):
                    mm = pe.matmul(bank(b), w("w2", m * P, (m + 1) * P), h1s[img][:, :],
                                   start=(n == 0), stop=(n == len(todo) - 1))
                mm.then_inc(s_done, 1)

            def w3(s, m):
                if m == 4:
                    pe.wait_ge(gated_set, UNITS * (s + 1))
                    pe.matmul(bank(L0), w3_half[:, 4 * C:], gated[(UNITS - 1) % 3][:, :], start=False,
                              stop=True).then_inc(w3_done, 1)
                    return
                for img in range(2):
                    u = 2 * m + img
                    pe.wait_ge(gated_set, UNITS * s + u + 1)
                    pe.matmul(bank(L0, p0=64 * img, p1=64 * img + 64), w3_half[:, m * C:(m + 1) * C],
                              gated[u % 3][:, :], start=(m == 0), stop=False).then_inc(w3_done, 1)

            def to_tokens(b, src, geo, done):
                nt, tw = geo
                for k in range(nt):
                    mm = pe.transpose(ps[0:tw, b, k * P:(k + 1) * P], src[:, k * tw:(k + 1) * tw], ident)
                mm.then_inc(done, 1)

            def to_channels(b, src, geo):
                nt, tw = geo
                for k in range(nt):
                    mm = pe.transpose(bank(b)[:, k * tw:(k + 1) * tw], src[0:tw, k * P:(k + 1) * P],
                                      ident[0:tw, 0:tw])
                return mm

            def center_a(s, geo, h):
                n = geo[0] * geo[1]
                if not is_step_0(s):
                    pe.wait_ge(h_set, s + 1)
                    pe.wait_ge(kvsum_set, s)
                pe.matmul(bank(L1, n), cst("center"), h[:, 0:n], start=True, stop=True).then_inc(ctr_done, 1)

            def var_mean_a(s, geo):
                pe.wait_ge(sqa_set, s + 1)
                pe.wait_ge(xca_set, s + 1)
                to_tokens(L1, sq_a, geo, vara_done)

            def spread_u(s, geo):
                pe.wait_ge(rxu_set, s + 1)
                pe.wait_ge(var_set, 2 * s + 2)
                to_channels(L1, rx_u, geo).then_inc(rxu_done, 1)

            def spread_hn(s, geo):
                pe.wait_ge(rxh_set, s + 1)
                pe.wait_ge(qf_set, s + 1)
                to_channels(L1, rx_h, geo).then_inc(rxh_done, 1)

            def q_prod(s, geo):
                n = geo[0] * geo[1]
                pe.wait_ge(u_set, s + 1)
                pe.matmul(bank(L1, n), wqkv_n[:, 0:P], u_a[:, 0:n], start=True, stop=True).then_inc(q_done, 1)

            def kv_prod(s, geo, t=None, f=None):
                nt, tw = geo
                pe.wait_ge(u_set, s + 1)
                if not is_step_0(s):
                    pe.wait_ge(kf_set, 2 * s)
                if t is not None:
                    pe.wait_ge(y_set, t + 1)
                if f is not None:
                    pe.wait_ge(gatesc_set, f + 1)
                for k in range(nt):
                    at = 2 * P * (k % 2)
                    mm = pe.matmul(ps[0:tw, KV[k // 2], at:at + 2 * P], u_a[:, k * tw:(k + 1) * tw],
                                   wqkv_n[:, P:3 * P], start=True, stop=True)
                mm.then_inc(kv_done, 1)

            def kv_outer(s, geo):
                nt, tw = geo if geo is FULL else (1, 1)
                pe.wait_ge(kf_set, 2 * s + 2)
                pe.wait_ge(v_set, s + 1)
                pe.wait_ge(hn_set, s + 1)
                for k in range(nt):
                    mm = pe.matmul(bank(L1, P + 2), k_tok[0:tw, k, :], v_tok[0:tw, k, :],
                                   start=(k == 0), stop=(k == nt - 1))
                mm.then_inc(kvp_done, 1)

            def cls_attention(i):
                pe.matmul(ps[:, S0, 0:1], kv_m[:, 0:P], cls_q[:, 0:1], start=True, stop=True)
                pe.matmul(ps[:, S0, 1:2], k_m[:, :], cls_q[:, 0:1], start=True, stop=True).then_inc(clsatt_done, 1)

            def attention(t, s, g, pairs, b=M0):
                pe.wait_ge(cur_loaded, 16 * t)
                pe.wait_ge(kvm_set, pairs)
                if g is not None:
                    pe.wait_ge(res_set, g + 1)
                if s is not None:
                    pe.wait_ge(kf_set, 2 * s)
                pe.wait_ge(y_set, t)
                for k in range(NT):
                    at = (P + 2 * HEADS) * (k % 2)
                    mm = pe.matmul(ps[0:TILE, b + k // 2, at:at + P + 2 * HEADS],
                                   cur[2][:, k * TILE:(k + 1) * TILE], kv_m[:, :], start=True, stop=True)
                mm.then_inc(attn_done, 1)

            def att_channels(t, g):
                pe.wait_ge(att_set, 2 * t + 2)
                if g is not None:
                    pe.wait_ge(outt_set, g + 1)
                to_channels(F6, att, FULL).then_inc(attc_done, 1)

            def out_proj(t, geo, b=M0):
                n = geo[0] * geo[1]
                pe.wait_ge(attc_set, t + 1)
                pe.matmul(bank(b, n), cst("wo"), att_c[:, 0:n], start=True, stop=True).then_inc(wo_done, 1)

            def mean_sq_b(t, geo):
                pe.wait_ge(sqb_set, t + 1)
                to_tokens(F5, sq_b, geo, ms_done)

            def spread_b(t, geo):
                pe.wait_ge(rxb_set, t + 1)
                to_channels(F5, rx_b, geo).then_inc(rxb_done, 1)

            def center_b(t, geo, b=M0):
                n = geo[0] * geo[1]
                pe.wait_ge(h3_set, t + 1)
                pe.matmul(bank(b, n), cst("center"), h3[:, 0:n], start=True, stop=True).then_inc(ctrb_done, 1)

            def var_mean_b(t, geo):
                pe.wait_ge(sqc_set, t + 1)
                to_tokens(F5, sq_c, geo, varb_done)

            def spread_c(t, geo):
                pe.wait_ge(rxc_set, t + 1)
                to_channels(F5, rx_c, geo).then_inc(rxc_done, 1)

            def router(t, geo, s):
                n = geo[0] * geo[1]
                if s is not None:
                    pe.wait_ge(kf_set, 2 * s)
                pe.wait_ge(gatesc_set, t)
                pe.wait_ge(yhi_set, 2 * t + 2)
                pe.wait_ge(ylo_set, 2 * t + 2)
                k = 0
                for img in range(2):
                    for w in (hi_of, lo_of):
                        mm = pe.matmul(bank(F7, n), w("rw1", img * P, (img + 1) * P), ys[img][:, 0:n],
                                       start=(k == 0), stop=(k == 3))
                        k += 1
                mm.then_inc(router_done, 1)

            def logits(t, geo):
                nt, tw = geo
                pe.wait_ge(rh_set, t + 1)
                for k in range(nt):
                    mm = pe.matmul(ps[0:tw, F7, 2 * E * k:2 * E * (k + 1)], rh[:, k * tw:(k + 1) * tw],
                                   cst("rw2")[0:2 * RH, :], start=True, stop=True)
                mm.then_inc(logit_done, 1)

            def gates_channels(t, geo):
                nt, tw = geo
                pe.wait_ge(gate_step, GATE_STEPS * (t + 1))
                for k in range(nt):
                    mm = pe.transpose(ps[0:4 * E, F7, k * tw:(k + 1) * tw],
                                      g_parts[0:tw, k].rearrange("p a e -> p (a e)").bitcast(F32),
                                      ident[0:tw, 0:tw])
                mm.then_inc(gt_done, 1)

            def expert_h1(t, geo, j, s=None):
                n = geo[0] * geo[1]
                ep, img = j // 2, j % 2
                pe.wait_ge(f1_set, E * t + j)
                if j == 0:
                    pe.wait_ge(ylo_set, 2 * t + 2)
                if j == 0 and s is not None:
                    pe.wait_ge(th_set, UNITS * (s + 1))
                for w in (hi_of, lo_of):
                    mm = pe.matmul(bank(S0, n), w("ew1", ep * P, (ep + 1) * P), ys[img][:, 0:n],
                                   start=(w is hi_of), stop=(w is lo_of))
                mm.then_inc(fh1_done, 1)

            def expert_gate(t, geo, j, tb=None):
                n = geo[0] * geo[1]
                if j == 0:
                    pe.wait_ge(gatesc_set, t + 1)
                    pe.wait_ge(outt_set, t)
                    if tb is not None:
                        pe.wait_ge(attc_set, tb + 1)
                else:
                    pe.wait_ge(gh_set, E * t + j)
                pe.matmul(bank(F6, n), hi_of("gate_sel", j * P, (j + 1) * P)[0:4 * E], gates_c[:, 0:n],
                          start=True, stop=True).then_inc(fgb_done, 1)

            def expert_h2(t, geo, j):
                n = geo[0] * geo[1]
                ep = j // 2
                pe.wait_ge(f1_set, E * t + j + 1)
                pe.wait_ge(f2_set, E * t + j)
                pe.matmul(bank(S1, n), cst("ew2", ep * P, (ep + 1) * P), f1[j % 2][:, 0:n],
                          start=True, stop=True).then_inc(fh2_done, 1)

            def expert_bias(t, geo, tb):
                n = geo[0] * geo[1]
                pe.wait_ge(gatesc_set, t + 1)
                pe.wait_ge(res_set, t)
                if tb is not None:
                    pe.wait_ge(sqc_set, tb + 1)
                    pe.wait_ge(xcb_set, tb + 1)
                pe.matmul(bank(M0, n), hi_of("eb3")[0:4 * E], gates_c[:, 0:n], start=True, stop=False)
                pe.matmul(bank(M0, n), lo_of("eb3")[0:4 * E], gates_c[:, 0:n], start=False, stop=False)

            def expert_out(t, geo, ep):
                n = geo[0] * geo[1]
                for img in range(2):
                    j = 2 * ep + img
                    pe.wait_ge(gh_set, E * t + j + 1)
                    pe.matmul(bank(M0, n, 64 * img, 64 * img + 64), cst("ew3", ep * C, (ep + 1) * C),
                              gh[j % 3][:, 0:n], start=False, stop=(j >= E - 2)).then_inc(fw3_done, 1)

            def out_tokens(t, geo):
                nt, tw = geo
                pe.wait_ge(res_set, t + 1)
                tiles = res[:, 0:nt * tw].rearrange("p (t k) -> p t k", k=nt)
                for k in range(nt):
                    mm = pe.transpose(ps[0:tw, F6, k * P:(k + 1) * P], tiles[:, :, k], ident)
                mm.then_inc(outt_done, 1)

            def step(s, t, f, g, pairs, cls=None, geo_t=FULL, geo_f=FULL, geo_g=FULL):
                a, b, x, z = s is not None, t is not None, f is not None, g is not None
                if a: w1(s, 0); w1(s, 1)
                if z: expert_out(g, geo_g, 2)
                if x: router(f, geo_f, s)
                if b and geo_t is FULL: attention(t, s, g, pairs)
                if a: w2(s, 0, f, cls)
                if z: out_tokens(g, geo_g)
                if a: w2(s, 1, f); w2(s, 2)
                if x: logits(f, geo_f)
                if b and geo_t is FULL: att_channels(t, g)
                if a: w2(s, 3); w2(s, 4); w3(s, 0)
                if b: out_proj(t, geo_t)
                if a: w2(s, 5); w2(s, 6); w3(s, 1); w2(s, 7); w2(s, 8); w3(s, 2)
                if b: mean_sq_b(t, geo_t)
                if x: expert_h1(f, geo_f, 0, s)
                if a: w3(s, 3); w3(s, 4)
                if x: expert_h1(f, geo_f, 1); expert_h2(f, geo_f, 0)
                if a: center_a(s, FULL, h_new)
                if x: expert_h1(f, geo_f, 2)
                if b: spread_b(t, geo_t)
                if x: expert_h2(f, geo_f, 1); gates_channels(f, geo_f)
                if a: var_mean_a(s, FULL)
                if x: expert_h1(f, geo_f, 3)
                if b: center_b(t, geo_t)
                if x: expert_gate(f, geo_f, 0, t); expert_h2(f, geo_f, 2)
                if b: var_mean_b(t, geo_t)
                if x: expert_gate(f, geo_f, 1); expert_h1(f, geo_f, 4); expert_h2(f, geo_f, 3)
                if x: expert_bias(f, geo_f, t)
                if a: spread_u(s, FULL)
                if x: expert_out(f, geo_f, 0); expert_gate(f, geo_f, 2)
                if a: q_prod(s, FULL)
                if b: spread_c(t, geo_t)
                if x: expert_gate(f, geo_f, 3); expert_h2(f, geo_f, 4)
                if a: kv_prod(s, FULL, t, f)
                if x: expert_gate(f, geo_f, 4)
                if a: spread_hn(s, FULL)
                if x: expert_h1(f, geo_f, 5); expert_out(f, geo_f, 1); expert_gate(f, geo_f, 5)
                if x: expert_h2(f, geo_f, 5)
                if a: kv_outer(s, FULL)

            def step_a(s, r, geo=FULL, h=h_new):
                if r is not None: center_a(r, geo, h)
                if s is not None: w1(s, 0)
                if r is not None: var_mean_a(r, geo)
                if s is not None: w1(s, 1)
                if r is not None: spread_u(r, geo); q_prod(r, geo)
                if s is not None: w2(s, 0); w2(s, 1)
                if r is not None: kv_prod(r, geo)
                if s is not None: w2(s, 2); w2(s, 3); w3(s, 0); w2(s, 4); w2(s, 5)
                if r is not None: spread_hn(r, geo)
                if s is not None: w2(s, 6); w3(s, 1); w2(s, 7); w2(s, 8); w3(s, 2); w3(s, 3); w3(s, 4)
                if r is not None: kv_outer(r, geo)

            def step_b(t, f, g, geo_t=FULL, geo_f=FULL, geo_g=FULL):
                b, x, z = t is not None, f is not None, g is not None
                if b and geo_t is FULL: attention(t, None, None, PAIRS, L0)
                if z: expert_out(g, geo_g, 2)
                if x: router(f, geo_f, None)
                if z: out_tokens(g, geo_g)
                if x: expert_h1(f, geo_f, 0); logits(f, geo_f)
                if b and geo_t is FULL: att_channels(t, g)
                if x: expert_h1(f, geo_f, 1)
                if b: out_proj(t, geo_t, L0)
                if x: expert_h2(f, geo_f, 0); expert_h1(f, geo_f, 2)
                if b: mean_sq_b(t, geo_t)
                if x: expert_h2(f, geo_f, 1); expert_h1(f, geo_f, 3); expert_h2(f, geo_f, 2)
                if x: expert_h1(f, geo_f, 4)
                if b: spread_b(t, geo_t)
                if x: gates_channels(f, geo_f); expert_h1(f, geo_f, 5); expert_gate(f, geo_f, 0, t)
                if b: center_b(t, geo_t, L0)
                if x: expert_bias(f, geo_f, f); expert_gate(f, geo_f, 1)
                if b: var_mean_b(t, geo_t)
                if x: expert_h2(f, geo_f, 3); expert_gate(f, geo_f, 2); expert_out(f, geo_f, 0)
                if x: expert_gate(f, geo_f, 3); expert_h2(f, geo_f, 4)
                if b: spread_c(t, geo_t)
                if x: expert_out(f, geo_f, 1); expert_gate(f, geo_f, 4); expert_h2(f, geo_f, 5)
                if x: expert_gate(f, geo_f, 5)

            pe.wait_ge(pack_loaded[0], 16)
            for done in (w1_done, attn_done, attc_done, wo_done, ms_done, rxb_done, ctrb_done, varb_done, rxc_done,
                         router_done, logit_done, gt_done, outt_done):
                pe.sem_inc(done, 1)
            for done in (s_done, w3_done):
                pe.sem_inc(done, UNITS)
            for done in (fh1_done, fgb_done, fh2_done, fw3_done):
                pe.sem_inc(done, E)
            step_a(1, 0, CLS, cls_h)
            with pe.Fori(1, CHUNKS) as c:
                step_a(c + 1, c + 0)
            step_a(None, CHUNKS)
            pe.wait_ge(setup_dve, SETUP_DVE)
            step(CHUNKS + 1, 1, None, None, 1)
            step(CHUNKS + 2, 2, 1, None, 1)
            with pe.Fori(2, CHUNKS) as c:
                step(c + (CHUNKS + 1), c + 1, c + 0, c - 1, 1)
            cls_attention(0)
            with pe.Fori(2, PAIRS) as i:
                with pe.Fori(0, CHUNKS) as c:
                    s = i * CHUNKS + c + 1
                    step(s, s - CHUNKS, s - (CHUNKS + 1), s - (CHUNKS + 2), i, i - 1)
                cls_attention(i - 1)
            pe.wait_ge(kvm_set, PAIRS)
            pe.wait_ge(clsatt_set, PAIRS - 1)
            cls_attention(PAIRS - 1)
            pe.wait_ge(clsatt_set, PAIRS)
            cls = (PAIRS - 1) * CHUNKS + 1
            step_b(cls, cls - 1, cls - 2, CLS)
            for done in (attn_done, attc_done):
                pe.sem_inc(done, 1)
            step_b(cls + 1, cls, cls - 1, FULL, CLS)
            step_b(cls + 2, cls + 1, cls, FULL, FULL, CLS)
            with pe.Fori(2, CHUNKS) as c:
                t = c + (cls + 1)
                step_b(t, t - 1, t - 2)
            step_b(None, cls + CHUNKS, cls + CHUNKS - 1)
            step_b(None, None, cls + CHUNKS)

        @block.scalar
        def _(act):
            def hidden(s):
                act.wait_ge(w1_done, s + 1)
                act.wait_ge(h1lo_set, 2 * s)
                act.activation(h1[:, :], bank(L0), ACT.Relu, bias=cst("b1")).then_inc(h1_set, 1)

            def hidden_hi(s, img):
                act.wait_ge(w1_done, s + 1)
                act.wait_ge(s_done, UNITS * s)
                act.activation(h1s[img][half(img), :], bank(L0, p0=64 * img, p1=64 * img + 64), ACT.Relu,
                               bias=cst("b1")[half(img)]).then_inc(h1hi_set, 1)

            def gate_tanh(s, u):
                m = u // 2
                act.wait_ge(s_done, UNITS * s + u + 1)
                act.wait_ge(gated_set, UNITS * s + u - 2)
                act.activation(th[u % 3][:, :], bank(S0 + u % 2), ACT.Tanh, bias=b2_half[:, m:m + 1],
                               scale=0.5).then_inc(th_set, 1)

            def unfold_out(s):
                act.wait_ge(w3_done, UNITS * (s + 1))
                act.wait_ge(ring_stored, 16 * s)
                act.activation(h_new[:, :], bank(L0), ACT.Identity, bias=cst("b3")).then_inc(h_set, 1)

            def square_a(s, geo):
                n = geo[0] * geo[1]
                act.wait_ge(ctr_done, s + 1)
                act.activation(sq_a[:, 0:n], bank(L1, n), ACT.Square).then_inc(sqa_set, 1)

            def center_a(s, geo):
                n = geo[0] * geo[1]
                act.wait_ge(ctr_done, s + 1)
                act.activation(xc_a[:, 0:n], bank(L1, n), ACT.Copy).then_inc(xca_set, 1)

            def exp_q(s, geo):
                n = geo[0] * geo[1]
                act.wait_ge(q_done, s + 1)
                act.activation(eq[:, 0:n], bank(L1, n), ACT.Exp).then_inc(eq_set, 1)

            def exp_k(s, geo):
                nt, tw = geo
                act.wait_ge(kv_done, s + 1)
                for b in range((nt + 1) // 2):
                    k = min(2, nt - 2 * b)
                    src = ps[0:tw, KV[b], 0:2 * P * k].rearrange("p (k c) -> p k c", k=k)
                    act.activation(ek[0:tw, 2 * b:2 * b + k, :], src[:, :, 0:P], ACT.Exp).then_inc(ek_set, 1)
                    op = act.activation(v_tok[0:tw, 2 * b:2 * b + k, 0:P], src[:, :, P:2 * P], ACT.Copy)
                    if b == (nt + 1) // 2 - 1:
                        op.then_inc(v_set, 1)
                if nt == 1:
                    act.sem_inc(ek_set, 1)

            def cls_att_copy(t):
                act.wait_ge(clsatt_set, PAIRS)
                act.wait_ge(wo_done, t)
                act.activation(att_c[:, 0:NCLS], cls_att[:, :], ACT.Copy).then_inc(attc_set, 1)

            def att_copy(t):
                act.wait_ge(attc_done, t + 1)
                act.activation(att_c[:, :], bank(F6), ACT.Copy).then_inc(attc_set, 1)

            def square_b(t, geo):
                n = geo[0] * geo[1]
                act.wait_ge(h2_set, t + 1)
                act.activation(sq_b[:, 0:n], h2[:, 0:n], ACT.Square).then_inc(sqb_set, 1)

            def square_c(t, geo, b=M0):
                n = geo[0] * geo[1]
                act.wait_ge(ctrb_done, t + 1)
                act.activation(sq_c[:, 0:n], bank(b, n), ACT.Square).then_inc(sqc_set, 1)

            def center_b(t, geo, b=M0):
                n = geo[0] * geo[1]
                act.wait_ge(ctrb_done, t + 1)
                act.activation(xc_b[:, 0:n], bank(b, n), ACT.Copy).then_inc(xcb_set, 1)

            def y_hi(t, geo, f):
                n = geo[0] * geo[1]
                act.wait_ge(y_set, t + 1)
                if f is not None:
                    act.wait_ge(fh1_done, E * (f + 1))
                for img in range(2):
                    act.activation(ys[img][half(img), 0:n], y[half(img), 0:n], ACT.Copy).then_inc(yhi_set, 1)

            def router_relu(t, geo):
                n = geo[0] * geo[1]
                act.wait_ge(router_done, t + 1)
                act.activation(rh[:, 0:n], ps[0:2 * RH, F7, 0:n], ACT.Relu,
                               bias=cst("rb1")[0:2 * RH]).then_inc(rh_set, 1)

            def gate_exp(t, geo):
                nt, tw = geo
                w = 2 * nt * E
                act.wait_ge(gate_step, GATE_STEPS * t + 3)
                act.activation(g_exp[0:tw, 0:w], g_shift[0:tw, 0:w], ACT.Exp).then_inc(gexp_set, 1)

            def gate_exp_top(t, geo):
                nt, tw = geo
                act.wait_ge(gate_step, GATE_STEPS * t + 15)
                act.activation(g_ed[0:tw, 0:2 * nt], g_dif[0:tw, 0:2 * nt], ACT.Exp).then_inc(ged_set, 1)

            def gates_copy(t, geo):
                n = geo[0] * geo[1]
                act.wait_ge(gt_done, t + 1)
                act.wait_ge(fgb_done, E * t)
                act.activation(gates_c[:, 0:n], ps[0:4 * E, F7, 0:n], ACT.Copy).then_inc(gatesc_set, 1)

            def relu1(t, geo, j):
                n = geo[0] * geo[1]
                act.wait_ge(fh1_done, E * t + j + 1)
                act.wait_ge(fh2_done, E * t + j - 1)
                act.activation(f1[j % 2][:, 0:n], bank(S0, n), ACT.Relu,
                               bias=cst("eb1")[:, j // 2:j // 2 + 1]).then_inc(f1_set, 1)

            def relu2(t, geo, j):
                n = geo[0] * geo[1]
                act.wait_ge(fh2_done, E * t + j + 1)
                act.wait_ge(gh_set, E * t + j - 1)
                act.activation(f2[j % 2][:, 0:n], bank(S1, n), ACT.Relu,
                               bias=cst("eb2")[:, j // 2:j // 2 + 1]).then_inc(f2_set, 1)

            def out_copy(t, geo):
                nt, tw = geo
                act.wait_ge(outt_done, t + 1)
                act.wait_ge(out_stored, 16 * t)
                act.activation(out_t[0:tw, 0:nt * P].rearrange("p (m k c) -> p m k c", m=2, c=C),
                               ps[0:tw, F6, 0:nt * P].rearrange("p (k m c) -> p m k c", m=2, c=C),
                               ACT.Copy).then_inc(outt_set, 1)

            def step(s, t, f, g, geo_t=FULL, geo_f=FULL, geo_g=FULL):
                a, b, x, z = s is not None, t is not None, f is not None, g is not None
                if a: hidden(s); hidden_hi(s, 0); hidden_hi(s, 1)
                if x: router_relu(f, geo_f)
                if a: gate_tanh(s, 0)
                if z: out_copy(g, geo_g)
                if a: gate_tanh(s, 1); gate_tanh(s, 2)
                if b and geo_t is FULL: att_copy(t)
                if b and geo_t is CLS: cls_att_copy(t)
                if a: gate_tanh(s, 3)
                if x: gate_exp(f, geo_f)
                if a: gate_tanh(s, 4); gate_tanh(s, 5); gate_tanh(s, 6); gate_tanh(s, 7)
                if b: square_b(t, geo_t)
                if a: gate_tanh(s, 8)
                if x: relu1(f, geo_f, 0)
                if a: unfold_out(s)
                if x: gate_exp_top(f, geo_f); relu1(f, geo_f, 1); relu2(f, geo_f, 0)
                if a: center_a(s, FULL)
                if x: relu1(f, geo_f, 2)
                if a: square_a(s, FULL)
                if x: relu2(f, geo_f, 1); gates_copy(f, geo_f)
                if b: square_c(t, geo_t)
                if x: relu1(f, geo_f, 3); relu2(f, geo_f, 2)
                if b: center_b(t, geo_t)
                if x: relu2(f, geo_f, 3); relu1(f, geo_f, 4)
                if a: exp_q(s, FULL)
                if x: relu2(f, geo_f, 4)
                if a: exp_k(s, FULL)
                if x: relu1(f, geo_f, 5)
                if b: y_hi(t, geo_t, f)
                if x: relu2(f, geo_f, 5)

            def step_a(s, r, geo=FULL):
                if r is not None: center_a(r, geo); square_a(r, geo)
                if s is not None: hidden(s); hidden_hi(s, 0); hidden_hi(s, 1)
                if r is not None: exp_q(r, geo)
                if s is not None: gate_tanh(s, 0); gate_tanh(s, 1); gate_tanh(s, 2); gate_tanh(s, 3)
                if s is not None: gate_tanh(s, 4); gate_tanh(s, 5); gate_tanh(s, 6)
                if r is not None: exp_k(r, geo)
                if s is not None: gate_tanh(s, 7); gate_tanh(s, 8); unfold_out(s)

            def step_b(t, f, g, geo_t=FULL, geo_f=FULL, geo_g=FULL):
                b, x, z = t is not None, f is not None, g is not None
                if x: router_relu(f, geo_f)
                if z: out_copy(g, geo_g)
                if x: relu1(f, geo_f, 0)
                if b and geo_t is FULL: att_copy(t)
                if b and geo_t is CLS: cls_att_copy(t)
                if x: gate_exp(f, geo_f); relu1(f, geo_f, 1)
                if b: square_b(t, geo_t)
                if x: relu2(f, geo_f, 0); relu1(f, geo_f, 2); gate_exp_top(f, geo_f)
                if x: relu2(f, geo_f, 1); relu1(f, geo_f, 3); relu1(f, geo_f, 4)
                if x: gates_copy(f, geo_f)
                if b: square_c(t, geo_t, L0)
                if x: relu2(f, geo_f, 2); relu2(f, geo_f, 3)
                if b: center_b(t, geo_t, L0)
                if x: relu2(f, geo_f, 4); relu1(f, geo_f, 5)
                if b: y_hi(t, geo_t, f)
                if x: relu2(f, geo_f, 5)

            act.wait_ge(pack_loaded[0], 16)
            act.activation(b2_half[:, :], cst("b2"), ACT.Copy, scale=0.5).then_inc(setup_act, 1)
            act.sem_inc(th_set, UNITS)
            act.sem_inc(h1_set, 1)
            act.sem_inc(h1hi_set, 2)
            act.sem_inc(xcb_set, 1)
            act.sem_inc(h_set, 1)
            for s_ in (attc_set, sqb_set, sqc_set, rh_set, gexp_set, ged_set, gatesc_set, outt_set):
                act.sem_inc(s_, 1)
            act.sem_inc(yhi_set, 2)
            act.sem_inc(f1_set, E)
            act.sem_inc(f2_set, E)
            step_a(1, 0, CLS)
            with act.Fori(1, CHUNKS) as c:
                step_a(c + 1, c + 0)
            step_a(None, CHUNKS)
            step(CHUNKS + 1, 1, None, None)
            step(CHUNKS + 2, 2, 1, None)
            with act.Fori(2, CHUNKS) as c:
                step(c + (CHUNKS + 1), c + 1, c + 0, c - 1)
            with act.Fori(2, PAIRS) as i:
                with act.Fori(0, CHUNKS) as c:
                    s = i * CHUNKS + c + 1
                    step(s, s - CHUNKS, s - (CHUNKS + 1), s - (CHUNKS + 2))
            cls = (PAIRS - 1) * CHUNKS + 1
            step_b(cls, cls - 1, cls - 2, CLS)
            step_b(cls + 1, cls, cls - 1, FULL, CLS)
            step_b(cls + 2, cls + 1, cls, FULL, FULL, CLS)
            with act.Fori(2, CHUNKS) as c:
                t = c + (cls + 1)
                step_b(t, t - 1, t - 2)
            step_b(None, cls + CHUNKS, cls + CHUNKS - 1)
            step_b(None, None, cls + CHUNKS)

        @block.gpsimd
        def _(pool):
            def power(dst, src, n, tw):
                return pool.tensor_tensor(dst[0:tw, 0:n], src[0:tw, 0:n], exponent[0:tw, 0:n], ALU.pow)

            def rstd_u_(s, geo):
                nt, tw = geo
                pool.wait_ge(var_set, 2 * s + 1)
                power(rstd_u, var_u, 2 * nt, tw).then_inc(rstdu_set, 1)

            def rstd_h_(s, geo):
                nt, tw = geo
                pool.wait_ge(var_set, 2 * s + 2)
                power(rstd_h, var_h, 2 * nt, tw).then_inc(rstdh_set, 1)

            def sum_b_(t, f, geo, h):
                n = geo[0] * geo[1]
                if f is not None:
                    pool.wait_ge(h3f_set, f + 1)
                pool.wait_ge(h2_set, t + 1)
                pool.wait_ge(h3_set, t)
                pool.tensor_tensor(sum_b[:, 0:n], h[:, 0:n], h2[:, 0:n], ALU.add).then_inc(sumb_set, 1)

            def rms_b_(t, geo):
                nt, tw = geo
                pool.wait_ge(msb_set, t + 1)
                power(rms_b, ms_b, 2 * nt, tw).then_inc(rmsb_set, 1)

            def rstd_b_(t, geo):
                nt, tw = geo
                pool.wait_ge(varb_set, t + 1)
                power(rstd_b, var_b, 2 * nt, tw).then_inc(rstdb_set, 1)

            def y_lo(t, s, geo):
                n = geo[0] * geo[1]
                pool.wait_ge(rstdb_set, t + 1)
                if s is not None:
                    pool.wait_ge(rstdh_set, s + 1)
                pool.wait_ge(y_set, t + 1)
                for img in range(2):
                    pool.wait_ge(yhi_set, 2 * t + 1 + img)
                    pool.tensor_tensor(ys[img][half(1 - img), 0:n], y[half(img), 0:n],
                                       ys[img][half(img), 0:n].bitcast(F32), ALU.subtract).then_inc(ylo_set, 1)
                    pool.wait_ge(ylo_set, 2 * t + 1 + img)

            def keep_h3(f, geo):
                n = geo[0] * geo[1]
                pool.wait_ge(nrm_set, f + 1)
                pool.wait_ge(sumb_set, f + 1)
                pool.wait_ge(res_set, f)
                pool.tensor_tensor(h3_ffn[:, 0:n], nrm_b[:, 0:n], sum_b[:, 0:n], ALU.add).then_inc(h3f_set, 1)

            def step(s, t, f, g, geo_t=FULL, geo_f=FULL, geo_g=FULL, h=cur[0]):
                a, b, x, z = s is not None, t is not None, f is not None, g is not None
                if x: keep_h3(f, geo_f)
                if b: sum_b_(t, f, geo_t, h); rms_b_(t, geo_t)
                if a: rstd_u_(s, FULL)
                if b: rstd_b_(t, geo_t)
                if a: rstd_h_(s, FULL)
                if b: y_lo(t, s, geo_t)

            def step_a(s, r, geo=FULL):
                if r is not None: rstd_u_(r, geo); rstd_h_(r, geo)

            def step_b(t, f, g, geo_t=FULL, geo_f=FULL, geo_g=FULL, h=cur[0]):
                b, x, z = t is not None, f is not None, g is not None
                if x: keep_h3(f, geo_f)
                if b: sum_b_(t, f, geo_t, h); rms_b_(t, geo_t); rstd_b_(t, geo_t)
                if b: y_lo(t, None, geo_t)

            pool.wait_ge(setup_dve, 2)
            for s_ in (sumb_set, rmsb_set, rstdb_set, h3f_set):
                pool.sem_inc(s_, 1)
            pool.sem_inc(ylo_set, 2)
            step_a(1, 0, CLS)
            with pool.Fori(1, CHUNKS) as c:
                step_a(c + 1, c + 0)
            step_a(None, CHUNKS)
            step(CHUNKS + 1, 1, None, None)
            step(CHUNKS + 2, 2, 1, None)
            with pool.Fori(2, CHUNKS) as c:
                step(c + (CHUNKS + 1), c + 1, c + 0, c - 1)
            with pool.Fori(2, PAIRS) as i:
                with pool.Fori(0, CHUNKS) as c:
                    s = i * CHUNKS + c + 1
                    step(s, s - CHUNKS, s - (CHUNKS + 1), s - (CHUNKS + 2))
            cls = (PAIRS - 1) * CHUNKS + 1
            step_b(cls, cls - 1, cls - 2, CLS, h=cls_h)
            step_b(cls + 1, cls, cls - 1, FULL, CLS)
            step_b(cls + 2, cls + 1, cls, FULL, FULL, CLS)
            with pool.Fori(2, CHUNKS) as c:
                t = c + (cls + 1)
                step_b(t, t - 1, t - 2)
            step_b(None, cls + CHUNKS, cls + CHUNKS - 1)
            step_b(None, None, cls + CHUNKS)

        @block.vector
        def _(dve):
            def hidden_lo(s, img):
                dve.wait_ge(h1_set, s + 1)
                dve.wait_ge(h1hi_set, 2 * s + 1 + img)
                dve.tensor_tensor(h1s[img][half(1 - img), :], h1[half(img), :],
                                  h1s[img][half(img), :].bitcast(F32), ALU.subtract).then_inc(h1lo_set, 1)

            def gate_pixels(s, u):
                dve.wait_ge(th_set, UNITS * s + u + 1)
                dve.wait_ge(w3_done, UNITS * s + u - 2)
                dve.scalar_tensor_tensor(as_rows(gated[u % 3][:, :]), as_rows(th[u % 3][:, :]), 1.0, x_view(u),
                                         ALU.add, ALU.mult).then_inc(gated_set, 1)

            def deviations_a(s, geo):
                nt, tw = geo
                n = 2 * nt
                dve.wait_ge(vara_done, s + 1)
                sum_channels(sums_a, L1, nt, tw, suma_set)
                dve.wait_ge(suma_set, s + 1)
                dve.tensor_scalar(var_u[0:tw, 0:n], sums_a[0:tw, 0:n], (1.0 + EPS_RMS) / C, EPS_LN * EPS_RMS,
                                  ALU.mult, ALU.add).then_inc(var_set, 1)
                dve.tensor_scalar(var_h[0:tw, 0:n], sums_a[0:tw, 0:n], 1.0 / C, EPS_LN,
                                  ALU.mult, ALU.add).then_inc(var_set, 1)

            def sum_channels(dst, b, nt, tw, done):
                dve.tensor_reduce(dst[0:tw, 0:2 * nt], ps[0:tw, b, 0:nt * P].rearrange("p (g c) -> p g c", c=C),
                                  AX_X, ALU.add).then_inc(done, 1)

            def spread_copy(dst, src, nt, tw, done):
                return dve.tensor_copy(dst.rearrange("p (g c) -> p g c", c=C),
                                       src.unsqueeze(2).to_broadcast([tw, 2 * nt, C])).then_inc(done, 1)

            def spread_u(s, geo):
                nt, tw = geo
                dve.wait_ge(rstdu_set, s + 1)
                spread_copy(rx_u[0:tw, 0:nt * P], rstd_u[0:tw, 0:2 * nt], nt, tw, rxu_set)

            def spread_hn(s, geo):
                nt, tw = geo
                dve.wait_ge(rstdh_set, s + 1)
                spread_copy(rx_h[0:tw, 0:nt * P], rstd_h[0:tw, 0:2 * nt], nt, tw, rxh_set)

            def normed_u(s, geo):
                n = geo[0] * geo[1]
                dve.wait_ge(rxu_done, s + 1)
                dve.wait_ge(xca_set, s + 1)
                dve.tensor_tensor(u_a[:, 0:n], xc_a[:, 0:n], bank(L1, n), ALU.mult).then_inc(u_set, 1)

            def normed_hn(s, geo, hn):
                n = geo[0] * geo[1]
                dve.wait_ge(rxh_done, s + 1)
                if not is_step_0(s):
                    dve.wait_ge(ring_stored, 16 * s)
                dve.tensor_tensor(hn[:, 0:n], xc_a[:, 0:n], bank(L1, n), ALU.mult).then_inc(hn_set, 1)

            def elu_q_min(s, geo):
                n = geo[0] * geo[1]
                dve.wait_ge(eq_set, s + 1)
                dve.tensor_scalar(eq1[:, 0:n], eq[:, 0:n], 1.0, None, ALU.min).then_inc(eq1_set, 1)

            def elu_q(s, geo, q):
                n = geo[0] * geo[1]
                dve.wait_ge(eq1_set, s + 1)
                if not is_step_0(s):
                    dve.wait_ge(ring_stored, 16 * s)
                dve.scalar_tensor_tensor(q[:, 0:n], bank(L1, n), 1.0, eq1[:, 0:n], ALU.add, ALU.max).then_inc(qf_set, 1)

            def elu_k_min(s, geo):
                nt, tw = geo
                dve.wait_ge(ek_set, 2 * s + 2)
                dve.tensor_scalar(ek1[0:tw, 0:nt, :], ek[0:tw, 0:nt, :], 1.0, None, ALU.min).then_inc(ek1_set, 1)

            def elu_k(s, geo):
                nt, tw = geo
                dve.wait_ge(ek1_set, s + 1)
                dve.wait_ge(v_set, s + 1)
                for b in range((nt + 1) // 2):
                    k = min(2, nt - 2 * b)
                    src = ps[0:tw, KV[b], 0:2 * P * k].rearrange("p (k c) -> p k c", k=k)
                    dve.scalar_tensor_tensor(k_tok[0:tw, 2 * b:2 * b + k, :], src[:, :, 0:P], 1.0,
                                             ek1[0:tw, 2 * b:2 * b + k, :], ALU.add, ALU.max).then_inc(kf_set, 1)
                if nt == 1:
                    dve.sem_inc(kf_set, 1)

            def sum_kv(s):
                dve.wait_ge(kvp_done, s + 1)
                if is_step_0(s):
                    dve.tensor_copy(kv_cls[:, :], bank(L1, P + 2)).then_inc(kvsum_set, 1)
                else:
                    dve.wait_ge(kvsum_set, s)
                    dve.tensor_tensor(kv_sum[:, :], kv_sum[:, :], bank(L1, P + 2), ALU.add).then_inc(kvsum_set, 1)

            def image_end(i, s, t):
                dve.wait_ge(kvsum_set, s)
                if t is not None:
                    dve.wait_ge(attn_done, t)
                    dve.wait_ge(clsatt_done, i)
                lo, _ = COLS["head_mask"]
                dve.tensor_tensor(kv_m[:, 0:P], kv_sum[:, 0:P], packed[:, lo:lo + P], ALU.mult)
                dve.tensor_scalar(kv_m[:, P:], packed[:, lo + P:lo + P + 2 * HEADS], kv_sum[:, P:P + 1], None,
                                  ALU.mult)
                dve.tensor_scalar(k_m[:, :], packed[:, lo:lo + P], kv_sum[:, P:P + 1], None,
                                  ALU.mult).then_inc(kvm_set, 1)
                dve.wait_ge(kvm_set, i + 1)
                dve.tensor_copy(kv_sum[:, :], kv_cls[:, :]).then_inc(kvnew_set, 1)
                dve.wait_ge(kvnew_set, i + 1)

            def cls_attended(i):
                dve.wait_ge(clsatt_done, i + 1)
                dve.tensor_scalar(cls_den[:, 0:1], ps[:, S0, 1:2], EPS_ATT, None, ALU.add).then_inc(clsden_set, 1)
                dve.wait_ge(clsden_set, 2 * i + 1)
                dve.reciprocal(cls_den[:, 1:2], cls_den[:, 0:1]).then_inc(clsden_set, 1)
                dve.wait_ge(clsden_set, 2 * i + 2)
                dve.tensor_tensor(cls_att[:, bass.ds(i, 1)], cls_den[:, 1:2], ps[:, S0, 0:1],
                                  ALU.mult).then_inc(clsatt_set, 1)

            def denominators(t, b=M0):
                dve.wait_ge(attn_done, t + 1)
                for two in range(2):
                    src = ps[0:TILE, b + two, 0:2 * WIDE].rearrange("p (k c) -> p k c", k=2)
                    dve.tensor_scalar(den[:, 32 * two:32 * two + 32].rearrange("p (k c) -> p k c", k=2),
                                      src[:, :, P:WIDE], EPS_ATT, None, ALU.add).then_inc(den_set, 1)

            def inverses(t):
                dve.wait_ge(den_set, 2 * t + 2)
                dve.reciprocal(zed[:, :], den[:, :]).then_inc(zed_set, 1)

            def attended(t, b=M0):
                dve.wait_ge(zed_set, t + 1)
                for k in range(NT):
                    src = ps[0:TILE, b + k // 2, WIDE * (k % 2):WIDE * (k % 2) + P]
                    op = dve.tensor_tensor(att[:, k * P:(k + 1) * P].rearrange("p (h c) -> p h c", c=HD),
                                           zed[:, 16 * k:16 * k + 16].unsqueeze(2).to_broadcast([TILE, 16, HD]),
                                           src.rearrange("p (h c) -> p h c", c=HD), ALU.mult)
                    if k % 2 == 1:
                        op.then_inc(att_set, 1)

            def residual(t, geo, hn, b=M0):
                n = geo[0] * geo[1]
                dve.wait_ge(wo_done, t + 1)
                dve.wait_ge(sumb_set, t)
                dve.scalar_tensor_tensor(h2[:, 0:n], bank(b, n), cst("bo"), hn[:, 0:n], ALU.add,
                                         ALU.add).then_inc(h2_set, 1)

            def mean_sq_b(t, geo):
                nt, tw = geo
                dve.wait_ge(ms_done, t + 1)
                sum_channels(sums_b, F5, nt, tw, summs_set)
                dve.wait_ge(summs_set, t + 1)
                dve.tensor_scalar(ms_b[0:tw, 0:2 * nt], sums_b[0:tw, 0:2 * nt], 1.0 / C, EPS_RMS,
                                  ALU.mult, ALU.add).then_inc(msb_set, 1)

            def spread_b(t, geo):
                nt, tw = geo
                dve.wait_ge(rmsb_set, t + 1)
                spread_copy(rx_b[0:tw, 0:nt * P], rms_b[0:tw, 0:2 * nt], nt, tw, rxb_set)

            def rms_normed(t, geo, f):
                n = geo[0] * geo[1]
                dve.wait_ge(rxb_done, t + 1)
                if f is not None:
                    dve.wait_ge(h3f_set, f + 1)
                dve.scalar_tensor_tensor(nrm_b[:, 0:n], h2[:, 0:n], cst("norm2"), bank(F5, n), ALU.mult,
                                         ALU.mult).then_inc(nrm_set, 1)

            def block_out(t, geo):
                n = geo[0] * geo[1]
                dve.wait_ge(nrm_set, t + 1)
                dve.wait_ge(sumb_set, t + 1)
                dve.tensor_tensor(h3[:, 0:n], nrm_b[:, 0:n], sum_b[:, 0:n], ALU.add).then_inc(h3_set, 1)

            def variance_b(t, geo):
                nt, tw = geo
                dve.wait_ge(varb_done, t + 1)
                sum_channels(sums_b, F5, nt, tw, sumvar_set)
                dve.wait_ge(sumvar_set, t + 1)
                dve.tensor_scalar(var_b[0:tw, 0:2 * nt], sums_b[0:tw, 0:2 * nt], 1.0 / C, EPS_LN,
                                  ALU.mult, ALU.add).then_inc(varb_set, 1)

            def spread_c(t, geo):
                nt, tw = geo
                dve.wait_ge(rstdb_set, t + 1)
                spread_copy(rx_c[0:tw, 0:nt * P], rstd_b[0:tw, 0:2 * nt], nt, tw, rxc_set)

            def normed_b(t, geo):
                n = geo[0] * geo[1]
                dve.wait_ge(rxc_done, t + 1)
                dve.wait_ge(xcb_set, t + 1)
                dve.wait_ge(ylo_set, 2 * t)
                dve.tensor_tensor(y[:, 0:n], xc_b[:, 0:n], bank(F5, n), ALU.mult).then_inc(y_set, 1)

            def gates_part(t, geo, part):
                nt, tw = geo
                g, w = 2 * nt, 2 * nt * E

                def flat(x):
                    return x[0:tw, 0:w]

                def grp(x):
                    return x[0:tw, 0:w].rearrange("p (g e) -> p g e", e=E)

                def one(x):
                    return x[0:tw, 0:g]

                def wide(x):
                    return x[0:tw, 0:g].unsqueeze(2).to_broadcast([tw, g, E])

                def after(k):
                    dve.wait_ge(gate_step, GATE_STEPS * t + k)

                if part == 0:
                    dve.wait_ge(logit_done, t + 1)
                    dve.tensor_tensor(flat(g_logit), ps[0:tw, F7, 0:w], cst("rb2")[0:tw, 0:w],
                                      ALU.add).then_inc(gate_step, 1)
                    after(1)
                    dve.tensor_reduce(one(g_max), grp(g_logit), AX_X, ALU.max).then_inc(gate_step, 1)
                    after(2)
                    dve.tensor_tensor(grp(g_shift), grp(g_logit), wide(g_max), ALU.subtract).then_inc(gate_step, 1)
                if part == 1:
                    dve.wait_ge(gexp_set, t + 1)
                    dve.tensor_reduce(one(g_tot), grp(g_exp), AX_X, ALU.add).then_inc(gate_step, 1)
                    after(4)
                    dve.reciprocal(one(g_inv), one(g_tot)).then_inc(gate_step, 1)
                if part == 2:
                    after(5)
                    dve.tensor_tensor(grp(g_p), grp(g_exp), wide(g_inv), ALU.mult).then_inc(gate_step, 1)
                    after(6)
                    dve.tensor_reduce(one(g_top), grp(g_p), AX_X, ALU.max).then_inc(gate_step, 1)
                if part == 3:
                    after(7)
                    dve.tensor_tensor(grp(g_e1), grp(g_p), wide(g_top), ALU.is_equal).then_inc(gate_step, 1)
                    after(8)
                    dve.tensor_tensor(flat(g_w1), flat(g_e1), cst("order")[0:tw, 0:w], ALU.mult).then_inc(gate_step, 1)
                if part == 4:
                    after(9)
                    dve.tensor_reduce(one(g_i1), grp(g_w1), AX_X, ALU.max).then_inc(gate_step, 1)
                    after(10)
                    dve.tensor_tensor(grp(g_o1), grp(g_w1), wide(g_i1), ALU.is_equal).then_inc(gate_step, 1)
                if part == 5:
                    after(11)
                    dve.scalar_tensor_tensor(flat(g_rest), flat(g_o1), -4.0, flat(g_p), ALU.mult,
                                             ALU.add).then_inc(gate_step, 1)
                    after(12)
                    dve.tensor_reduce(one(g_top2), grp(g_rest), AX_X, ALU.max).then_inc(gate_step, 1)
                if part == 6:
                    after(13)
                    dve.tensor_tensor(grp(g_e2), grp(g_rest), wide(g_top2), ALU.is_equal).then_inc(gate_step, 1)
                    dve.tensor_tensor(one(g_dif), one(g_top2), one(g_top), ALU.subtract).then_inc(gate_step, 1)
                    after(14)
                    dve.tensor_tensor(flat(g_w2), flat(g_e2), cst("order")[0:tw, 0:w], ALU.mult).then_inc(gate_step, 1)
                if part == 7:
                    after(16)
                    dve.tensor_reduce(one(g_i2), grp(g_w2), AX_X, ALU.max).then_inc(gate_step, 1)
                    after(17)
                    dve.tensor_tensor(grp(g_o2), grp(g_w2), wide(g_i2), ALU.is_equal).then_inc(gate_step, 1)
                if part == 8:
                    dve.wait_ge(ged_set, t + 1)
                    dve.tensor_scalar(one(g_one), one(g_ed), 1.0, None, ALU.add).then_inc(gate_step, 1)
                    after(19)
                    dve.reciprocal(one(g_r1), one(g_one)).then_inc(gate_step, 1)
                if part == 9:
                    after(20)
                    dve.tensor_tensor(one(g_r2), one(g_r1), one(g_ed), ALU.mult)
                    dve.tensor_tensor(grp(g_a), grp(g_o1), wide(g_r1), ALU.mult).then_inc(gate_step, 1)
                    after(21)
                    dve.tensor_tensor(grp(g_b), grp(g_o2), wide(g_r2), ALU.mult).then_inc(gate_step, 1)
                if part == 10:
                    after(22)
                    dve.tensor_tensor(flat(g_sum), flat(g_a), flat(g_b), ALU.add)
                    by_tile = g_sum[0:tw, 0:w].rearrange("p (n e) -> p n e", n=nt)
                    dve.tensor_tensor(g_parts[0:tw, 0:nt, 0, :], g_a[0:tw, 0:w].rearrange("p (n e) -> p n e", n=nt),
                                      g_b[0:tw, 0:w].rearrange("p (n e) -> p n e", n=nt), ALU.add).then_inc(gate_step, 1)
                    after(23)
                    dve.tensor_tensor(g_parts[0:tw, 0:nt, 1, :], by_tile, g_parts[0:tw, 0:nt, 0, :].bitcast(F32),
                                      ALU.subtract).then_inc(gate_step, 1)

            def gate_hidden(t, geo, j):
                n = geo[0] * geo[1]
                dve.wait_ge(f2_set, E * t + j + 1)
                dve.wait_ge(fgb_done, E * t + j + 1)
                dve.wait_ge(fw3_done, E * t + j - 2)
                dve.tensor_tensor(gh[j % 3][:, 0:n], f2[j % 2][:, 0:n], bank(F6, n), ALU.mult).then_inc(gh_set, 1)

            def result(t, geo):
                n = geo[0] * geo[1]
                dve.wait_ge(fw3_done, E * (t + 1))
                dve.wait_ge(outt_done, t)
                dve.wait_ge(h3f_set, t + 1)
                dve.tensor_tensor(res[:, 0:n], h3_ffn[:, 0:n], bank(M0, n), ALU.add).then_inc(res_set, 1)

            def step(s, t, f, g, geo_t=FULL, geo_f=FULL, geo_g=FULL, hn=cur[1]):
                a, b, x, z = s is not None, t is not None, f is not None, g is not None
                if z: gate_hidden(g, geo_g, 5); result(g, geo_g)
                if a: hidden_lo(s, 0); hidden_lo(s, 1)
                if b and geo_t is FULL: denominators(t); inverses(t); attended(t)
                if a: gate_pixels(s, 0); gate_pixels(s, 1)
                if x: gates_part(f, geo_f, 0)
                if a: gate_pixels(s, 2)
                if x: gates_part(f, geo_f, 1)
                if a: gate_pixels(s, 3)
                if x: gates_part(f, geo_f, 2)
                if a: gate_pixels(s, 4)
                if b: residual(t, geo_t, hn)
                if a: gate_pixels(s, 5)
                if x: gates_part(f, geo_f, 3)
                if a: gate_pixels(s, 6)
                if x: gates_part(f, geo_f, 4)
                if a: gate_pixels(s, 7); gate_pixels(s, 8)
                if b: mean_sq_b(t, geo_t)
                if x: gates_part(f, geo_f, 5); gates_part(f, geo_f, 6); gates_part(f, geo_f, 7)
                if x: gates_part(f, geo_f, 8)
                if b: spread_b(t, geo_t)
                if x: gates_part(f, geo_f, 9); gates_part(f, geo_f, 10)
                if b: rms_normed(t, geo_t, f); block_out(t, geo_t)
                if a: deviations_a(s, FULL)
                if x: gate_hidden(f, geo_f, 0)
                if b: variance_b(t, geo_t)
                if a: spread_u(s, FULL)
                if x: gate_hidden(f, geo_f, 1)
                if a: normed_u(s, FULL)
                if b: spread_c(t, geo_t)
                if x: gate_hidden(f, geo_f, 2)
                if b: normed_b(t, geo_t)
                if a: elu_q_min(s, FULL)
                if x: gate_hidden(f, geo_f, 3)
                if a: spread_hn(s, FULL); elu_q(s, FULL, q_new)
                if x: gate_hidden(f, geo_f, 4)
                if a: normed_hn(s, FULL, hn_new); elu_k_min(s, FULL); elu_k(s, FULL); sum_kv(s)

            def step_a(s, r, geo=FULL, hn=hn_new, q=q_new):
                if r is not None: deviations_a(r, geo); spread_u(r, geo); normed_u(r, geo)
                if s is not None: hidden_lo(s, 0); hidden_lo(s, 1)
                if r is not None: elu_q_min(r, geo)
                if s is not None: gate_pixels(s, 0); gate_pixels(s, 1)
                if r is not None: elu_q(r, geo, q)
                if s is not None: gate_pixels(s, 2)
                if r is not None: spread_hn(r, geo)
                if s is not None: gate_pixels(s, 3)
                if r is not None: normed_hn(r, geo, hn)
                if s is not None: gate_pixels(s, 4); gate_pixels(s, 5); gate_pixels(s, 6)
                if r is not None: elu_k_min(r, geo)
                if s is not None: gate_pixels(s, 7); gate_pixels(s, 8)
                if r is not None: elu_k(r, geo); sum_kv(r)

            def step_b(t, f, g, geo_t=FULL, geo_f=FULL, geo_g=FULL, hn=cur[1]):
                b, x, z = t is not None, f is not None, g is not None
                if z: gate_hidden(g, geo_g, 5)
                if b and geo_t is FULL: denominators(t, L0)
                if z: result(g, geo_g)
                if b and geo_t is FULL: inverses(t); attended(t, L0)
                if x: gates_part(f, geo_f, 0); gates_part(f, geo_f, 1); gates_part(f, geo_f, 2)
                if b: residual(t, geo_t, hn, L0)
                if x: gates_part(f, geo_f, 3); gates_part(f, geo_f, 4); gates_part(f, geo_f, 5)
                if b: mean_sq_b(t, geo_t)
                if x: gates_part(f, geo_f, 6); gates_part(f, geo_f, 7); gates_part(f, geo_f, 8)
                if x: gates_part(f, geo_f, 9)
                if b: spread_b(t, geo_t)
                if x: gates_part(f, geo_f, 10)
                if b: rms_normed(t, geo_t, f); block_out(t, geo_t)
                if x: gate_hidden(f, geo_f, 0); gate_hidden(f, geo_f, 1)
                if b: variance_b(t, geo_t)
                if x: gate_hidden(f, geo_f, 2)
                if b: spread_c(t, geo_t)
                if x: gate_hidden(f, geo_f, 3)
                if b: normed_b(t, geo_t)
                if x: gate_hidden(f, geo_f, 4)

            def split(to, lo, hi, n):
                high, low = split_hi[:, to:to + hi - lo], split_lo[:, to:to + hi - lo]
                dve.tensor_copy(high, packed[:, lo:hi]).then_inc(setup_dve, 1)
                dve.wait_ge(setup_dve, n)
                dve.tensor_tensor(low, packed[:, lo:hi], high.bitcast(F32), ALU.subtract).then_inc(setup_dve, 1)

            dve.memset(exponent[:, :], -0.5).then_inc(setup_dve, 1)
            dve.memset(v_tok[:, :, :], 1.0).then_inc(setup_dve, 1)
            dve.sem_inc(gated_set, UNITS)
            for s_ in (summs_set, sumvar_set, den_set, den_set, zed_set, att_set, att_set, h2_set, msb_set,
                       rxb_set, nrm_set, h3_set, varb_set, rxc_set, y_set, res_set):
                dve.sem_inc(s_, 1)
            dve.sem_inc(h1lo_set, 2)
            dve.sem_inc(gate_step, GATE_STEPS)
            dve.sem_inc(gh_set, E)
            dve.wait_ge(pack_loaded[0], 16)
            dve.tensor_scalar(wqkv_n[:, :], cst("wqkv"), cst("norm1"), None, ALU.mult).then_inc(setup_dve, 1)
            dve.wait_ge(pack_loaded[1], 16)
            dve.tensor_scalar(w3_half[:, :], cst("w3"), 0.5, None, ALU.mult).then_inc(setup_dve, 1)
            split(0, W2_AT, W2_END, 5)
            step_a(1, 0, CLS, cls_hn, cls_q)
            dve.wait_ge(kvsum_set, 1)
            dve.tensor_copy(kv_sum[:, :], kv_cls[:, :]).then_inc(setup_dve, 1)
            dve.wait_ge(pack_loaded[2], 16)
            split(6 * P, EW1_AT, EB3_END, 8)
            with dve.Fori(1, CHUNKS) as c:
                step_a(c + 1, c + 0)
            step_a(None, CHUNKS)
            image_end(0, CHUNKS + 1, None)
            step(CHUNKS + 1, 1, None, None)
            step(CHUNKS + 2, 2, 1, None)
            with dve.Fori(2, CHUNKS) as c:
                step(c + (CHUNKS + 1), c + 1, c + 0, c - 1)
            image_end(1, 2 * CHUNKS + 1, CHUNKS + 1)
            cls_attended(0)
            with dve.Fori(2, PAIRS) as i:
                with dve.Fori(0, CHUNKS) as c:
                    s = i * CHUNKS + c + 1
                    step(s, s - CHUNKS, s - (CHUNKS + 1), s - (CHUNKS + 2))
                image_end(i, i * CHUNKS + CHUNKS + 1, i * CHUNKS + 1)
                cls_attended(i - 1)
            cls_attended(PAIRS - 1)
            cls = (PAIRS - 1) * CHUNKS + 1
            step_b(cls, cls - 1, cls - 2, CLS, hn=cls_hn)
            for done in (den_set, den_set, zed_set, att_set, att_set):
                dve.sem_inc(done, 1)
            step_b(cls + 1, cls, cls - 1, FULL, CLS)
            step_b(cls + 2, cls + 1, cls, FULL, FULL, CLS)
            with dve.Fori(2, CHUNKS) as c:
                t = c + (cls + 1)
                step_b(t, t - 1, t - 2)
            step_b(None, cls + CHUNKS, cls + CHUNKS - 1)
            step_b(None, None, cls + CHUNKS)



def kernel(**inputs):
    import concourse.bacc as bacc
    from concourse.bass_utils import run_bass_kernel_spmd

    a = {k: np.asarray(v) for k, v in inputs.items()}
    f32 = np.float32
    xpad = np.zeros((B, C, PW * PW + 2 * PW), f32)
    xpad[:, :, 0:PW * PW] = np.pad(a["x"], ((0, 0), (0, 0), (1, 1), (1, 1))).reshape(B, C, PW * PW)
    x_rows = np.zeros((PAIRS, P, CHUNKS, X_W), f32)
    for c in range(CHUNKS):
        at = c * ROWS * PW
        for img in range(2):
            for part in range(2):
                rows = slice(64 * part, 64 * part + 64)
                x_rows[:, rows, c, XC_AT[img]:XC_AT[img] + XC_W] = xpad[img::2, :, at + part:at + part + XC_W]
                of = at + 2 + part * PW
                x_rows[:, rows, c, XR_AT[img]:XR_AT[img] + XR_W] = xpad[img::2, :, of:of + XR_W]
            of = at + 2 * PW + 2
            x_rows[:, 64 * img:64 * img + 64, c, XP_AT:XP_AT + XR_W] = xpad[img::2, :, of:of + XR_W]
    x_rows = x_rows.reshape(PAIRS * P, CHUNKS * X_W)

    def pair_diag(w):
        z = np.zeros((2 * w.shape[0], 2 * w.shape[1]), f32)
        z[:w.shape[0], :w.shape[1]] = w
        z[w.shape[0]:, w.shape[1]:] = w
        return z

    pack = np.zeros((P, PACK_W), f32)

    def put(name, v, at=0):
        lo, _ = COLS[name]
        pack[0:v.shape[0], lo + at:lo + at + v.shape[1]] = v

    w1, w2, w3 = a["L0_tok_W1"].reshape(C, 9, C), a["L0_tok_W2"].reshape(C, C, 9), a["L0_tok_W3"].reshape(C, 9, C)
    b2 = a["L0_tok_b2"].reshape(C, 9)

    def k_of(offset):
        return 3 * offset[0] + offset[1]

    for m, (o1, o2) in enumerate(OFFSET_PAIRS):
        put("w1", np.concatenate([w1[:, k_of(o1)], w1[:, k_of(o2)]]), m * C)
        put("w3", np.concatenate([w3[:, k_of(o1)], w3[:, k_of(o2)]]), m * C)
        both = np.concatenate([w2[:, :, k_of(o1)], w2[:, :, k_of(o2)]], axis=1)
        put("w2", np.concatenate([both, both]), m * P)
        put("b2", np.concatenate([b2[:, k_of(o1)], b2[:, k_of(o2)]])[:, None], m)
    last = k_of(LAST_OFFSET)
    put("w1", pair_diag(w1[:, last]), 4 * C)
    put("w3", pair_diag(w3[:, last]), 4 * C)
    for img in range(2):
        put("w2", np.concatenate([w2[:, :, last]] * 2), (4 + img) * P + 64 * img)
    put("b2", np.concatenate([b2[:, last]] * 2)[:, None], 4)
    wq, wk, wv = np.split(a["L0_attn_w_qkv"], 3, axis=1)
    put("wqkv", pair_diag(wq))
    put("wqkv", pair_diag(wk), P)
    put("wqkv", pair_diag(wv), 2 * P)
    put("wo", pair_diag(a["L0_attn_w_out"]))
    e1, e2, e3 = (a[f"L0_ffn_expert_w{k}"] for k in (1, 2, 3))
    eb1, eb2, eb3 = (a[f"L0_ffn_expert_b{k}"] for k in (1, 2, 3))
    for ep in range(E // 2):
        first = np.concatenate([e1[2 * ep], e1[2 * ep + 1]], axis=1)
        put("ew1", np.concatenate([first, first]), ep * P)
        put("ew2", e2[2 * ep], ep * P)
        lo, _ = COLS["ew2"]
        pack[64:, lo + ep * P + 64:lo + (ep + 1) * P] = e2[2 * ep + 1]
        put("ew3", np.concatenate([e3[2 * ep], e3[2 * ep + 1]]), ep * C)
        put("eb1", np.concatenate([eb1[2 * ep], eb1[2 * ep + 1]])[:, None], ep)
        put("eb2", np.concatenate([eb2[2 * ep], eb2[2 * ep + 1]])[:, None], ep)
    sel_at, eb3_at = COLS["gate_sel"][0], COLS["eb3"][0]
    for part in range(2):
        for img in range(2):
            for e in range(E):
                row = part * 2 * E + img * E + e
                j = 2 * (e // 2) + img
                at = sel_at + j * P + 64 * (e % 2)
                pack[row, at:at + 64] = 1.0
                pack[row, eb3_at + 64 * img:eb3_at + 64 * img + 64] = eb3[e]
    for img in range(2):
        put("rw1", np.concatenate([a["L0_ffn_router_w1"]] * 2), img * P + RH * img)
    put("rw2", pair_diag(a["L0_ffn_router_w2"]))
    put("ident", np.eye(P, dtype=f32))
    put("center", pair_diag(np.eye(C, dtype=f32) - f32(1.0 / C)))
    head = np.arange(P) // HD
    put("head_mask", (head[:, None] == head[None, :]).astype(f32))
    put("head_mask", (head[:, None] == np.arange(2 * HEADS)[None, :]).astype(f32), P)
    put("order", np.tile(np.arange(E, 0, -1, dtype=f32), (P, 2 * NT)))
    put("rb2", np.tile(a["L0_ffn_router_b2"], (P, 2 * NT)))
    put("cls", np.tile(np.concatenate([a["cls_tok"].reshape(C)] * 2)[:, None], (1, NCLS)))

    def column(name, v):
        put(name, np.concatenate([v, v])[:, None])

    column("b1", a["L0_tok_b1"])
    column("b3", a["L0_tok_b3"])
    column("norm1", a["L0_attn_w_norm1"])
    column("norm2", a["L0_attn_w_norm2"])
    column("bo", a["L0_attn_b_out"])
    column("rb1", a["L0_ffn_router_b1"])

    nc = bacc.Bacc("TRN2", target_bir_lowering=False, num_devices=1)
    ap_x = nc.dram_tensor("x_rows", x_rows.shape, F32, kind="ExternalInput").ap()
    ap_p = nc.dram_tensor("pack", pack.shape, F32, kind="ExternalInput").ap()
    ap_o = nc.dram_tensor("out", (B, TOKENS, C), F32, kind="ExternalOutput").ap()
    build(nc, ap_x, ap_p, ap_o)
    r = run_bass_kernel_spmd(nc, [{"x_rows": x_rows, "pack": pack}], core_ids=[0])
    return r.results[0]["out"]
```
